# Optimizing a Trainium2 kernel written in Bass

```python
import numpy as np
import jax
import jax.numpy as jnp

def _softmax(x, axis=-1):
    return jax.nn.softmax(x, axis=axis)

def _gelu(x):
    return jax.nn.gelu(x, approximate=True)

def _silu(x):
    return jax.nn.silu(x)

def _sigmoid(x):
    return jax.nn.sigmoid(x)

def _layernorm(x, axis=-1, eps=1e-05):
    m = jnp.mean(x, axis=axis, keepdims=True)
    v = jnp.var(x, axis=axis, keepdims=True)
    return (x - m) / jnp.sqrt(v + eps)

def _scatter_add(tgt, idx, src, axis=0):
    return tgt.at[idx].add(src)

def _segment_sum(src, seg, n):
    return jax.ops.segment_sum(src, seg, n)
kernel_name = 'mk_prb_d2_jaxref_r8_1f216a'

def setup_inputs(seed: int=0):
    np.random.seed(seed)
    _w = jnp.asarray

    def _L0_attn_setup():
        import jax, jax.numpy as jnp
        import numpy as np
        N_HEAD = 16
        D_MODEL = 128
        HEAD_DIM = D_MODEL // N_HEAD
        LAMBDA_INIT = 0.8 - 0.6 * float(np.exp(-0.3 * 1))

        def _rms_norm(x):
            eps = jnp.finfo(x.dtype).eps
            return x * jax.lax.rsqrt(jnp.mean(jnp.square(x), axis=-1, keepdims=True) + eps)

        def _rotary_cos_sin(T, dim, base=10000.0):
            inv_freq = 1.0 / base ** (jnp.arange(0, dim, 2, dtype=jnp.float32) / dim)
            freqs = jnp.outer(jnp.arange(T, dtype=jnp.float32), inv_freq)
            return (jnp.cos(freqs), jnp.sin(freqs))

        def _apply_rotary(x, cos, sin):
            d = x.shape[-1] // 2
            c = cos[None, :, None, None, :]
            s = sin[None, :, None, None, :]
            x1, x2 = (x[..., :d], x[..., d:])
            return jnp.concatenate([x1 * c + x2 * s, -x1 * s + x2 * c], axis=-1)

        def _causal_attn(q, k, v, scale):
            T = q.shape[1]
            scores = jnp.einsum('bthd,bshd->bhts', q, k) * scale
            mask = jnp.tril(jnp.ones((T, T), dtype=bool))
            scores = jnp.where(mask, scores, -jnp.inf)
            w = jax.nn.softmax(scores, axis=-1)
            return jnp.einsum('bhts,bshd->bthd', w, v)
        key = jax.random.key(seed)
        ks = jax.random.split(key, 10)
        B, T, D = (1, 256, D_MODEL)
        std = 0.02
        return {'x': jax.random.normal(ks[0], (B, T, D), jnp.float32), 'Wq': jax.random.normal(ks[1], (D, D), jnp.float32) * std, 'Wk': jax.random.normal(ks[2], (D, D), jnp.float32) * std, 'Wv': jax.random.normal(ks[3], (D, D), jnp.float32) * std, 'Wproj': jax.random.normal(ks[4], (D, D), jnp.float32) * std, 'lambda_q1': jax.random.normal(ks[5], (HEAD_DIM // 2,), jnp.float32) * 0.1, 'lambda_k1': jax.random.normal(ks[6], (HEAD_DIM // 2,), jnp.float32) * 0.1, 'lambda_q2': jax.random.normal(ks[7], (HEAD_DIM // 2,), jnp.float32) * 0.1, 'lambda_k2': jax.random.normal(ks[8], (HEAD_DIM // 2,), jnp.float32) * 0.1}
    _L0_attn_in = _L0_attn_setup()

    def _L0_ffn_setup():
        import jax, jax.numpy as jnp
        import numpy as np
        BLOCK_SIZE = 32
        FP6_E2M3_MAX = 7.5

        def _build_fp6_e2m3_grid():
            vals = set()
            for bits in range(64):
                s = bits >> 5 & 1
                e = bits >> 3 & 3
                m = bits & 7
                v = m / 8.0 if e == 0 else (1.0 + m / 8.0) * 2.0 ** (e - 1)
                vals.add(-v if s else v)
            return np.array(sorted(vals), dtype=np.float32)
        _GRID = jnp.asarray(_build_fp6_e2m3_grid())

        def _nearest_on_grid(x, grid):
            idx = jnp.clip(jnp.searchsorted(grid, x), 0, grid.shape[0] - 1)
            idx_lo = jnp.maximum(idx - 1, 0)
            v_hi = grid[idx]
            v_lo = grid[idx_lo]
            return jnp.where(jnp.abs(x - v_lo) <= jnp.abs(x - v_hi), v_lo, v_hi)

        def _mx_quantize(t, eps=1e-30):
            rows, K = t.shape
            blocks = t.reshape(rows, K // BLOCK_SIZE, BLOCK_SIZE)
            scales = jnp.maximum(jnp.max(jnp.abs(blocks), axis=-1) / FP6_E2M3_MAX, eps)
            q = _nearest_on_grid(blocks / scales[..., None], _GRID)
            return (q, scales)
        key = jax.random.key(seed)
        k1, k2, k3 = jax.random.split(key, 3)
        x = jax.random.normal(k1, (8, 1024, 128), dtype=jnp.float32)
        weight = jax.random.normal(k2, (128, 128), dtype=jnp.float32) * 0.02
        bias = jax.random.normal(k3, (128,), dtype=jnp.float32) * 0.02
        return {'x': x, 'weight': weight, 'bias': bias}
    _L0_ffn_in = _L0_ffn_setup()

    def _L1_attn_setup():
        import jax, jax.numpy as jnp
        import numpy as np
        D_MODEL = 128
        NUM_HEADS = 16
        HEAD_DIM = D_MODEL // NUM_HEADS
        EPS = 1e-08
        key = jax.random.key(seed)
        ks = jax.random.split(key, 6)
        B, T = (4, 256)
        s = 0.02
        return {'x': jax.random.normal(ks[0], (B, T, D_MODEL), dtype=jnp.float32), 'Wq': jax.random.normal(ks[1], (D_MODEL, D_MODEL), dtype=jnp.float32) * s, 'Wk': jax.random.normal(ks[2], (D_MODEL, D_MODEL), dtype=jnp.float32) * s, 'Wv': jax.random.normal(ks[3], (D_MODEL, D_MODEL), dtype=jnp.float32) * s, 'Wo': jax.random.normal(ks[4], (D_MODEL, D_MODEL), dtype=jnp.float32) * s, 'bo': jnp.zeros((D_MODEL,), dtype=jnp.float32)}
    _L1_attn_in = _L1_attn_setup()

    def _L1_ffn_setup():
        import jax, jax.numpy as jnp
        import numpy as np
        DIM = 128
        DEPTH = 6
        HEADS = 16
        DIM_HEAD = 64
        WINDOW = 32
        INNER = HEADS * DIM_HEAD
        DIM_INNER = int(DIM * 4 * 2 / 3)
        QK_SCALE = 8.0

        def shift_tokens(t):
            a, s = jnp.split(t, 2, -1)
            s = jnp.pad(s, ((0, 0), (1, 0), (0, 0)))[:, :-1]
            return jnp.concatenate([a, s], -1)

        def l2norm(t):
            return t / jnp.maximum(jnp.linalg.norm(t, axis=-1, keepdims=True), 1e-12)

        def rotate_half(x):
            x1, x2 = jnp.split(x, 2, -1)
            return jnp.concatenate([-x2, x1], -1)

        def rotary_tables(n):
            half = jnp.arange(0, DIM_HEAD, 2, dtype=jnp.float32)
            inv_freq = 1.0 / 10000.0 ** (half / DIM_HEAD)
            t = jnp.arange(n, dtype=jnp.float32)
            freqs = t[:, None] * inv_freq[None, :]
            freqs = jnp.concatenate([freqs, freqs], -1)
            base_scale = (half + 0.4 * DIM_HEAD) / (1.4 * DIM_HEAD)
            power = (t - n // 2) / (WINDOW // 2)
            scale = base_scale[None, :] ** power[:, None]
            scale = jnp.concatenate([scale, scale], -1)
            return (freqs, scale)

        def local_attention(q, k, v):
            b, h, n, d = q.shape
            w = WINDOW
            nw = n // w
            bq = q.reshape(b, h, nw, w, d)
            bk = k.reshape(b, h, nw, w, d)
            bv = v.reshape(b, h, nw, w, d)

            def look(t):
                p = jnp.pad(t, ((0, 0), (0, 0), (1, 0), (0, 0), (0, 0)))
                return jnp.concatenate([p[:, :, :nw], p[:, :, 1:]], axis=3)
            bk2, bv2 = (look(bk), look(bv))
            seq = jnp.arange(n).reshape(nw, w)
            seq_p = jnp.pad(seq, ((1, 0), (0, 0)), constant_values=-1)
            jt = jnp.concatenate([seq_p[:nw], seq_p[1:]], axis=1)
            it = seq[:, :, None]
            jb = jt[:, None, :]
            mask = (it < jb) | (it > jb + w) | (jb == -1)
            sim = jnp.einsum('bhwie,bhwje->bhwij', bq, bk2) * QK_SCALE
            sim = jnp.where(mask, -jnp.finfo(sim.dtype).max, sim)
            attn = jax.nn.softmax(sim, -1)
            out = jnp.einsum('bhwij,bhwje->bhwie', attn, bv2)
            return out.reshape(b, h, n, d)

        def attn_layer(x, Wqkv, qs, ksc, Wo):
            b, n, _ = x.shape
            qkv = x @ Wqkv
            q, k, v = jnp.split(qkv, 3, -1)
            sh = lambda t: t.reshape(b, n, HEADS, DIM_HEAD).transpose(0, 2, 1, 3)
            q, k, v = (sh(q), sh(k), sh(v))
            q = l2norm(q) * qs
            k = l2norm(k) * ksc
            freqs, scale = rotary_tables(n)
            cos, sin = (jnp.cos(freqs), jnp.sin(freqs))
            q = q * cos * scale + rotate_half(q) * sin * scale
            inv = 1.0 / scale
            k = k * cos * inv + rotate_half(k) * sin * inv
            out = local_attention(q, k, v)
            out = out.transpose(0, 2, 1, 3).reshape(b, n, INNER)
            return out @ Wo

        def ffn_layer(x, g, bln, W1, b1, W2, b2):
            mu = x.mean(-1, keepdims=True)
            var = ((x - mu) ** 2).mean(-1, keepdims=True)
            xn = (x - mu) / jnp.sqrt(var + 1e-05) * g + bln
            hg = xn @ W1 + b1
            a, gate = jnp.split(hg, 2, -1)
            return a * jax.nn.gelu(gate, approximate=False) @ W2 + b2
        key = jax.random.key(seed)
        ks = jax.random.split(key, 8)
        B, N = (2, 256)
        init = lambda k, shape: jax.random.normal(k, shape, jnp.float32) * 0.02
        return {'x': jax.random.normal(ks[0], (B, N, DIM), jnp.float32), 'Wqkv': init(ks[1], (DEPTH, DIM, 3 * INNER)), 'q_scale': jnp.ones((DEPTH, DIM_HEAD), jnp.float32), 'k_scale': jnp.ones((DEPTH, DIM_HEAD), jnp.float32), 'Wo': init(ks[2], (DEPTH, INNER, DIM)), 'ln_g': jnp.ones((DEPTH, DIM), jnp.float32), 'ln_b': jnp.zeros((DEPTH, DIM), jnp.float32), 'W1': init(ks[3], (DEPTH, DIM, 2 * DIM_INNER)), 'b1': jnp.zeros((DEPTH, 2 * DIM_INNER), jnp.float32), 'W2': init(ks[4], (DEPTH, DIM_INNER, DIM)), 'b2': jnp.zeros((DEPTH, DIM), jnp.float32)}
    _L1_ffn_in = _L1_ffn_setup()
    _d = {'L0_attn_x': _L0_attn_in['x'], 'L0_attn_Wq': _L0_attn_in['Wq'], 'L0_attn_Wk': _L0_attn_in['Wk'], 'L0_attn_Wv': _L0_attn_in['Wv'], 'L0_attn_Wproj': _L0_attn_in['Wproj'], 'L0_attn_lambda_q1': _L0_attn_in['lambda_q1'], 'L0_attn_lambda_k1': _L0_attn_in['lambda_k1'], 'L0_attn_lambda_q2': _L0_attn_in['lambda_q2'], 'L0_attn_lambda_k2': _L0_attn_in['lambda_k2'], 'L0_ffn_weight': _L0_ffn_in['weight'], 'L0_ffn_bias': _L0_ffn_in['bias'], 'L1_attn_Wq': _L1_attn_in['Wq'], 'L1_attn_Wk': _L1_attn_in['Wk'], 'L1_attn_Wv': _L1_attn_in['Wv'], 'L1_attn_Wo': _L1_attn_in['Wo'], 'L1_attn_bo': _L1_attn_in['bo'], 'L1_ffn_Wqkv': _L1_ffn_in['Wqkv'], 'L1_ffn_q_scale': _L1_ffn_in['q_scale'], 'L1_ffn_k_scale': _L1_ffn_in['k_scale'], 'L1_ffn_Wo': _L1_ffn_in['Wo'], 'L1_ffn_ln_g': _L1_ffn_in['ln_g'], 'L1_ffn_ln_b': _L1_ffn_in['ln_b'], 'L1_ffn_W1': _L1_ffn_in['W1'], 'L1_ffn_b1': _L1_ffn_in['b1'], 'L1_ffn_W2': _L1_ffn_in['W2'], 'L1_ffn_b2': _L1_ffn_in['b2']}
    _x0 = _d['L0_attn_x']
    _d['L0_attn_x'] = jax.random.normal(jax.random.fold_in(jax.random.key(seed), 1), (8, 512, 128), dtype=_x0.dtype)
    del _x0
    return _d

def reference(L0_attn_x, L0_attn_Wq, L0_attn_Wk, L0_attn_Wv, L0_attn_Wproj, L0_attn_lambda_q1, L0_attn_lambda_k1, L0_attn_lambda_q2, L0_attn_lambda_k2, L0_ffn_weight, L0_ffn_bias, L1_attn_Wq, L1_attn_Wk, L1_attn_Wv, L1_attn_Wo, L1_attn_bo, L1_ffn_Wqkv, L1_ffn_q_scale, L1_ffn_k_scale, L1_ffn_Wo, L1_ffn_ln_g, L1_ffn_ln_b, L1_ffn_W1, L1_ffn_b1, L1_ffn_W2, L1_ffn_b2):

    def _L0_attn_ref(x, Wq, Wk, Wv, Wproj, lambda_q1, lambda_k1, lambda_q2, lambda_k2):
        import jax, jax.numpy as jnp
        import numpy as np
        N_HEAD = 16
        D_MODEL = 128
        HEAD_DIM = D_MODEL // N_HEAD
        LAMBDA_INIT = 0.8 - 0.6 * float(np.exp(-0.3 * 1))

        def _rms_norm(x):
            eps = jnp.finfo(x.dtype).eps
            return x * jax.lax.rsqrt(jnp.mean(jnp.square(x), axis=-1, keepdims=True) + eps)

        def _rotary_cos_sin(T, dim, base=10000.0):
            inv_freq = 1.0 / base ** (jnp.arange(0, dim, 2, dtype=jnp.float32) / dim)
            freqs = jnp.outer(jnp.arange(T, dtype=jnp.float32), inv_freq)
            return (jnp.cos(freqs), jnp.sin(freqs))

        def _apply_rotary(x, cos, sin):
            d = x.shape[-1] // 2
            c = cos[None, :, None, None, :]
            s = sin[None, :, None, None, :]
            x1, x2 = (x[..., :d], x[..., d:])
            return jnp.concatenate([x1 * c + x2 * s, -x1 * s + x2 * c], axis=-1)

        def _causal_attn(q, k, v, scale):
            T = q.shape[1]
            scores = jnp.einsum('bthd,bshd->bhts', q, k) * scale
            mask = jnp.tril(jnp.ones((T, T), dtype=bool))
            scores = jnp.where(mask, scores, -jnp.inf)
            w = jax.nn.softmax(scores, axis=-1)
            return jnp.einsum('bhts,bshd->bthd', w, v)
        B, T, D = x.shape
        nh, hd = (N_HEAD, HEAD_DIM)
        q = (x @ Wq.T).reshape(B, T, 2, nh // 2, hd)
        k = (x @ Wk.T).reshape(B, T, 2, nh // 2, hd)
        v = (x @ Wv.T).reshape(B, T, nh // 2, 2 * hd)
        q, k = (_rms_norm(q), _rms_norm(k))
        cos, sin = _rotary_cos_sin(T, hd)
        q, k = (_apply_rotary(q, cos, sin), _apply_rotary(k, cos, sin))
        q1, q2 = (q[:, :, 0], q[:, :, 1])
        k1, k2 = (k[:, :, 0], k[:, :, 1])
        scale = 1.0 / jnp.sqrt(jnp.asarray(hd, x.dtype))
        y1 = _causal_attn(q1, k1, v, scale)
        y2 = _causal_attn(q2, k2, v, scale)
        lambda_1 = jnp.exp(jnp.sum(lambda_q1 * lambda_k1))
        lambda_2 = jnp.exp(jnp.sum(lambda_q2 * lambda_k2))
        lambda_full = lambda_1 - lambda_2 + LAMBDA_INIT
        y = (y1 - lambda_full * y2).reshape(B, T, D)
        return y @ Wproj.T

    def _L0_ffn_ref(x, weight, bias):
        import jax, jax.numpy as jnp
        import numpy as np
        BLOCK_SIZE = 32
        FP6_E2M3_MAX = 7.5

        def _build_fp6_e2m3_grid():
            vals = set()
            for bits in range(64):
                s = bits >> 5 & 1
                e = bits >> 3 & 3
                m = bits & 7
                v = m / 8.0 if e == 0 else (1.0 + m / 8.0) * 2.0 ** (e - 1)
                vals.add(-v if s else v)
            return np.array(sorted(vals), dtype=np.float32)
        _GRID = jnp.asarray(_build_fp6_e2m3_grid())

        def _nearest_on_grid(x, grid):
            idx = jnp.clip(jnp.searchsorted(grid, x), 0, grid.shape[0] - 1)
            idx_lo = jnp.maximum(idx - 1, 0)
            v_hi = grid[idx]
            v_lo = grid[idx_lo]
            return jnp.where(jnp.abs(x - v_lo) <= jnp.abs(x - v_hi), v_lo, v_hi)

        def _mx_quantize(t, eps=1e-30):
            rows, K = t.shape
            blocks = t.reshape(rows, K // BLOCK_SIZE, BLOCK_SIZE)
            scales = jnp.maximum(jnp.max(jnp.abs(blocks), axis=-1) / FP6_E2M3_MAX, eps)
            q = _nearest_on_grid(blocks / scales[..., None], _GRID)
            return (q, scales)
        batch_shape = x.shape[:-1]
        in_features = x.shape[-1]
        x2 = x.astype(jnp.float32).reshape(-1, in_features)
        w2 = weight.astype(jnp.float32)
        xq, xs = _mx_quantize(x2)
        wq, ws = _mx_quantize(w2)
        xd = (xq * xs[..., None]).reshape(x2.shape)
        wd = (wq * ws[..., None]).reshape(w2.shape)
        out = xd @ wd.T + bias
        return out.reshape(*batch_shape, -1)

    def _L1_attn_ref(x, Wq, Wk, Wv, Wo, bo):
        import jax, jax.numpy as jnp
        import numpy as np
        D_MODEL = 128
        NUM_HEADS = 16
        HEAD_DIM = D_MODEL // NUM_HEADS
        EPS = 1e-08
        B, T, _ = x.shape
        H, D = (NUM_HEADS, HEAD_DIM)
        scale = jnp.sqrt(jnp.asarray(D, dtype=x.dtype))
        q = (x @ Wq.T).reshape(B, T, H, D).transpose(0, 2, 1, 3)
        k = (x @ Wk.T).reshape(B, T, H, D).transpose(0, 2, 1, 3)
        v = (x @ Wv.T).reshape(B, T, H, D).transpose(0, 2, 1, 3)
        s = jnp.einsum('bhtd,bhsd->bhts', q, k) / scale
        m = jnp.max(s, axis=-1, keepdims=True)
        e = jnp.exp(s - m)
        num = jnp.einsum('bhts,bhsd->bhtd', e, v)
        den = jnp.sum(e, axis=-1, keepdims=True) + EPS
        out = (num / den).transpose(0, 2, 1, 3).reshape(B, T, H * D)
        return out @ Wo.T + bo

    def _L1_ffn_ref(x, Wqkv, q_scale, k_scale, Wo, ln_g, ln_b, W1, b1, W2, b2):
        import jax, jax.numpy as jnp
        import numpy as np
        DIM = 128
        DEPTH = 6
        HEADS = 16
        DIM_HEAD = 64
        WINDOW = 32
        INNER = HEADS * DIM_HEAD
        DIM_INNER = int(DIM * 4 * 2 / 3)
        QK_SCALE = 8.0

        def shift_tokens(t):
            a, s = jnp.split(t, 2, -1)
            s = jnp.pad(s, ((0, 0), (1, 0), (0, 0)))[:, :-1]
            return jnp.concatenate([a, s], -1)

        def l2norm(t):
            return t / jnp.maximum(jnp.linalg.norm(t, axis=-1, keepdims=True), 1e-12)

        def rotate_half(x):
            x1, x2 = jnp.split(x, 2, -1)
            return jnp.concatenate([-x2, x1], -1)

        def rotary_tables(n):
            half = jnp.arange(0, DIM_HEAD, 2, dtype=jnp.float32)
            inv_freq = 1.0 / 10000.0 ** (half / DIM_HEAD)
            t = jnp.arange(n, dtype=jnp.float32)
            freqs = t[:, None] * inv_freq[None, :]
            freqs = jnp.concatenate([freqs, freqs], -1)
            base_scale = (half + 0.4 * DIM_HEAD) / (1.4 * DIM_HEAD)
            power = (t - n // 2) / (WINDOW // 2)
            scale = base_scale[None, :] ** power[:, None]
            scale = jnp.concatenate([scale, scale], -1)
            return (freqs, scale)

        def local_attention(q, k, v):
            b, h, n, d = q.shape
            w = WINDOW
            nw = n // w
            bq = q.reshape(b, h, nw, w, d)
            bk = k.reshape(b, h, nw, w, d)
            bv = v.reshape(b, h, nw, w, d)

            def look(t):
                p = jnp.pad(t, ((0, 0), (0, 0), (1, 0), (0, 0), (0, 0)))
                return jnp.concatenate([p[:, :, :nw], p[:, :, 1:]], axis=3)
            bk2, bv2 = (look(bk), look(bv))
            seq = jnp.arange(n).reshape(nw, w)
            seq_p = jnp.pad(seq, ((1, 0), (0, 0)), constant_values=-1)
            jt = jnp.concatenate([seq_p[:nw], seq_p[1:]], axis=1)
            it = seq[:, :, None]
            jb = jt[:, None, :]
            mask = (it < jb) | (it > jb + w) | (jb == -1)
            sim = jnp.einsum('bhwie,bhwje->bhwij', bq, bk2) * QK_SCALE
            sim = jnp.where(mask, -jnp.finfo(sim.dtype).max, sim)
            attn = jax.nn.softmax(sim, -1)
            out = jnp.einsum('bhwij,bhwje->bhwie', attn, bv2)
            return out.reshape(b, h, n, d)

        def attn_layer(x, Wqkv, qs, ksc, Wo):
            b, n, _ = x.shape
            qkv = x @ Wqkv
            q, k, v = jnp.split(qkv, 3, -1)
            sh = lambda t: t.reshape(b, n, HEADS, DIM_HEAD).transpose(0, 2, 1, 3)
            q, k, v = (sh(q), sh(k), sh(v))
            q = l2norm(q) * qs
            k = l2norm(k) * ksc
            freqs, scale = rotary_tables(n)
            cos, sin = (jnp.cos(freqs), jnp.sin(freqs))
            q = q * cos * scale + rotate_half(q) * sin * scale
            inv = 1.0 / scale
            k = k * cos * inv + rotate_half(k) * sin * inv
            out = local_attention(q, k, v)
            out = out.transpose(0, 2, 1, 3).reshape(b, n, INNER)
            return out @ Wo

        def ffn_layer(x, g, bln, W1, b1, W2, b2):
            mu = x.mean(-1, keepdims=True)
            var = ((x - mu) ** 2).mean(-1, keepdims=True)
            xn = (x - mu) / jnp.sqrt(var + 1e-05) * g + bln
            hg = xn @ W1 + b1
            a, gate = jnp.split(hg, 2, -1)
            return a * jax.nn.gelu(gate, approximate=False) @ W2 + b2
        for i in range(DEPTH):
            x = attn_layer(shift_tokens(x), Wqkv[i], q_scale[i], k_scale[i], Wo[i]) + x
            x = ffn_layer(shift_tokens(x), ln_g[i], ln_b[i], W1[i], b1[i], W2[i], b2[i]) + x
        return x
    x = L0_attn_x
    xn = _layernorm(x, axis=-1)
    x = x + _L0_attn_ref(xn, L0_attn_Wq, L0_attn_Wk, L0_attn_Wv, L0_attn_Wproj, L0_attn_lambda_q1, L0_attn_lambda_k1, L0_attn_lambda_q2, L0_attn_lambda_k2) + _L0_ffn_ref(xn, L0_ffn_weight, L0_ffn_bias)
    xn = _layernorm(x, axis=-1)
    x = x + _L1_attn_ref(xn, L1_attn_Wq, L1_attn_Wk, L1_attn_Wv, L1_attn_Wo, L1_attn_bo) + _L1_ffn_ref(xn, L1_ffn_Wqkv, L1_ffn_q_scale, L1_ffn_k_scale, L1_ffn_Wo, L1_ffn_ln_g, L1_ffn_ln_b, L1_ffn_W1, L1_ffn_b1, L1_ffn_W2, L1_ffn_b2)
    return x

_drawn_inputs = setup_inputs


def setup_inputs(seed=0):
    import zlib

    import numpy as np

    out = dict(_drawn_inputs(seed))
    spreads = {'L1_attn_bo': (0.0, 0.577),
     'L1_ffn_q_scale': (1.0, 0.6),
     'L1_ffn_k_scale': (1.0, 0.6),
     'L1_ffn_ln_g': (1.0, 0.6),
     'L1_ffn_ln_b': (0.0, 0.8),
     'L1_ffn_b1': (0.0, 0.8),
     'L1_ffn_b2': (0.0, 0.1)}
    factors = {'L0_attn_Wq': 8.0,
     'L0_attn_Wk': 8.0,
     'L0_attn_Wv': 8.0,
     'L0_attn_Wproj': 8.0,
     'L0_attn_lambda_q1': 8.0,
     'L0_attn_lambda_k1': 8.0,
     'L0_attn_lambda_q2': 8.0,
     'L0_attn_lambda_k2': 8.0,
     'L0_ffn_bias': 2.889,
     'L1_attn_Wq': 8.0,
     'L1_attn_Wk': 8.0,
     'L1_attn_Wv': 8.0,
     'L1_attn_Wo': 8.0,
     'L1_ffn_W1': 3.69,
     'L1_ffn_W2': 3.628}
    for name, (base, spread) in spreads.items():
        noise = np.random.default_rng([zlib.crc32(name.encode()), seed]).standard_normal(out[name].shape)
        drawn = base * np.exp(spread * noise) if base else spread * noise
        out[name] = jnp.asarray(drawn.astype(out[name].dtype))
    for name, factor in factors.items():
        out[name] = (out[name] * factor).astype(out[name].dtype)
    return out
```

```python
from contextlib import ExitStack

import numpy as np

import concourse.bass as bass
from concourse import mybir

F32 = mybir.dt.float32
BF16 = mybir.dt.bfloat16
ALU = mybir.AluOpType
ACT = mybir.ActivationFunctionType
AX = mybir.AxisListType

P = 128
D = 128
B = 8
T = 512
NT = T // P
SLOTS = NT + 1
NEG = -1e30
H = 16
HD = D // H
HV0 = 2 * HD
NV0 = H // 2
PAD = 32
DEPTH = 6
DH = 64
INNER = H * DH
WIN = 32
DI = int(D * 4 * 2 / 3)
DCH = 3
DLAST = DI - 2 * P
LAMBDA_INIT = 0.8 - 0.6 * float(np.exp(-0.3 * 1))
MAGIC = 1.5 * 2.0 ** 23
PAIRS = B // 2

C_ID, C_SH, C_ED, C_BAND, C_TRI, C_PREV = 0, 128, 256, 384, 512, 640
C_ROT = 672
C_XP = C_ROT + 2 * NT * HD
C_ALL = C_XP + 4 * NT * DH


def constants():
    c = np.zeros((P, C_ALL), np.float32)
    i = np.arange(P)
    c[:, C_ID:C_ID + P] = np.eye(P)
    c[i[:-1], C_SH + i[1:]] = 1.0
    c[P - 1, C_ED] = 1.0
    q, k = i[:, None], i[None, :]
    c[:, C_BAND:C_BAND + P] = np.where((k <= q) & (q - k <= WIN), 0.0, NEG)
    c[:, C_TRI:C_TRI + P] = np.where(q <= k, 0.0, NEG)
    w = np.arange(WIN)
    c[:WIN, C_PREV:C_PREV + WIN] = np.where(w[None, :] >= w[:, None], 0.0, NEG)
    pos = np.arange(T, dtype=np.float64).reshape(NT, P).T
    f = 1.0 / 10000.0 ** (np.arange(0, HD, 2) / HD)
    a = pos[:, :, None] * f
    rot = np.stack([np.concatenate([np.cos(a), np.cos(a)], -1),
                    np.concatenate([np.sin(a), -np.sin(a)], -1)], 1)
    c[:, C_ROT:C_XP] = rot.reshape(P, -1)
    half = np.arange(0, DH, 2)
    a = pos[:, :, None] * (1.0 / 10000.0 ** (half / DH))
    s = ((half + 0.4 * DH) / (1.4 * DH)) ** ((pos[:, :, None] - T // 2) / (WIN // 2))
    cos, sin = np.cos(a), np.sin(a)
    xp = [np.concatenate([cos * s, cos * s], -1), np.concatenate([-sin * s, sin * s], -1),
          np.concatenate([cos / s, cos / s], -1) * 8.0, np.concatenate([-sin / s, sin / s], -1) * 8.0]
    c[:, C_XP:] = np.stack(xp, 1).reshape(P, -1)
    return c


def program(nc, x, consts, wqkv0, wproj0, wff0, rows0, wqkv1, wo1, wqkv, wo, qkscale, w1, w2, cols, b2, out):
    with ExitStack() as outer:
        def sb(name, shape, dt=F32, ctx=outer):
            return ctx.enter_context(nc.sbuf_tensor(name, shape, dt))

        PS = outer.enter_context(nc.psum_tensor("PS", [P, 8, 512], F32))
        CT = sb("CT", [P, C_ALL])
        ident = CT[:, C_ID:C_ID + P]
        identb = sb("identb", [P, P], BF16)
        bandb = sb("bandb", [P, P], BF16)
        trib = sb("trib", [P, P], BF16)
        prevb = sb("prevb", [P, WIN], BF16)
        nhalf = sb("nhalf", [P, 128])
        X1 = sb("X1", [P, B * NT, D])
        XL = sb("XL", [P, B, SLOTS, D])

        I32 = mybir.dt.int32

        def rsqrt(link, y, v, t):
            link(nc.vector.tensor_scalar(y.bitcast(I32), v.bitcast(I32), -0.5, float(0x5F3759DF), ALU.mult, ALU.add))
            for _ in range(3):
                link(nc.vector.tensor_tensor(t, y, y, ALU.mult))
                link(nc.vector.scalar_tensor_tensor(out=t, in0=t, scalar=-0.5, in1=v, op0=ALU.mult, op1=ALU.mult))
                link(nc.vector.scalar_tensor_tensor(out=y, in0=t, scalar=1.5, in1=y, op0=ALU.add, op1=ALU.mult))

        NRS = 10

        used = []

        def scoped(ctx, name):
            used.append(ctx.enter_context(nc.semaphore(name)))
            return used[-1]

        def phase(ctx):
            mine = used[:]
            used.clear()

            def clear():
                with nc.Block() as block:
                    @block.gpsimd
                    def _(pool):
                        for s in mine:
                            pool.sem_clear(s)

            ctx.callback(clear)
            return ctx.enter_context(nc.Block())

        def normalise_rows(block, src, sem, sums, sqs, loaded=None):
            s_sum, s_cen, s_sq, s_var, s_pow, s_ch = sem

            @block.vector
            def _(dve):
                for b in range(B):
                    s = src[:, b * NT:b * NT + NT, :]
                    o = XL[:, b, 1:SLOTS, :]
                    if loaded is not None:
                        dve.wait_ge(loaded[b], 16)
                    dve.tensor_reduce(sums[:, b, :], s, AX.X, ALU.add).then_inc(s_ch, 1)
                    dve.wait_ge(s_ch, 2 * b + 1)
                    dve.tensor_scalar(sums[:, b, :], sums[:, b, :], -1.0 / D, None, ALU.mult).then_inc(s_ch, 1)
                    dve.wait_ge(s_ch, 2 * b + 2)
                    dve.tensor_tensor(o, s, sums[:, b, :].unsqueeze(2).to_broadcast([P, NT, D]), ALU.add).then_inc(s_cen, 1)
                for b in range(B):
                    dve.wait_ge(s_sq, b + 1)
                    dve.tensor_reduce(sums[:, b, :], sqs[:, b % 2, :, :], AX.X, ALU.add).then_inc(s_sum, 1)
                    dve.wait_ge(s_sum, b + 1)
                    dve.tensor_scalar(sums[:, b, :], sums[:, b, :], 1.0 / D, 1e-5, ALU.mult, ALU.add).then_inc(s_var, 1)
                    dve.wait_ge(s_pow, b + 1)
                    o = XL[:, b, 1:SLOTS, :]
                    dve.tensor_tensor(o, o, sums[:, b, :].unsqueeze(2).to_broadcast([P, NT, D]), ALU.mult)

            @block.scalar
            def _(act):
                for b in range(B):
                    act.wait_ge(s_cen, b + 1)
                    if b >= 2:
                        act.wait_ge(s_sum, b - 1)
                    act.activation(sqs[:, b % 2, :, :], XL[:, b, 1:SLOTS, :], ACT.Square).then_inc(s_sq, 1)

            @block.gpsimd
            def _(pool):
                for b in range(B):
                    pool.wait_ge(s_var, b + 1)
                    pool.tensor_tensor(sums[:, b, :], sums[:, b, :], nhalf[:, 0:NT], ALU.pow).then_inc(s_pow, 1)

        with ExitStack() as ctx:
            X0 = sb("X0", [P, B * NT, D], F32, ctx)
            W0 = sb("W0", [P, 3 * D], F32, ctx)
            WP0 = sb("WP0", [P, D], F32, ctx)
            WF0 = sb("WF0", [P, D], F32, ctx)
            WFT = sb("WFT", [P, D], F32, ctx)
            W1q = sb("W1q", [P, 3 * D], F32, ctx)
            WO1 = sb("WO1", [P, D], F32, ctx)
            ROWS = sb("ROWS", [P, 2 * D + 16], F32, ctx)
            bias0, bias1, lamv = ROWS[:, 0:D], ROWS[:, D:2 * D], ROWS[:, 2 * D:]
            lam = sb("lam", [P, 8], F32, ctx)
            sums = sb("sums", [P, B, NT], F32, ctx)
            sqs = sb("sqs", [P, 2, NT, D], F32, ctx)
            xs = sb("xs", [P, NT, D], F32, ctx)
            xT = sb("xT", [P, T], F32, ctx)
            sq = sb("sq", [P, NT, 2 * D], F32, ctx)
            qn = sb("qn", [P, NT, 2 * D], F32, ctx)
            ra = sb("ra", [P, NT, 2 * D], F32, ctx)
            rms = sb("rms", [P, NT, 2 * H], F32, ctx)
            QP = sb("QP", [P, NT, 2, H, PAD], F32, ctx)
            QT = sb("QT", [P, 4, T], F32, ctx)
            KT = sb("KT", [P, 4, T], F32, ctx)
            V1 = sb("V1", [P, NT, NV0, HV0 + 1], F32, ctx)
            V2 = sb("V2", [P, NT, H, HD + 1], F32, ctx)
            PT = sb("PT", [P, 2, NT * T], F32, ctx)
            Y = sb("Y", [P, NT, D], F32, ctx)
            yt = sb("yt", [P, NT, 4, HV0], F32, ctx)
            rec = sb("rec", [P, 2, NT, 4], F32, ctx)
            YT = sb("YT", [P, T], F32, ctx)
            xd = sb("xd", [P, NT, D], F32, ctx)
            xdT = sb("xdT", [P, T], F32, ctx)
            qa = sb("qa", [P, NT * D], F32, ctx)
            qb = sb("qb", [P, NT * D], F32, ctx)
            qc = sb("qc", [P, NT * D], F32, ctx)
            qs = sb("qs", [P, 2, 16], F32, ctx)

            with ExitStack() as c2:
                def sem(name):
                    return scoped(c2, name)

                s_ld = [sem(f"x_loaded{b}") for b in range(B)]
                s_cst = sem("constants_loaded")
                s_mem = sem("memsets_done")
                names = [sem(n) for n in ("ln0_sum", "ln0_centred", "ln0_sq", "ln0_var", "ln0_pow", "ln0_chain")]
                block = phase(c2)

                @block.sync
                def _(sp):
                    xv = x.rearrange("b (t p) d -> p b t d", p=P)
                    for b in range(B):
                        sp.dma_start(X0[:, b * NT:b * NT + NT, :], xv[:, b]).then_inc(s_ld[b], 16)
                    for dst, src in ((CT, consts), (W0, wqkv0), (WP0, wproj0), (WF0, wff0), (ROWS, rows0), (W1q, wqkv1), (WO1, wo1)):
                        sp.dma_start(dst[:, :], src).then_inc(s_cst, 16)
                    sp.wait_ge(s_cst, 7 * 16)

                @block.gpsimd
                def _(pool):
                    pool.memset(nhalf[:, :], -0.5).then_inc(s_mem, 1)
                    pool.memset(QP[:, :, :, :, :], 0.0).then_inc(s_mem, 1)
                    pool.memset(V1[:, :, :, :], 1.0).then_inc(s_mem, 1)
                    pool.memset(V2[:, :, :, :], 1.0).then_inc(s_mem, 1)
                    for b in range(B):
                        pool.memset(XL[:, b, 0, :], 0.0).then_inc(s_mem, 1)
                    pool.wait_ge(s_mem, 4 + B)
                    pool.memset(QP[:, :, 1, :, HD:HD + 1], 1.0)

                normalise_rows(block, X0, names, sums, sqs, s_ld)

            with ExitStack() as c2:
                def sem(name):
                    return scoped(c2, name)

                s_lam = sem("lambda_chain")
                s_exp = sem("lambda_exp")
                block = phase(c2)

                @block.vector
                def _(dve):
                    dve.tensor_copy(identb[:, :], ident)
                    dve.tensor_copy(bandb[:, :], CT[:, C_BAND:C_BAND + P])
                    dve.tensor_copy(trib[:, :], CT[:, C_TRI:C_TRI + P])
                    dve.tensor_copy(prevb[:, :], CT[:, C_PREV:C_PREV + WIN])
                    dve.tensor_tensor(qa[:, 0:8], lamv[:, 0:8], lamv[:, 8:16], ALU.mult).then_inc(s_lam, 1)
                    dve.wait_ge(s_lam, 1)
                    dve.tensor_reduce(lam[:, 0:2], qa[:, 0:8].rearrange("p (a c) -> p a c", a=2), AX.X, ALU.add).then_inc(s_lam, 1)
                    dve.wait_ge(s_exp, 1)
                    dve.tensor_tensor(lam[:, 4:5], lam[:, 3:4], lam[:, 2:3], ALU.subtract).then_inc(s_lam, 1)
                    dve.wait_ge(s_lam, 3)
                    dve.tensor_scalar(lam[:, 5:6], lam[:, 4:5], -LAMBDA_INIT, None, ALU.add).then_inc(s_lam, 1)

                @block.scalar
                def _(act):
                    act.wait_ge(s_lam, 2)
                    act.activation(lam[:, 2:4], lam[:, 0:2], ACT.Exp).then_inc(s_exp, 1)

            nlam = lam[:, 5:6]

            def fake_quant(link, src, dst, nblk):
                n = nblk * 32
                v, a, bb = qa[:, 0:n], qb[:, 0:n], qc[:, 0:n]
                blk = lambda t: t.rearrange("p (n k) -> p n k", k=32)
                sc, rs = qs[:, 0, 0:nblk], qs[:, 1, 0:nblk]
                wide = lambda t: t.unsqueeze(2).to_broadcast([P, nblk, 32])
                e = nc.vector
                link(e.tensor_reduce(sc, blk(src), AX.X, ALU.max, apply_absolute_value=True))
                link(e.tensor_scalar(sc, sc, 1.0 / 7.5, 1e-30, ALU.mult, ALU.max))
                link(e.reciprocal(rs, sc))
                link(e.tensor_tensor(blk(v), blk(src), wide(rs), ALU.mult))
                link(e.tensor_tensor(a, v, v, ALU.mult))
                link(e.tensor_scalar(bb, a, 16.0, 0.25, ALU.is_ge, ALU.mult))
                link(e.tensor_scalar(a, a, 4.0, 0.125, ALU.is_ge, ALU.mult))
                link(e.scalar_tensor_tensor(out=a, in0=a, scalar=0.125, in1=bb, op0=ALU.add, op1=ALU.add))
                link(e.reciprocal(bb, a))
                link(e.tensor_tensor(v, v, bb, ALU.mult))
                link(e.tensor_scalar(v, v, -0.5, None, ALU.add))
                link(e.tensor_scalar(bb, v, MAGIC, None, ALU.add))
                link(e.tensor_scalar(bb, bb, -MAGIC, None, ALU.add))
                link(e.tensor_tensor(v, bb, v, ALU.is_lt))
                link(e.tensor_tensor(v, v, bb, ALU.add))
                link(e.tensor_tensor(v, v, a, ALU.mult))
                return e.tensor_tensor(blk(dst), blk(v), wide(sc), ALU.mult)
            NQ = 17

            with ExitStack() as c2:
                def sem(name):
                    return scoped(c2, name)

                s_ch, s_wt = sem("wquant_chain"), sem("wquant_transposed")
                block = phase(c2)

                @block.vector
                def _(dve):
                    n = [0]

                    def link(ins):
                        n[0] += 1
                        ins.then_inc(s_ch, 1)
                        dve.wait_ge(s_ch, n[0])

                    link(fake_quant(link, WF0[:, :], WF0[:, :], 4))
                    dve.wait_ge(s_wt, 1)
                    dve.tensor_copy(WFT[:, :], PS[:, 0, 0:P])

                @block.tensor
                def _(pe):
                    pe.wait_ge(s_ch, NQ)
                    pe.transpose(PS[:, 0, 0:P], WF0[:, :], ident).then_inc(s_wt, 1)

            def attention(first):
                with ExitStack() as c2:
                    def sem(name):
                        return scoped(c2, f"a{0 if first else 1}_{name}")

                    s_xs, s_xT, s_xTr, s_qkv = sem("xs"), sem("xT"), sem("xT_sbuf"), sem("qkv")
                    s_sq, s_ms, s_r, s_qp, s_ch = sem("squares"), sem("meansq"), sem("rms"), sem("qk_padded"), sem("dve_chain")
                    s_qt, s_kt, s_qe, s_ke = sem("q_transposed"), sem("k_transposed"), sem("qT_sbuf"), sem("kT_sbuf")
                    s_mp, s_mx, s_mxd, s_q2, s_q2e = sem("max_scores"), sem("max_taken"), sem("max_all"), sem("q_transposed2"), sem("qT2_sbuf")
                    s_sc, s_ex, s_y, s_yn = sem("scores"), sem("exps"), sem("values_summed"), sem("heads_done")
                    s_yt, s_ye, s_xd, s_xt, s_xe = sem("y_transposed"), sem("yT_sbuf"), sem("xd"), sem("xd_transposed"), sem("xdT_sbuf")
                    s_pr, s_bt = sem("projected"), sem("batch_done")
                    block = phase(c2)
                    wqkv_, wo_, bias_ = (W0, WP0, bias0) if first else (W1q, WO1, bias1)
                    hv = HV0 if first else HD
                    V = V1 if first else V2
                    scale = float(HD) ** -0.5
                    K = HD if first else HD + 1
                    NC = 48 if first else 15
                    GH = 4

                    def keys(jt):
                        if not first:
                            return jt * T, 0
                        return (0, T, 2 * T, T + 3 * P)[jt], jt * P

                    @block.gpsimd
                    def _(pool):
                        pool.memset(nhalf[:, 127:128], -0.5).then_inc(s_bt, 1)
                        with pool.Fori(0, B) as b:
                            pool.wait_ge(s_bt, b + 1)
                            pool.tensor_copy(xs[:, :, :], XL[:, b, 1:SLOTS, :]).then_inc(s_xs, 1)
                            if first:
                                pool.wait_ge(s_ms, b + 1)
                                pool.tensor_tensor(rms[:, :, :], rms[:, :, :],
                                                   nhalf[:, :].rearrange("p (t h) -> p t h", t=NT), ALU.pow).then_inc(s_r, 1)

                    @block.tensor
                    def _(pe):
                        def transposes(which, done, bank):
                            for g in range(4):
                                for t in range(NT):
                                    ins = pe.transpose(PS[:, bank + g, t * P:t * P + P],
                                                       QP[:, t, which, 4 * g:4 * g + 4, :].rearrange("p h k -> p (h k)"), ident)
                            ins.then_inc(done, 1)

                        with pe.Fori(0, B) as b:
                            pe.wait_ge(s_xs, b + 1)
                            for t in range(NT):
                                ins = pe.transpose(PS[:, 0, t * P:t * P + P], xs[:, t, :], ident)
                            ins.then_inc(s_xT, 1)
                            pe.wait_ge(s_xTr, b + 1)
                            for t in range(NT):
                                ins = pe.matmul(PS[:, t, 0:3 * D], xT[:, t * P:t * P + P], wqkv_[:, :], start=True, stop=True)
                            ins.then_inc(s_qkv, 1)
                            pe.wait_ge(s_qp, b + 1)
                            transposes(0, s_qt, 0)
                            transposes(1, s_kt, 4)
                            pe.wait_ge(s_qe, b + 1)
                            pe.wait_ge(s_ke, b + 1)
                            if not first:
                                for h in range(H):
                                    g, r = h // 4, PAD * (h % 4)
                                    for a in range(2):
                                        m = 2 * h + a
                                        if m >= 2:
                                            pe.wait_ge(s_mx, b * 2 * H + m - 1)
                                        for i in range(2):
                                            it = 2 * a + i
                                            ins = pe.matmul(PS[:, 2 * (m % 2) + i, :], QT[r:r + HD, g, it * P:it * P + P],
                                                            KT[r:r + HD, g, :], start=True, stop=True)
                                        ins.then_inc(s_mp, 1)
                                pe.wait_ge(s_mx, (b + 1) * 2 * H)
                                transposes(0, s_q2, 0)
                                pe.wait_ge(s_q2e, b + 1)

                            def scores(h):
                                g, r = h // 4, PAD * (h % 4)
                                q, k = QT[r:r + K, g, :], KT[r:r + K, g, :]
                                if first:
                                    if h >= 2:
                                        pe.wait_ge(s_ex, b * H + h - 1)
                                    base = 3 * (h % 2)
                                    for jt in range(NT):
                                        n = T - jt * P
                                        o = PS[:, base + (0, 1, 2, 1)[jt], (0, 0, 0, 3 * P)[jt]:]
                                        pe.matmul(o[:, 0:n], k[:, jt * P:jt * P + P], q[:, jt * P:T], start=True, stop=False)
                                        ins = pe.matmul(o[:, 0:P], identb[:, :], trib[:, :], start=False, stop=True)
                                    ins.then_inc(s_sc, 1)
                                else:
                                    for a in range(2):
                                        m = 2 * h + a
                                        if m >= 2:
                                            pe.wait_ge(s_ex, b * 2 * H + m - 1)
                                        for i in range(2):
                                            jt = 2 * a + i
                                            ins = pe.matmul(PS[:, 2 * (m % 2) + i, :], k[:, jt * P:jt * P + P], q, start=True, stop=True)
                                        ins.then_inc(s_sc, 1)

                            def values(h):
                                if first:
                                    pe.wait_ge(s_ex, b * H + h + 1)
                                else:
                                    pe.wait_ge(s_ex, b * 2 * H + 2 * h + 2)
                                gr = h // GH
                                if h % GH == 0 and gr >= 2:
                                    pe.wait_ge(s_yn, b * (H // GH) + gr - 1)
                                o = PS[:, 6 + gr % 2, 0:NT * GH * (hv + 1)].rearrange("p (t h e) -> p t h e", t=NT, h=GH)
                                for it in range(NT):
                                    last = it if first else NT - 1
                                    for jt in range(last + 1):
                                        at, q0 = keys(jt)
                                        at += it * P - q0
                                        ins = pe.matmul(o[:, it, h % GH, :], PT[:, h % 2, at:at + P], V[:, jt, h % NV0 if first else h, :],
                                                        start=(jt == 0), stop=(jt == last))
                                ins.then_inc(s_y, 1)

                            scores(0)
                            for h in range(H):
                                if h + 1 < H:
                                    scores(h + 1)
                                values(h)
                            if first:
                                pe.wait_ge(s_xd, b + 1)
                                for t in range(NT):
                                    ins = pe.transpose(PS[:, 1, t * P:t * P + P], xd[:, t, :], ident)
                                ins.then_inc(s_xt, 1)
                            pe.wait_ge(s_yn, (b + 1) * (H // GH))
                            for t in range(NT):
                                ins = pe.transpose(PS[:, 0, t * P:t * P + P], Y[:, t, :], ident)
                            ins.then_inc(s_yt, 1)
                            pe.wait_ge(s_ye, b + 1)
                            if first:
                                pe.wait_ge(s_xe, b + 1)
                            for t in range(NT):
                                o = PS[:, 2, t * P:t * P + P]
                                if first:
                                    pe.matmul(o, xdT[:, t * P:t * P + P], WFT[:, :], start=True, stop=False)
                                ins = pe.matmul(o, YT[:, t * P:t * P + P], wo_[:, :], start=not first, stop=True)
                            ins.then_inc(s_pr, 1)

                    @block.scalar
                    def _(act):
                        with act.Fori(0, B) as b:
                            act.wait_ge(s_xT, b + 1)
                            act.activation(xT[:, :], PS[:, 0, :], ACT.Copy).then_inc(s_xTr, 1)
                            if first:
                                act.wait_ge(s_qkv, b + 1)
                                act.activation(sq[:, :, :], PS[:, 0:NT, 0:2 * D], ACT.Square).then_inc(s_sq, 1)
                            act.wait_ge(s_qt, b + 1)
                            act.activation(QT[:, :, :], PS[:, 0:4, :], ACT.Copy).then_inc(s_qe, 1)
                            if not first:
                                act.wait_ge(s_q2, b + 1)
                                act.activation(QT[:, :, :], PS[:, 0:4, :], ACT.Copy).then_inc(s_q2e, 1)
                            for h in range(H):
                                if first:
                                    act.wait_ge(s_sc, b * H + h + 1)
                                    if h >= 2:
                                        act.wait_ge(s_y, b * H + h - 1)
                                    n = 10 * P
                                    act.activation(PT[:, h % 2, 0:n],
                                                   PS[:, 3 * (h % 2):3 * (h % 2) + 3, :].rearrange("p k n -> p (k n)")[:, 0:n],
                                                   ACT.Exp, scale=scale).then_inc(s_ex, 1)
                                else:
                                    if h >= 2:
                                        act.wait_ge(s_y, b * H + h - 1)
                                    for a in range(2):
                                        m = 2 * h + a
                                        act.wait_ge(s_sc, b * 2 * H + m + 1)
                                        act.activation(PT[:, h % 2, a * 2 * T:(a + 1) * 2 * T],
                                                       PS[:, 2 * (m % 2):2 * (m % 2) + 2, :].rearrange("p k n -> p (k n)"),
                                                       ACT.Exp, scale=scale).then_inc(s_ex, 1)
                            if first:
                                act.wait_ge(s_xt, b + 1)
                                act.activation(xdT[:, :], PS[:, 1, :], ACT.Copy).then_inc(s_xe, 1)
                            act.wait_ge(s_yt, b + 1)
                            act.activation(YT[:, :], PS[:, 0, :], ACT.Copy).then_inc(s_ye, 1)

                    @block.vector
                    def _(dve):
                        with dve.Fori(0, B) as b:
                            n = [0]

                            def link(ins):
                                n[0] += 1
                                ins.then_inc(s_ch, 1)
                                dve.wait_ge(s_ch, b * NC + n[0])

                            dve.wait_ge(s_qkv, b + 1)
                            qk = PS[:, 0:NT, 0:2 * D].rearrange("p t (h e) -> p t h e", e=HD)
                            v = PS[:, 0:NT, 2 * D:3 * D].rearrange("p t (h e) -> p t h e", e=hv)
                            heads = QP[:, :, :, :, 0:HD].rearrange("p t a h e -> p t (a h) e")
                            if first:
                                dve.wait_ge(s_sq, b + 1)
                            for t in range(NT):
                                nc.vector.tensor_copy(V[:, t, :, 0:hv], v[:, t])
                            if first:
                                link(nc.vector.tensor_reduce(rms[:, :, :], sq[:, :, :].rearrange("p t (h e) -> p t h e", e=HD), AX.X, ALU.add))
                                nc.vector.tensor_scalar(rms[:, :, :], rms[:, :, :], 1.0 / HD, float(np.finfo(np.float32).eps),
                                                        ALU.mult, ALU.add).then_inc(s_ms, 1)
                                dve.wait_ge(s_r, b + 1)
                                for t in range(NT):
                                    q_ = qn[:, t, :].rearrange("p (h e) -> p h e", e=HD)
                                    link(nc.vector.tensor_tensor(q_, qk[:, t], rms[:, t, :].unsqueeze(2).to_broadcast([P, 2 * H, HD]), ALU.mult))
                                rot = CT[:, C_ROT:C_XP].rearrange("p (a t e) -> p a t e", a=2, t=NT)
                                for t in range(NT):
                                    q_ = qn[:, t, :].rearrange("p (h e) -> p h e", e=HD)
                                    a_ = ra[:, t, :].rearrange("p (h e) -> p h e", e=HD)
                                    o_ = QP[:, t, :, :, 0:HD].rearrange("p a h e -> p (a h) e")
                                    half = HD // 2
                                    wide = lambda z, e: z.unsqueeze(1).to_broadcast([P, 2 * H, e])
                                    nc.vector.tensor_tensor(a_[:, :, 0:half], q_[:, :, half:HD], wide(rot[:, 1, t, 0:half], half), ALU.mult)
                                    link(nc.vector.tensor_tensor(a_[:, :, half:HD], q_[:, :, 0:half], wide(rot[:, 1, t, half:HD], half), ALU.mult))
                                    link(nc.vector.tensor_tensor(q_, q_, wide(rot[:, 0, t, :], HD), ALU.mult))
                                    ins = nc.vector.tensor_tensor(o_, q_, a_, ALU.add)
                            else:
                                for t in range(NT):
                                    ins = nc.vector.tensor_copy(QP[:, t, :, :, 0:HD].rearrange("p a h e -> p (a h) e"), qk[:, t])
                            ins.then_inc(s_qp, 1)
                            dve.wait_ge(s_kt, b + 1)
                            nc.vector.tensor_copy(KT[:, :, :], PS[:, 4:8, :]).then_inc(s_ke, 1)
                            if first:
                                fake_quant(link, xs[:, :, :].rearrange("p t d -> p (t d)"),
                                           xd[:, :, :].rearrange("p t d -> p (t d)"), 16).then_inc(s_xd, 1)
                            else:
                                for h in range(H):
                                    for a in range(2):
                                        m = 2 * h + a
                                        dve.wait_ge(s_mp, b * 2 * H + m + 1)
                                        for i in range(2):
                                            ins = nc.vector.tensor_reduce(QP[:, 2 * a + i, 0, h, HD:HD + 1], PS[:, 2 * (m % 2) + i, :],
                                                                          AX.X, ALU.max, negate=True)
                                        ins.then_inc(s_mx, 1)
                            for gr in range(H // GH):
                                dve.wait_ge(s_y, b * H + GH * (gr + 1))
                                o = PS[:, 6 + gr % 2, 0:NT * GH * (hv + 1)].rearrange("p (t h e) -> p t h e", t=NT, h=GH)
                                den, rc = o[:, :, :, hv], rec[:, gr % 2, :, :]
                                if not first:
                                    link(nc.vector.tensor_scalar(rc, den, 1e-8, None, ALU.add))
                                    den = rc
                                link(nc.vector.reciprocal(rc, den))
                                h0 = GH * gr if not first else GH * (gr % 2)
                                for t in range(NT):
                                    yo = Y[:, t, h0 * hv:(h0 + GH) * hv].rearrange("p (h e) -> p h e", e=hv)
                                    rw = rc[:, t, :].unsqueeze(2).to_broadcast([P, GH, hv])
                                    if first and gr >= 2:
                                        link(nc.vector.tensor_tensor(yt[:, t, :, :], o[:, t, :, 0:hv], rw, ALU.mult))
                                        ins = nc.vector.scalar_tensor_tensor(out=yo, in0=yt[:, t, :, :], scalar=nlam, in1=yo,
                                                                             op0=ALU.mult, op1=ALU.add)
                                    else:
                                        ins = nc.vector.tensor_tensor(yo, o[:, t, :, 0:hv], rw, ALU.mult)
                                ins.then_inc(s_yn, 1)
                            src = X0 if first else X1
                            dve.wait_ge(s_pr, b + 1)
                            for t in range(NT):
                                link(nc.vector.tensor_tensor(qn[:, 0, 0:D], PS[:, 2, t * P:t * P + P], bias_, ALU.add))
                                ins = nc.vector.tensor_tensor(X1[:, b * NT + t, :], src[:, b * NT + t, :], qn[:, 0, 0:D], ALU.add)
                                if t < NT - 1:
                                    link(ins)
                            ins.then_inc(s_bt, 1)
                            assert n[0] == NC, n[0]

            attention(True)

            with ExitStack() as c2:
                def sem(name):
                    return scoped(c2, name)

                names = [sem(n) for n in ("ln1_sum", "ln1_centred", "ln1_sq", "ln1_var", "ln1_pow", "ln1_chain")]
                block = phase(c2)
                normalise_rows(block, X1, names, sums, sqs)

            attention(False)

        with ExitStack() as ctx:
            XM = sb("XM", [P, B, SLOTS, D], F32, ctx)
            WQ = sb("WQ", [P, 3 * INNER], F32, ctx)
            WO = sb("WO", [P, INNER // P, D], F32, ctx)
            QK = sb("QK", [P, 2, DH], F32, ctx)
            WA = sb("WA", [P, 2 * DI], F32, ctx)
            WB = sb("WB", [P, DCH, D], F32, ctx)
            COL = sb("COL", [P, 2 + 2 * DCH], F32, ctx)
            B2 = sb("B2", [P, D], F32, ctx)
            TC = sb("TC", [P, NT, 2, DH], F32, ctx)
            TS = sb("TS", [P, NT, 2, DH], F32, ctx)

            def two(name, shape):
                return [sb(f"{name}{s}", shape, F32, ctx) for s in range(2)]

            xs = two("ls_xs", [P, NT, D])
            xsT = two("ls_xsT", [P, T])
            Q = two("ls_q", [P, 2 * INNER])
            A = two("ls_a", [P, 2 * INNER])
            R = two("ls_r", [P, 2 * INNER])
            qT = two("ls_qT", [P, H, P])
            kT = two("ls_kT", [P, 2, H // 2, P])
            VT = two("ls_v", [P, H + 1, DH + 1])
            VP = two("ls_vp", [WIN, H, DH + 1])
            Pp = two("ls_pp", [WIN, H, WIN])
            PTp = two("ls_ptp", [WIN, H, WIN])
            Y = [a[:, 0:INNER] for a in A]
            YT = [a[:, INNER:].rearrange("p (i n) -> p i n", n=P) for a in A]
            ss = two("ls_ss", [P, 2 * H])
            rn = two("ls_rn", [P, 2, 2 * H])
            mx = two("ls_mx", [P, 2, H])
            rc = two("ls_rc", [P, H])
            st = two("ls_st", [P, NT])

            def sem(name):
                return scoped(ctx, name)

            def sems(name):
                return [scoped(ctx, f"{name}{s}") for s in range(2)]

            w_attn, w_ffn = sem("attn_weights"), sem("ffn_weights")
            free_attn, free_ffn = sem("attn_weights_free"), sem("ffn_weights_free")
            s_tab = sem("tables")
            s_xl, s_xm = sems("stream_new"), sems("stream_mid")
            s_sh, s_xu, s_xlo, s_xt, s_xe = sems("shifted"), sems("xs_upper"), sems("xs_lower"), sems("xs_transposed"), sems("xsT_sbuf")
            s_qk, s_sq, s_qn = sems("qk"), sems("squares_qk"), sems("qk_normal")
            s_v, s_ve, s_a, s_b, s_rot = sems("v"), sems("v_sbuf"), sems("cos_term"), sems("sin_term"), sems("rotated")
            s_qt, s_qe, s_kt, s_ke = sems("lq_transposed"), sems("lqT_sbuf"), sems("lk_transposed"), sems("lkT_sbuf")
            s_sp, s_spe, s_so, s_sub = sems("prev_scores"), sems("prev_sbuf"), sems("own_scores"), sems("less_max")
            s_pe, s_p, s_pp, s_pt, s_pte = sems("prev_exp"), sems("own_exp"), sems("prev_expT"), sems("expT"), sems("expT_sbuf")
            s_o, s_vp, s_yn, s_yt, s_ye, s_w = sems("weighted"), sems("prev_v"), sems("out_normal"), sems("out_T"), sems("outT_sbuf"), sems("attn_out")
            f_sh, f_xu, f_xlo, f_c, f_sq, f_xn = (sems("f_" + n) for n in (
                "shifted", "xs_upper", "xs_lower", "centred", "squares", "normal"))
            f_xt, f_xe, f_g, f_ge, f_a, f_u, f_w, f_rb = (sems("f_" + n) for n in (
                "transposed", "xnT_sbuf", "gate", "gelu", "linear", "product", "out", "residual"))
            ch = sems("vector_chain")
            NA, NF = NT * (4 + NRS) + 2 * (NT - 1), 4 + NRS
            NB = PAIRS * (NA + NF)
            block = phase(ctx)

            def bank(s, i, n=1):
                v = PS[:, 4 * s + i:4 * s + i + n, :]
                return v.rearrange("p b n -> p (b n)")

            @block.sync
            def _(sp):
                with sp.Fori(0, DEPTH) as l:
                    sp.wait_ge(free_attn, l + 1)
                    sp.dma_start(WQ[:, :], wqkv[l]).then_inc(w_attn, 16)
                    sp.dma_start(WO[:, :, :], wo[l]).then_inc(w_attn, 16)
                    sp.dma_start(QK[:, :, :], qkscale[l].rearrange("p (a e) -> p a e", a=2)).then_inc(w_attn, 16)
                    sp.wait_ge(free_ffn, l + 1)
                    sp.dma_start(WA[:, :], w1[l]).then_inc(w_ffn, 16)
                    sp.dma_start(WB[:, :, :], w2[l]).then_inc(w_ffn, 16)
                    sp.dma_start(COL[:, :], cols[l]).then_inc(w_ffn, 16)
                    sp.dma_start(B2[:, :], b2[l]).then_inc(w_ffn, 16)
                sp.wait_ge(w_ffn, DEPTH * 64)

            @block.gpsimd
            def _(pool):
                pool.memset(nhalf[:, 0:1], -0.5).then_inc(free_attn, 1)
                pool.memset(nhalf[:, 1:2], -0.5).then_inc(free_ffn, 1)
                for s in range(2):
                    for i in range(PAIRS):
                        pool.memset(ss[s][:, i:i + 1], 0.0).then_inc(s_xl[s], 1)
                    pool.memset(qT[s][:, :, :], 0.0)
                    pool.memset(VT[s][:, :, :], 1.0).then_inc(s_vp[s], 1)
                    for b in range(PAIRS):
                        ins = pool.memset(XM[:, s * PAIRS + b, 0, :], 0.0)
                    ins.then_inc(s_xm[s], 1)
                with pool.Fori(0, DEPTH) as l:
                    pool.wait_ge(w_attn, l * 48 + 48)
                    base = CT[:, C_XP:C_ALL].rearrange("p (k t e) -> p k t e", k=4, t=NT)
                    h2 = DH // 2
                    for a in range(2):
                        wide = lambda z, e: z.unsqueeze(1).to_broadcast([P, NT, e])
                        pool.tensor_tensor(TC[:, :, a, :], base[:, 2 * a], wide(QK[:, a, :], DH), ALU.mult)
                        pool.tensor_tensor(TS[:, :, a, 0:h2], base[:, 2 * a + 1, :, 0:h2], wide(QK[:, a, h2:DH], h2), ALU.mult)
                        ins = pool.tensor_tensor(TS[:, :, a, h2:DH], base[:, 2 * a + 1, :, h2:DH], wide(QK[:, a, 0:h2], h2), ALU.mult)
                    ins.then_inc(s_tab, 1)
                    with pool.Fori(0, PAIRS) as p:
                        m = l * PAIRS + p + 1
                        for s in range(2):
                            pool.wait_ge(s_xl[s], (l + 1) * PAIRS)
                            pool.wait_ge(s_xm[s], m * NT - NT + 1)
                            pool.tensor_copy(xs[s][:, :, 0:D // 2], XL[:, p + s * PAIRS, 1:SLOTS, 0:D // 2]).then_inc(s_xlo[s], 1)
                        for t in range(NT):
                            n = (m - 1) * NT + t + 1
                            for s in range(2):
                                if t == 0 and s == 0:
                                    pool.wait_ge(s_tab, l + 1)
                                v4 = lambda z: z[:, :].rearrange("p (a h e) -> p a h e", a=2, h=H)
                                for a in range(2):
                                    tab = TC[:, t, a, :].unsqueeze(1).to_broadcast([P, H, DH])
                                    if a == 0:
                                        pool.wait_ge(s_qn[s], n)
                                    ins = pool.tensor_tensor(v4(A[s])[:, a], v4(Q[s])[:, a], tab, ALU.mult)
                                ins.then_inc(s_a[s], 1)
                                pool.wait_ge(s_b[s], n)
                                pool.wait_ge(s_a[s], n)
                                pool.tensor_tensor(A[s][:, :], A[s][:, :], R[s][:, :], ALU.add).then_inc(s_rot[s], 1)
                    with pool.Fori(0, PAIRS) as p:
                        m = l * PAIRS + p + 1
                        pool.wait_ge(w_ffn, l * 64 + 64)
                        for s in range(2):
                            pool.wait_ge(s_xm[s], (l + 1) * PAIRS * NT + 1)
                            pool.wait_ge(s_xl[s], m + PAIRS - 1)
                            pool.tensor_copy(xs[s][:, :, 0:D // 2], XM[:, p + s * PAIRS, 1:SLOTS, 0:D // 2]).then_inc(f_xlo[s], 1)
                        for s in range(2):
                            pool.tensor_tensor(R[s][:, T:2 * T].rearrange("p (t d) -> p t d", t=NT), XM[:, p + s * PAIRS, 1:SLOTS, :],
                                               B2[:, :].unsqueeze(1).to_broadcast([P, NT, D]), ALU.add).then_inc(f_rb[s], 1)

            @block.tensor
            def _(pe):
                def shift(s, src, b, done):
                    o = bank(s, 0)[:, 0:NT * D // 2]
                    pe.matmul(o, CT[:, C_SH:C_SH + P], src[:, b, 1:SLOTS, D // 2:D], start=True, stop=False)
                    pe.matmul(o, CT[:, C_ED:C_ED + P], src[:, b, 0:NT, D // 2:D], start=False, stop=True).then_inc(done, 1)

                with pe.Fori(0, DEPTH) as l:
                    with pe.Fori(0, PAIRS) as p:
                        m = l * PAIRS + p + 1
                        for s in range(2):
                            pe.wait_ge(s_xl[s], (l + 1) * PAIRS)
                            pe.wait_ge(s_xm[s], m * NT - NT + 1)
                            shift(s, XL, p + s * PAIRS, s_sh[s])
                        for s in range(2):
                            pe.wait_ge(s_xu[s], m)
                            pe.wait_ge(s_xlo[s], m)
                            for t in range(NT):
                                ins = pe.transpose(bank(s, 1)[:, t * P:t * P + P], xs[s][:, t, :], ident)
                            ins.then_inc(s_xt[s], 1)
                        for t in range(NT):
                            n = (m - 1) * NT + t + 1
                            now = t % 2
                            for s in range(2):
                                if t == 0:
                                    pe.wait_ge(s_xe[s], m)
                                    pe.wait_ge(w_attn, l * 48 + 48)
                                else:
                                    pe.wait_ge(s_xm[s], n)
                                for c in range(4):
                                    ins = pe.matmul(bank(s, c), xsT[s][:, t * P:t * P + P], WQ[:, c * 512:c * 512 + 512], start=True, stop=True)
                                ins.then_inc(s_qk[s], 1)
                            for s in range(2):
                                pe.wait_ge(s_qn[s], n)
                                for c in range(2):
                                    ins = pe.matmul(bank(s, c), xsT[s][:, t * P:t * P + P], WQ[:, (4 + c) * 512:(5 + c) * 512], start=True, stop=True)
                                ins.then_inc(s_v[s], 1)
                            for s in range(2):
                                pe.wait_ge(s_rot[s], n)
                                for i in range(H // 2):
                                    ins = pe.transpose(bank(s, 2, 2)[:, i * P:i * P + P], A[s][:, i * P:i * P + P], ident)
                                ins.then_inc(s_qt[s], 1)
                                pe.wait_ge(s_ve[s], n)
                                for i in range(H // 2):
                                    ins = pe.transpose(bank(s, 0, 2)[:, i * P:i * P + P], A[s][:, INNER + i * P:INNER + i * P + P], ident)
                                ins.then_inc(s_kt[s], 1)
                            for s in range(2):
                                pe.wait_ge(s_qe[s], n)
                                pe.wait_ge(s_ke[s], n)
                                if t:
                                    pe.matmul(bank(s, 2)[0:WIN, :], identb[:, 0:WIN], prevb[:, :].unsqueeze(1).to_broadcast([P, H, WIN]),
                                              start=True, stop=False)
                                    for h in range(H):
                                        ins = pe.matmul(bank(s, 2)[0:WIN, h * WIN:h * WIN + WIN], qT[s][:, h, 0:WIN],
                                                        kT[s][:, 1 - now, h // 2, P - WIN:P], start=False, stop=(h == H - 1))
                                    ins.then_inc(s_sp[s], 1)
                            for s in range(2):
                                if t:
                                    pe.wait_ge(s_spe[s], (m - 1) * (NT - 1) + t)
                                for h in range(H):
                                    if h % 4 == 0:
                                        pe.matmul(bank(s, h // 4), identb[:, :], bandb[:, :].unsqueeze(1).to_broadcast([P, 4, P]), start=True, stop=False)
                                    ins = pe.matmul(bank(s, h // 4)[:, h % 4 * P:h % 4 * P + P], qT[s][:, h, :], kT[s][:, now, h // 2, :],
                                                    start=False, stop=(h % 4 == 3))
                                ins.then_inc(s_so[s], 1)
                            for s in range(2):
                                pe.wait_ge(s_p[s], n)
                                for h in range(H):
                                    ins = pe.transpose(bank(s, 0, 4)[:, h * P:h * P + P], Q[s][:, h * P:h * P + P], ident)
                                ins.then_inc(s_pt[s], 1)
                            for s in range(2):
                                pe.wait_ge(s_pte[s], n)
                                if t:
                                    pe.wait_ge(s_pp[s], (m - 1) * (NT - 1) + t)
                                    pe.wait_ge(s_vp[s], (m - 1) * (NT - 1) + t + 1)
                                for h in range(H):
                                    o = bank(s, h // 4)[:, (h % 4) * (DH + 1):(h % 4 + 2) * (DH + 1)]
                                    ins = pe.matmul(o, R[s][:, h * P:h * P + P], VT[s][:, h:h + 2, :].rearrange("p h e -> p (h e)"),
                                                    start=True, stop=True)
                                    if t:
                                        ins = pe.matmul(o[0:WIN, 0:DH + 1], PTp[s][:, h, :], VP[s][:, h, :], start=False, stop=True, skip_group_check=True)
                                ins.then_inc(s_o[s], 1)
                            for s in range(2):
                                pe.wait_ge(s_yn[s], n)
                                for i in range(INNER // P):
                                    ins = pe.transpose(bank(s, 0, 2)[:, i * P:i * P + P], Y[s][:, i * P:i * P + P], ident)
                                ins.then_inc(s_yt[s], 1)
                            for s in range(2):
                                pe.wait_ge(s_ye[s], n)
                                for i in range(INNER // P):
                                    ins = pe.matmul(bank(s, 2)[:, 0:D], YT[s][:, i, :], WO[:, i, :], start=(i == 0), stop=(i == INNER // P - 1))
                                ins.then_inc(s_w[s], 1)
                    with pe.Fori(0, PAIRS) as p:
                        m = l * PAIRS + p + 1
                        for s in range(2):
                            pe.wait_ge(s_xm[s], m * NT + 1)
                            pe.wait_ge(s_xl[s], m + PAIRS - 1)
                            shift(s, XM, p + s * PAIRS, f_sh[s])
                        for s in range(2):
                            pe.wait_ge(f_xn[s], m)
                            for t in range(NT):
                                ins = pe.transpose(bank(s, 1)[:, t * P:t * P + P], xs[s][:, t, :], ident)
                            ins.then_inc(f_xt[s], 1)
                        for part, done, after in ((1, f_g, f_xe), (0, f_a, f_ge)):
                            for s in range(2):
                                if part and s == 0:
                                    pe.wait_ge(w_ffn, l * 64 + 64)
                                pe.wait_ge(after[s], m)
                                for c in range(DCH):
                                    k = P if c < DCH - 1 else DLAST
                                    at = part * DI + c * P
                                    ins = pe.matmul(bank(s, 1 + c)[0:k], WA[:, at:at + k], xsT[s][:, :], start=True, stop=True)
                                ins.then_inc(done[s], 1)
                        for s in range(2):
                            pe.wait_ge(f_u[s], m)
                            for t in range(NT):
                                for c in range(DCH):
                                    k = P if c < DCH - 1 else DLAST
                                    ins = pe.matmul(bank(s, 0)[:, t * P:t * P + P], A[s][0:k, c * T + t * P:c * T + t * P + P], WB[0:k, c, :],
                                                    start=(c == 0), stop=(c == DCH - 1))
                            ins.then_inc(f_w[s], 1)

            @block.scalar
            def _(act):
                with act.Fori(0, DEPTH) as l:
                    with act.Fori(0, PAIRS) as p:
                        m = l * PAIRS + p + 1
                        for s in range(2):
                            act.wait_ge(s_sh[s], m)
                            act.activation(xs[s][:, :, D // 2:D], bank(s, 0)[:, 0:NT * D // 2].rearrange("p (t d) -> p t d", t=NT), ACT.Copy).then_inc(s_xu[s], 1)
                        for s in range(2):
                            act.wait_ge(s_xt[s], m)
                            act.activation(xsT[s][:, :], bank(s, 1), ACT.Copy).then_inc(s_xe[s], 1)
                        for t in range(NT):
                            n = (m - 1) * NT + t + 1
                            now = t % 2
                            for s in range(2):
                                act.wait_ge(s_qk[s], n)
                                act.activation(R[s][:, :], bank(s, 0, 4), ACT.Square).then_inc(s_sq[s], 1)
                            for s in range(2):
                                act.wait_ge(s_v[s], n)
                                act.activation(VT[s][:, 0:H, 0:DH], bank(s, 0, 2).rearrange("p (h e) -> p h e", h=H), ACT.Copy).then_inc(s_ve[s], 1)
                            for s in range(2):
                                act.wait_ge(s_qt[s], n)
                                for a in range(2):
                                    ins = act.activation(qT[s][a * DH:a * DH + DH, a:H:2, :],
                                                         bank(s, 2, 2)[a * DH:a * DH + DH].rearrange("p (h n) -> p h n", n=P), ACT.Copy)
                                ins.then_inc(s_qe[s], 1)
                                act.wait_ge(s_kt[s], n)
                                act.activation(kT[s][:, now, :, :].rearrange("p h n -> p (h n)"), bank(s, 0, 2), ACT.Copy).then_inc(s_ke[s], 1)
                            for s in range(2):
                                act.wait_ge(s_sub[s], n)
                                if t:
                                    act.activation(Pp[s][:, :, :], Pp[s][:, :, :], ACT.Exp).then_inc(s_pe[s], 1)
                                act.activation(Q[s][:, :], Q[s][:, :], ACT.Exp).then_inc(s_p[s], 1)
                            for s in range(2):
                                act.wait_ge(s_pt[s], n)
                                act.activation(R[s][:, :], bank(s, 0, 4), ACT.Copy).then_inc(s_pte[s], 1)
                            for s in range(2):
                                act.wait_ge(s_o[s], n)
                                if t < NT - 1:
                                    act.activation(VP[s][:, :, :], VT[s][P - WIN:P, 0:H, :], ACT.Copy).then_inc(s_vp[s], 1)
                            for s in range(2):
                                act.wait_ge(s_yt[s], n)
                                act.activation(YT[s][:, :, :].rearrange("p i n -> p (i n)"), bank(s, 0, 2), ACT.Copy).then_inc(s_ye[s], 1)
                    with act.Fori(0, PAIRS) as p:
                        m = l * PAIRS + p + 1
                        for s in range(2):
                            act.wait_ge(f_sh[s], m)
                            act.activation(xs[s][:, :, D // 2:D], bank(s, 0)[:, 0:NT * D // 2].rearrange("p (t d) -> p t d", t=NT), ACT.Copy).then_inc(f_xu[s], 1)
                        for s in range(2):
                            act.wait_ge(f_c[s], m)
                            act.activation(R[s][:, 0:T].rearrange("p (t d) -> p t d", t=NT), xs[s][:, :, :], ACT.Square).then_inc(f_sq[s], 1)
                        for s in range(2):
                            if s == 0:
                                act.wait_ge(w_ffn, l * 64 + 64)
                            act.wait_ge(f_xt[s], m)
                            act.activation(xsT[s][:, :], bank(s, 1), ACT.Identity, scale=COL[:, 0:1], bias=COL[:, 1:2]).then_inc(f_xe[s], 1)
                        for s in range(2):
                            act.wait_ge(f_g[s], m)
                            for c in range(DCH):
                                k = P if c < DCH - 1 else DLAST
                                at = 2 + DCH + c
                                ins = act.activation(Q[s][0:k, c * T:c * T + T], bank(s, 1 + c)[0:k], ACT.Gelu, bias=COL[0:k, at:at + 1])
                            ins.then_inc(f_ge[s], 1)

            @block.vector
            def _(dve):
                with dve.Fori(0, DEPTH) as l:
                    with dve.Fori(0, PAIRS) as p:
                        m = l * PAIRS + p + 1
                        k = [0, 0]

                        def link(s, ins):
                            k[s] += 1
                            ins.then_inc(ch[s], 1)
                            dve.wait_ge(ch[s], l * NB + p * NA + k[s])

                        for t in range(NT):
                            n = (m - 1) * NT + t + 1
                            for s in range(2):
                                dve.wait_ge(s_sq[s], n)
                                link(s, nc.vector.tensor_reduce(ss[s][:, :], R[s][:, :].rearrange("p (h e) -> p h e", e=DH), AX.X, ALU.add))
                                link(s, nc.vector.tensor_scalar(ss[s][:, :], ss[s][:, :], 1e-24, None, ALU.max))
                                rsqrt(lambda ins: link(s, ins), rn[s][:, 0, :], ss[s][:, :], rn[s][:, 1, :])
                                v3 = lambda z: z.rearrange("p (h e) -> p h e", e=DH)
                                nc.vector.tensor_tensor(v3(Q[s][:, :]), v3(bank(s, 0, 4)), rn[s][:, 0, :].unsqueeze(2).to_broadcast([P, 2 * H, DH]),
                                                        ALU.mult).then_inc(s_qn[s], 1)
                            for s in range(2):
                                dve.wait_ge(s_qn[s], n)
                                if t == 0 and s == 0:
                                    dve.wait_ge(s_tab, l + 1)
                                v4 = lambda z: z[:, :].rearrange("p (a h e) -> p a h e", a=2, h=H)
                                h2 = DH // 2
                                for a in range(2):
                                    for lo, hi in ((0, h2), (h2, 0)):
                                        ins = nc.vector.tensor_tensor(v4(R[s])[:, a, :, lo:lo + h2], v4(Q[s])[:, a, :, hi:hi + h2],
                                                                      TS[:, t, a, lo:lo + h2].unsqueeze(1).to_broadcast([P, H, h2]), ALU.mult)
                                ins.then_inc(s_b[s], 1)
                            if t:
                                for s in range(2):
                                    dve.wait_ge(s_sp[s], (m - 1) * (NT - 1) + t)
                                    nc.vector.tensor_copy(Pp[s][:, :, :].rearrange("p h n -> p (h n)"), bank(s, 2)[0:WIN, :]).then_inc(s_spe[s], 1)
                            for s in range(2):
                                so = bank(s, 0, 4).rearrange("p (h n) -> p h n", h=H)
                                dve.wait_ge(s_so[s], n)
                                link(s, nc.vector.tensor_reduce(mx[s][:, 0, :], so, AX.X, ALU.max))
                                if t:
                                    link(s, nc.vector.tensor_reduce(mx[s][0:WIN, 1, :], Pp[s][:, :, :], AX.X, ALU.max))
                                    link(s, nc.vector.tensor_tensor(mx[s][0:WIN, 0, :], mx[s][0:WIN, 0, :], mx[s][0:WIN, 1, :], ALU.max))
                                    nc.vector.tensor_tensor(Pp[s][:, :, :], Pp[s][:, :, :], mx[s][0:WIN, 0, :].unsqueeze(2).to_broadcast([WIN, H, WIN]),
                                                            ALU.subtract)
                                nc.vector.tensor_tensor(Q[s][:, :].rearrange("p (h n) -> p h n", h=H), so,
                                                        mx[s][:, 0, :].unsqueeze(2).to_broadcast([P, H, P]), ALU.subtract).then_inc(s_sub[s], 1)
                            if t:
                                for s in range(2):
                                    dve.wait_ge(s_pe[s], (m - 1) * (NT - 1) + t)
                                    nc.vector.transpose(PTp[s][:, :, :].rearrange("p h n -> p (h n)"), Pp[s][:, :, :].rearrange("p h n -> p (h n)")).then_inc(s_pp[s], 1)
                            for s in range(2):
                                dve.wait_ge(s_o[s], n)
                                o = PS[:, 4 * s:4 * s + 4, 0:4 * (DH + 1)].rearrange("p b (h e) -> p b h e", h=4)
                                r4 = rc[s][:, :].rearrange("p (b h) -> p b h", b=4)
                                link(s, nc.vector.reciprocal(r4, o[:, :, :, DH]))
                                y4 = Y[s][:, :].rearrange("p (b h e) -> p b h e", b=4, h=4)
                                for c in range(4):
                                    ins = nc.vector.tensor_tensor(y4[:, c], o[:, c, :, 0:DH], r4[:, c].unsqueeze(2).to_broadcast([P, 4, DH]), ALU.mult)
                                ins.then_inc(s_yn[s], 1)
                            for s in range(2):
                                dve.wait_ge(s_w[s], n)
                                ins = nc.vector.tensor_tensor(XM[:, p + s * PAIRS, t + 1, :], bank(s, 2)[:, 0:D], XL[:, p + s * PAIRS, t + 1, :], ALU.add)
                                ins.then_inc(s_xm[s], 1)
                        assert k == [NA, NA], k
                    nc.vector.memset(mx[0][:, 0, 0:1], 0.0).then_inc(free_attn, 1)
                    with dve.Fori(0, PAIRS) as p:
                        m = l * PAIRS + p + 1
                        k = [0, 0]

                        def link(s, ins):
                            k[s] += 1
                            ins.then_inc(ch[s], 1)
                            dve.wait_ge(ch[s], l * NB + p * NF + PAIRS * NA + k[s])

                        wide = lambda z: z[:, :].unsqueeze(2).to_broadcast([P, NT, D])
                        for s in range(2):
                            dve.wait_ge(f_xu[s], m)
                            dve.wait_ge(f_xlo[s], m)
                            link(s, nc.vector.tensor_reduce(st[s][:, :], xs[s][:, :, :], AX.X, ALU.add))
                            link(s, nc.vector.tensor_scalar(st[s][:, :], st[s][:, :], -1.0 / D, None, ALU.mult))
                            nc.vector.tensor_tensor(xs[s][:, :, :], xs[s][:, :, :], wide(st[s]), ALU.add).then_inc(f_c[s], 1)
                        for s in range(2):
                            dve.wait_ge(f_sq[s], m)
                            link(s, nc.vector.tensor_reduce(st[s][:, :], R[s][:, 0:T].rearrange("p (t d) -> p t d", t=NT), AX.X, ALU.add))
                            link(s, nc.vector.tensor_scalar(st[s][:, :], st[s][:, :], 1.0 / D, 1e-5, ALU.mult, ALU.add))
                            rsqrt(lambda ins: link(s, ins), rn[s][:, 0, 0:NT], st[s][:, :], rn[s][:, 1, 0:NT])
                            nc.vector.tensor_tensor(xs[s][:, :, :], xs[s][:, :, :], rn[s][:, 0, 0:NT].unsqueeze(2).to_broadcast([P, NT, D]), ALU.mult).then_inc(f_xn[s], 1)
                        for s in range(2):
                            dve.wait_ge(f_a[s], m)
                            for c in range(DCH):
                                kk = P if c < DCH - 1 else DLAST
                                ins = nc.vector.scalar_tensor_tensor(out=A[s][0:kk, c * T:c * T + T], in0=bank(s, 1 + c)[0:kk], scalar=COL[0:kk, 2 + c:3 + c],
                                                                     in1=Q[s][0:kk, c * T:c * T + T], op0=ALU.add, op1=ALU.mult)
                            ins.then_inc(f_u[s], 1)
                        for s in range(2):
                            dve.wait_ge(f_rb[s], m)
                            dve.wait_ge(f_w[s], m)
                            nc.vector.tensor_tensor(XL[:, p + s * PAIRS, 1:SLOTS, :], bank(s, 0).rearrange("p (t d) -> p t d", t=NT),
                                                    R[s][:, T:2 * T].rearrange("p (t d) -> p t d", t=NT), ALU.add).then_inc(s_xl[s], 1)
                        assert k == [NF, NF], k
                    nc.vector.memset(mx[0][:, 0, 0:1], 0.0).then_inc(free_ffn, 1)

        with ExitStack() as c2:
            s_o = scoped(c2, "stored")
            s_f = scoped(c2, "summed")
            block = phase(c2)

            @block.vector
            def _(dve):
                for b in range(B):
                    o = X1[:, b * NT:b * NT + NT, :]
                    dve.tensor_tensor(o, o, XL[:, b, 1:SLOTS, :], ALU.add).then_inc(s_f, 1)

            @block.sync
            def _(sp):
                ov = out.rearrange("b (t p) d -> p b t d", p=P)
                for b in range(B):
                    sp.wait_ge(s_f, b + 1)
                    sp.dma_start(ov[:, b], X1[:, b * NT:b * NT + NT, :]).then_inc(s_o, 16)
                sp.wait_ge(s_o, 16 * B)


def kernel(**inputs):
    import concourse.bacc as _bacc
    from concourse.bass_utils import run_bass_kernel_spmd as _run

    a = {k: np.asarray(v) for k, v in inputs.items()}
    rep = lambda v, n=P: np.ascontiguousarray(np.broadcast_to(v, (n,) + v.shape))
    l0, l1, lf = "L0_attn_", "L1_attn_", "L1_ffn_"
    rows0 = np.concatenate([a["L0_ffn_bias"], a[l1 + "bo"], a[l0 + "lambda_q1"], a[l0 + "lambda_q2"],
                            a[l0 + "lambda_k1"], a[l0 + "lambda_k2"]])
    qk = np.concatenate([a[lf + "q_scale"], a[lf + "k_scale"]], 1)
    pad = lambda w, n: np.concatenate([w, np.zeros((DEPTH, n) + w.shape[2:], w.dtype)], 1)
    fill = DCH * P - DI
    b1 = a[lf + "b1"]
    b1c = [pad(b1[:, i * DI:(i + 1) * DI], fill).reshape(DEPTH, DCH, P).transpose(0, 2, 1) for i in range(2)]
    cols = np.concatenate([a[lf + "ln_g"][:, :, None], a[lf + "ln_b"][:, :, None]] + b1c, 2)
    arrays = {
        "x": a[l0 + "x"], "consts": constants(),
        "wqkv0": np.concatenate([a[l0 + n].T for n in ("Wq", "Wk", "Wv")], 1), "wproj0": a[l0 + "Wproj"].T,
        "wff0": a["L0_ffn_weight"], "rows0": rep(rows0),
        "wqkv1": np.concatenate([a[l1 + n].T for n in ("Wq", "Wk", "Wv")], 1), "wo1": a[l1 + "Wo"].T,
        "wqkv": a[lf + "Wqkv"], "wo": a[lf + "Wo"].reshape(DEPTH, INNER // P, P, D).transpose(0, 2, 1, 3),
        "qkscale": rep(qk).transpose(1, 0, 2), "w1": a[lf + "W1"],
        "w2": pad(a[lf + "W2"], fill).reshape(DEPTH, DCH, P, D).transpose(0, 2, 1, 3),
        "cols": cols, "b2": rep(a[lf + "b2"]).transpose(1, 0, 2),
    }
    arrays = {k: np.ascontiguousarray(v) for k, v in arrays.items()}
    nc = _bacc.Bacc("TRN2", target_bir_lowering=False, num_devices=1)
    args = [nc.dram_tensor(k, v.shape, mybir.dt.from_np(v.dtype), kind="ExternalInput").ap() for k, v in arrays.items()]
    out = nc.dram_tensor("out", (B, T, D), F32, kind="ExternalOutput").ap()
    program(nc, *args, out)
    r = _run(nc, [arrays], core_ids=[0])
    return r.results[0]["out"]
```

```python
from contextlib import ExitStack

import numpy as np

import concourse.bass as bass
from concourse import mybir

F32 = mybir.dt.float32
BF16 = mybir.dt.bfloat16
ALU = mybir.AluOpType
ACT = mybir.ActivationFunctionType
AX = mybir.AxisListType

P = 128
D = 128
B = 8
T = 512
NT = T // P
SLOTS = NT + 1
NEG = -1e30
H = 16
HD = D // H
HV0 = 2 * HD
NV0 = H // 2
PAD = 32
GH = P // PAD
NG = H // GH
PTN = 2 * GH
KS = 9 * HD
MROW = 96
DEPTH = 6
DH = 64
INNER = H * DH
WIN = 32
NW = P // WIN
DI = int(D * 4 * 2 / 3)
DCH = 3
DLAST = DI - 2 * P
LAMBDA_INIT = 0.8 - 0.6 * float(np.exp(-0.3 * 1))
MAGIC = 1.5 * 2.0 ** 23
PAIRS = B // 2

C_ID, C_SH, C_ED, C_TRI, C_WIN, C_WIN0 = 0, 128, 256, 384, 512, 576
C_ROT = C_WIN0 + 2 * WIN
C_XP = C_ROT + 2 * NT * HD
C_ALL = C_XP + 4 * NT * DH


def constants():
    c = np.zeros((P, C_ALL), np.float32)
    i = np.arange(P)
    c[:, C_ID:C_ID + P] = np.eye(P)
    c[i[:-1], C_SH + i[1:]] = 1.0
    c[P - 1, C_ED] = 1.0
    q, k = i[:, None], i[None, :]
    w, r = np.arange(P)[:, None] % WIN, np.arange(2 * WIN)[None, :] - WIN
    c[:, C_WIN:C_WIN + 2 * WIN] = np.where((r <= w) & (w - r <= WIN), 0.0, NEG)
    c[:, C_WIN0:C_WIN0 + 2 * WIN] = c[:, C_WIN:C_WIN + 2 * WIN]
    c[:WIN, C_WIN0:C_WIN0 + WIN] = NEG
    c[:, C_TRI:C_TRI + P] = np.where(q <= k, 0.0, NEG)
    pos = np.arange(T, dtype=np.float64).reshape(NT, P).T
    f = 1.0 / 10000.0 ** (np.arange(0, HD, 2) / HD)
    a = pos[:, :, None] * f
    rot = np.stack([np.concatenate([np.cos(a), np.cos(a)], -1),
                    np.concatenate([np.sin(a), -np.sin(a)], -1)], 1)
    c[:, C_ROT:C_XP] = rot.reshape(P, -1)
    half = np.arange(0, DH, 2)
    a = pos[:, :, None] * (1.0 / 10000.0 ** (half / DH))
    s = ((half + 0.4 * DH) / (1.4 * DH)) ** ((pos[:, :, None] - T // 2) / (WIN // 2))
    cos, sin = np.cos(a), np.sin(a)
    xp = [np.concatenate([cos * s, cos * s], -1), np.concatenate([-sin * s, sin * s], -1),
          np.concatenate([cos / s, cos / s], -1) * 8.0, np.concatenate([-sin / s, sin / s], -1) * 8.0]
    c[:, C_XP:] = np.stack(xp, 1).reshape(P, -1)
    return c


def program(nc, x, consts, wqkv0, wproj0, wff0, rows0, wqkv1, wo1, wqkv, wo, qkscale, w1, w2, cols, b2, out):
    with ExitStack() as outer:
        def sb(name, shape, dt=F32, ctx=outer):
            return ctx.enter_context(nc.sbuf_tensor(name, shape, dt))

        PS = outer.enter_context(nc.psum_tensor("PS", [P, 8, 512], F32))
        CT = sb("CT", [P, C_ALL])
        ident = CT[:, C_ID:C_ID + P]
        identb = sb("identb", [P, P], BF16)
        winb = sb("winb", [P, 2, 2 * WIN], BF16)
        trib = sb("trib", [P, P], BF16)
        nhalf = sb("nhalf", [P, 128])
        X1 = sb("X1", [P, B * NT, D])
        XL = sb("XL", [P, B, SLOTS, D])

        I32 = mybir.dt.int32

        def rsqrt(link, y, v, t):
            link(nc.vector.tensor_scalar(y.bitcast(I32), v.bitcast(I32), -0.5, float(0x5F3759DF), ALU.mult, ALU.add))
            for _ in range(3):
                link(nc.vector.tensor_tensor(t, y, y, ALU.mult))
                link(nc.vector.scalar_tensor_tensor(out=t, in0=t, scalar=-0.5, in1=v, op0=ALU.mult, op1=ALU.mult))
                link(nc.vector.scalar_tensor_tensor(out=y, in0=t, scalar=1.5, in1=y, op0=ALU.add, op1=ALU.mult))

        NRS = 10

        used = []

        def scoped(ctx, name):
            used.append(ctx.enter_context(nc.semaphore(name)))
            return used[-1]

        def phase(ctx):
            mine = used[:]
            used.clear()

            def clear():
                with nc.Block() as block:
                    @block.gpsimd
                    def _(pool):
                        for s in mine:
                            pool.sem_clear(s)

            ctx.callback(clear)
            return ctx.enter_context(nc.Block())

        def normalise_rows(block, src, sem, sums, sqs, loaded=None):
            s_sum, s_cen, s_sq, s_ch = sem
            mean, var, inv, tmp = (sums[:, i] for i in range(4))

            @block.vector
            def _(dve):
                n = [0]

                def link(ins):
                    n[0] += 1
                    ins.then_inc(s_ch, 1)
                    dve.wait_ge(s_ch, n[0])

                wide = lambda z: z.unsqueeze(2).to_broadcast([P, NT, D])
                for b in range(B):
                    s = src[:, b * NT:b * NT + NT, :]
                    if loaded is not None:
                        dve.wait_ge(loaded[b], 16)
                    link(dve.tensor_reduce(mean[:, b, :], s, AX.X, ALU.add))
                    link(dve.tensor_scalar(mean[:, b, :], mean[:, b, :], -1.0 / D, None, ALU.mult))
                    dve.tensor_tensor(XL[:, b, 1:SLOTS, :], s, wide(mean[:, b, :]), ALU.add).then_inc(s_cen, 1)
                    if b:
                        dve.wait_ge(s_sq, b)
                        dve.tensor_reduce(var[:, b - 1, :], sqs[:, (b - 1) % 2, :, :], AX.X, ALU.add).then_inc(s_sum, 1)
                dve.wait_ge(s_sq, B)
                link(dve.tensor_reduce(var[:, B - 1, :], sqs[:, (B - 1) % 2, :, :], AX.X, ALU.add))
                dve.wait_ge(s_sum, B - 1)
                flat = lambda z: z.rearrange("p b t -> p (b t)")
                link(dve.tensor_scalar(flat(var), flat(var), 1.0 / D, 1e-5, ALU.mult, ALU.add))
                rsqrt(link, flat(inv), flat(var), flat(tmp))
                dve.wait_ge(s_cen, B)
                for b in range(B):
                    o = XL[:, b, 1:SLOTS, :]
                    dve.tensor_tensor(o, o, wide(inv[:, b, :]), ALU.mult)

            @block.scalar
            def _(act):
                for b in range(B):
                    act.wait_ge(s_cen, b + 1)
                    if b >= 2:
                        act.wait_ge(s_sum, b - 1)
                    act.activation(sqs[:, b % 2, :, :], XL[:, b, 1:SLOTS, :], ACT.Square).then_inc(s_sq, 1)

        with ExitStack() as ctx:
            X0 = sb("X0", [P, B * NT, D], F32, ctx)
            W0 = sb("W0", [P, 3 * D], F32, ctx)
            WP0 = sb("WP0", [P, D], F32, ctx)
            WF0 = sb("WF0", [P, D], F32, ctx)
            WFT = sb("WFT", [P, D], F32, ctx)
            W1q = sb("W1q", [P, 3 * D], F32, ctx)
            WO1 = sb("WO1", [P, D], F32, ctx)
            ROWS = sb("ROWS", [P, 2 * D + 16], F32, ctx)
            bias0, bias1, lamv = ROWS[:, 0:D], ROWS[:, D:2 * D], ROWS[:, 2 * D:]
            lam = sb("lam", [P, 8], F32, ctx)
            sums = sb("sums", [P, 4, B, NT], F32, ctx)
            xs = sb("xs", [P, NT, D], F32, ctx)
            xT = sb("xT", [P, T], F32, ctx)
            rms = sb("rms", [P, 3, NT, 2 * H], F32, ctx)
            SP = sb("SP", [P, 2, NT, H, 3, HD], BF16, ctx)
            QT = sb("QT", [P, H, T], BF16, ctx)
            KT = sb("KT", [P, H, T], BF16, ctx)
            mxs = sb("mxs", [P, NT, GH], F32, ctx)
            MXS = sb("MXS", [P, NT, GH, PAD], BF16, ctx)
            MXT = sb("MXT", [P, T], BF16, ctx)
            ONE = sb("ONE", [P, T], BF16, ctx)
            V1 = sb("V1", [P, NT, NV0, PAD], F32, ctx)
            V2 = sb("V2", [P, NT, H, PAD], F32, ctx)
            PT = sb("PT", [P, PTN, NT * T], F32, ctx)
            half = NT * T // 2
            sq, ra = (PT[:, 0, i * half:(i + 1) * half].rearrange("p (t c) -> p t c", t=NT) for i in range(2))
            qn = PT[:, 1, 0:half].rearrange("p (t c) -> p t c", t=NT)
            PK = PT[:, 2:5, :].rearrange("p a n -> p (a n)")[:, 0:NT * H * KS].bitcast(BF16)
            PK = PK.rearrange("p (a n k) -> p a n k", a=2, k=KS)
            sqs = PT[:, 1, half:].rearrange("p (a t d) -> p a t d", a=2, t=NT)
            OT = sb("OT", [P, T], F32, ctx)
            Y = sb("Y", [P, NT, D], F32, ctx)
            yt = sb("yt", [P, NT, GH, HV0], F32, ctx)
            rec = sb("rec", [P, 2, NT, GH], F32, ctx)
            YT = sb("YT", [P, T], F32, ctx)
            xd = sb("xd", [P, NT, D], F32, ctx)
            xdT = sb("xdT", [P, T], F32, ctx)
            qa = sb("qa", [P, NT * D], F32, ctx)
            qb = sb("qb", [P, NT * D], F32, ctx)
            qc = sb("qc", [P, NT * D], F32, ctx)
            qs = sb("qs", [P, 2, 16], F32, ctx)

            with ExitStack() as c2:
                def sem(name):
                    return scoped(c2, name)

                s_ld = [sem(f"x_loaded{b}") for b in range(B)]
                s_cst = sem("constants_loaded")
                s_mem = sem("memsets_done")
                names = [sem(n) for n in ("ln0_sum", "ln0_centred", "ln0_sq", "ln0_chain")]
                block = phase(c2)

                @block.sync
                def _(sp):
                    xv = x.rearrange("b (t p) d -> p b t d", p=P)
                    for b in range(B):
                        sp.dma_start(X0[:, b * NT:b * NT + NT, :], xv[:, b]).then_inc(s_ld[b], 16)
                    for dst, src in ((CT, consts), (W0, wqkv0), (WP0, wproj0), (WF0, wff0), (ROWS, rows0), (W1q, wqkv1), (WO1, wo1)):
                        sp.dma_start(dst[:, :], src).then_inc(s_cst, 16)
                    sp.wait_ge(s_cst, 7 * 16)

                @block.gpsimd
                def _(pool):
                    pool.memset(nhalf[:, :], -0.5).then_inc(s_mem, 1)
                    pool.memset(QT[:, :, :], 0.0).then_inc(s_mem, 1)
                    pool.memset(KT[:, :, :], 0.0).then_inc(s_mem, 1)
                    pool.memset(MXS[:, :, :, :], 0.0).then_inc(s_mem, 1)
                    pool.memset(ONE[:, :], 1.0).then_inc(s_mem, 1)
                    pool.memset(V1[:, :, :, :], 0.0).then_inc(s_mem, 1)
                    pool.memset(V2[:, :, :, :], 0.0).then_inc(s_mem, 1)
                    for b in range(B):
                        pool.memset(XL[:, b, 0, :], 0.0).then_inc(s_mem, 1)
                    pool.wait_ge(s_mem, 7 + B)
                    pool.memset(KT[MROW:MROW + 3, :, :], 1.0).then_inc(s_mem, 1)
                    pool.wait_ge(s_mem, 8 + B)
                    pool.memset(V1[:, :, :, HV0:HV0 + 1], 1.0)
                    pool.memset(V2[:, :, :, HD:HD + 1], 1.0)

                normalise_rows(block, X0, names, sums, sqs, s_ld)

            with ExitStack() as c2:
                def sem(name):
                    return scoped(c2, name)

                s_lam = sem("lambda_chain")
                s_exp = sem("lambda_exp")
                block = phase(c2)

                @block.vector
                def _(dve):
                    dve.tensor_copy(identb[:, :], ident)
                    dve.tensor_copy(winb[:, :, :].rearrange("p a r -> p (a r)"), CT[:, C_WIN:C_ROT])
                    dve.tensor_copy(trib[:, :], CT[:, C_TRI:C_TRI + P])
                    dve.tensor_tensor(qa[:, 0:8], lamv[:, 0:8], lamv[:, 8:16], ALU.mult).then_inc(s_lam, 1)
                    dve.wait_ge(s_lam, 1)
                    dve.tensor_reduce(lam[:, 0:2], qa[:, 0:8].rearrange("p (a c) -> p a c", a=2), AX.X, ALU.add).then_inc(s_lam, 1)
                    dve.wait_ge(s_exp, 1)
                    dve.tensor_tensor(lam[:, 4:5], lam[:, 3:4], lam[:, 2:3], ALU.subtract).then_inc(s_lam, 1)
                    dve.wait_ge(s_lam, 3)
                    dve.tensor_scalar(lam[:, 5:6], lam[:, 4:5], -LAMBDA_INIT, None, ALU.add).then_inc(s_lam, 1)

                @block.scalar
                def _(act):
                    act.wait_ge(s_lam, 2)
                    act.activation(lam[:, 2:4], lam[:, 0:2], ACT.Exp).then_inc(s_exp, 1)

            nlam = lam[:, 5:6]

            def fake_quant(link, src, dst, nblk):
                n = nblk * 32
                v, a, bb = qa[:, 0:n], qb[:, 0:n], qc[:, 0:n]
                blk = lambda t: t.rearrange("p (n k) -> p n k", k=32)
                sc, rs = qs[:, 0, 0:nblk], qs[:, 1, 0:nblk]
                wide = lambda t: t.unsqueeze(2).to_broadcast([P, nblk, 32])
                e = nc.vector
                link(e.tensor_reduce(sc, blk(src), AX.X, ALU.max, apply_absolute_value=True))
                link(e.tensor_scalar(sc, sc, 1.0 / 7.5, 1e-30, ALU.mult, ALU.max))
                link(e.reciprocal(rs, sc))
                link(e.tensor_tensor(blk(v), blk(src), wide(rs), ALU.mult))
                link(e.tensor_tensor(a, v, v, ALU.mult))
                link(e.tensor_scalar(bb, a, 16.0, 0.25, ALU.is_ge, ALU.mult))
                link(e.tensor_scalar(a, a, 4.0, 0.125, ALU.is_ge, ALU.mult))
                link(e.scalar_tensor_tensor(out=a, in0=a, scalar=0.125, in1=bb, op0=ALU.add, op1=ALU.add))
                link(e.reciprocal(bb, a))
                link(e.tensor_tensor(v, v, bb, ALU.mult))
                link(e.tensor_scalar(v, v, -0.5, None, ALU.add))
                link(e.tensor_scalar(bb, v, MAGIC, None, ALU.add))
                link(e.tensor_scalar(bb, bb, -MAGIC, None, ALU.add))
                link(e.tensor_tensor(v, bb, v, ALU.is_lt))
                link(e.tensor_tensor(v, v, bb, ALU.add))
                link(e.tensor_tensor(v, v, a, ALU.mult))
                return e.tensor_tensor(blk(dst), blk(v), wide(sc), ALU.mult)
            NQ = 17

            with ExitStack() as c2:
                def sem(name):
                    return scoped(c2, name)

                s_ch, s_wt = sem("wquant_chain"), sem("wquant_transposed")
                block = phase(c2)

                @block.vector
                def _(dve):
                    n = [0]

                    def link(ins):
                        n[0] += 1
                        ins.then_inc(s_ch, 1)
                        dve.wait_ge(s_ch, n[0])

                    link(fake_quant(link, WF0[:, :], WF0[:, :], 4))
                    dve.wait_ge(s_wt, 1)
                    dve.tensor_copy(WFT[:, :], PS[:, 0, 0:P])

                @block.tensor
                def _(pe):
                    pe.wait_ge(s_ch, NQ)
                    pe.transpose(PS[:, 0, 0:P], WF0[:, :], ident).then_inc(s_wt, 1)

            def attention(first):
                with ExitStack() as c2:
                    def sem(name):
                        return scoped(c2, f"a{0 if first else 1}_{name}")

                    s_xs, s_xT, s_xTr, s_qkv = sem("xs"), sem("xT"), sem("xT_sbuf"), sem("qkv")
                    s_sq, s_spl, s_ch = sem("squares"), sem("parts"), sem("dve_chain")
                    s_qp, s_kp = sem("q_repeated"), sem("k_repeated")
                    s_qt, s_qe, s_ke = sem("qk_transposed"), sem("qT_sbuf"), sem("kT_sbuf")
                    s_mp, s_mx, s_ms = sem("max_scores"), sem("max_taken"), sem("max_parts")
                    s_mt, s_me, s_mc = sem("max_transposed"), sem("max_sbuf"), sem("max_rows")
                    s_sc, s_ex, s_pv, s_pve = sem("scores"), sem("exps"), sem("values_summed"), sem("sums_sbuf")
                    s_yg, s_yn = sem("group_transposed"), sem("group_normal")
                    s_yt, s_ye, s_xd, s_xt, s_xe = sem("y_transposed"), sem("yT_sbuf"), sem("xd"), sem("xd_transposed"), sem("xdT_sbuf")
                    s_pr, s_bt = sem("projected"), sem("batch_done")
                    block = phase(c2)
                    wqkv_, wo_, bias_ = (W0, WP0, bias0) if first else (W1q, WO1, bias1)
                    hv = HV0 if first else HD
                    V = V1 if first else V2
                    scale = float(HD) ** -0.5
                    LAG = 0 if first else 1
                    STEPS = NG + LAG + 2
                    NC = 43 if first else 29

                    def keys(jt):
                        if not first:
                            return jt * T, 0
                        return (0, T, 2 * T, T + 3 * P)[jt], jt * P

                    @block.gpsimd
                    def _(pool):
                        pool.memset(nhalf[:, 127:128], -0.5).then_inc(s_bt, 1)
                        with pool.Fori(0, B) as b:
                            pool.wait_ge(s_bt, b + 1)
                            pool.tensor_copy(xs[:, :, :], XL[:, b, 1:SLOTS, :]).then_inc(s_xs, 1)
                            if not first:
                                for g in range(NG):
                                    pool.wait_ge(s_me, b * NG + g + 1)
                                    for i in range(GH):
                                        pool.tensor_tensor(QT[MROW:MROW + 3, GH * g + i, :], MXT[PAD * i:PAD * i + 3, :],
                                                           ONE[PAD * i:PAD * i + 3, :], ALU.mult).then_inc(s_mc, 1)

                    @block.tensor
                    def _(pe):
                        with pe.Fori(0, B) as b:
                            pe.wait_ge(s_xs, b + 1)
                            for t in range(NT):
                                ins = pe.transpose(PS[:, 0, t * P:t * P + P], xs[:, t, :], ident)
                            ins.then_inc(s_xT, 1)
                            pe.wait_ge(s_xTr, b + 1)
                            for t in range(NT):
                                ins = pe.matmul(PS[:, t, 0:3 * D], xT[:, t * P:t * P + P], wqkv_[:, :], start=True, stop=True)
                            ins.then_inc(s_qkv, 1)
                            pe.wait_ge(s_qp, b + 1)
                            pe.wait_ge(s_kp, b + 1)
                            for i in range(H // 2):
                                if i >= 2:
                                    pe.wait_ge(s_qe, b * (H // 2) + i - 1)
                                    pe.wait_ge(s_ke, b * (H // 2) + i - 1)
                                for a in range(2):
                                    for j in range(2):
                                        h = 2 * i + j
                                        for t in range(NT):
                                            ins = pe.matmul(PS[0:KS, 4 * (i % 2) + 2 * a + j, t * P:t * P + P],
                                                            PK[:, a, t * H + h, :], identb[:, :], start=True, stop=True)
                                    ins.then_inc(s_qt, 1)
                            pe.wait_ge(s_qe, (b + 1) * (H // 2))
                            pe.wait_ge(s_ke, (b + 1) * (H // 2))

                            def maxima(h):
                                for it in range(NT):
                                    m = NT * h + it
                                    if m >= 2:
                                        pe.wait_ge(s_mx, b * H * NT + m - 1)
                                    pe.matmul(PS[:, m % 2, :], QT[0:KS, h, it * P:it * P + P], KT[0:KS, h, :],
                                              start=True, stop=True).then_inc(s_mp, 1)

                            def scores(h):
                                if first:
                                    if h >= 2:
                                        pe.wait_ge(s_ex, b * H + h - 1)
                                    base = 3 * (h % 2)
                                    for jt in range(NT):
                                        n = T - jt * P
                                        o = PS[:, base + (0, 1, 2, 1)[jt], (0, 0, 0, 3 * P)[jt]:]
                                        pe.matmul(o[:, 0:n], KT[0:KS, h, jt * P:jt * P + P], QT[0:KS, h, jt * P:T], start=True, stop=False)
                                        ins = pe.matmul(o[:, 0:P], identb[:, :], trib[:, :], start=False, stop=True)
                                    ins.then_inc(s_sc, 1)
                                else:
                                    pe.wait_ge(s_mc, b * H + h + 1)
                                    for a in range(2):
                                        m = 2 * h + a
                                        if m >= 2:
                                            pe.wait_ge(s_ex, b * 2 * H + m - 1)
                                        for i in range(2):
                                            jt = 2 * a + i
                                            ins = pe.matmul(PS[:, 2 + 2 * (m % 2) + i, :], KT[:, h, jt * P:jt * P + P], QT[:, h, :],
                                                            start=True, stop=True)
                                        ins.then_inc(s_sc, 1)

                            def values(g, jt):
                                if jt == 0:
                                    pe.wait_ge(s_ex, (b * H + GH * (g + 1)) * (1 if first else 2))
                                    if g:
                                        pe.wait_ge(s_pve, b * NG + g)
                                for i in range(GH):
                                    h = GH * g + i
                                    at, q0 = keys(jt)
                                    ins = pe.matmul(PS[PAD * i:PAD * i + PAD, 6, q0:T], V[:, jt, h % NV0 if first else h, :],
                                                    PT[:, h % PTN, at:at + T - q0], start=(jt == 0), stop=(jt == NT - 1),
                                                    skip_group_check=True)
                                if jt == NT - 1:
                                    ins.then_inc(s_pv, 1)

                            for st in range(STEPS):
                                gm, ge, gv, gy = st, st - LAG, st - LAG - 1, st - LAG - 2
                                if LAG and 0 <= gm - 1 < NG:
                                    pe.wait_ge(s_ms, b * NG + gm)
                                    if gy - 1 >= 0:
                                        pe.wait_ge(s_yn, b * NG + gy)
                                    for t in range(NT):
                                        ins = pe.matmul(PS[:, 7, t * P:t * P + P], MXS[:, t, :, :].rearrange("p h k -> p (h k)"), identb[:, :],
                                                        start=True, stop=True)
                                    ins.then_inc(s_mt, 1)
                                for k in range(GH):
                                    if LAG and gm < NG:
                                        maxima(GH * gm + k)
                                    if k == 0 and 0 <= gy < NG:
                                        pe.wait_ge(s_pve, b * NG + gy + 1)
                                        if LAG and gm - 1 < NG:
                                            pe.wait_ge(s_me, b * NG + gm)
                                        elif gy:
                                            pe.wait_ge(s_yn, b * NG + gy)
                                        for t in range(NT):
                                            ins = pe.transpose(PS[:, 7, t * P:t * P + P], OT[:, t * P:t * P + P], ident)
                                        ins.then_inc(s_yg, 1)
                                    if 0 <= ge < NG:
                                        scores(GH * ge + k)
                                    if 0 <= gv < NG:
                                        values(gv, k)
                            if first:
                                pe.wait_ge(s_xd, b + 1)
                                for t in range(NT):
                                    ins = pe.transpose(PS[:, 1, t * P:t * P + P], xd[:, t, :], ident)
                                ins.then_inc(s_xt, 1)
                            pe.wait_ge(s_yn, (b + 1) * NG)
                            for t in range(NT):
                                ins = pe.transpose(PS[:, 0, t * P:t * P + P], Y[:, t, :], ident)
                            ins.then_inc(s_yt, 1)
                            pe.wait_ge(s_ye, b + 1)
                            if first:
                                pe.wait_ge(s_xe, b + 1)
                            for t in range(NT):
                                o = PS[:, 2, t * P:t * P + P]
                                if first:
                                    pe.matmul(o, xdT[:, t * P:t * P + P], WFT[:, :], start=True, stop=False)
                                ins = pe.matmul(o, YT[:, t * P:t * P + P], wo_[:, :], start=not first, stop=True)
                            ins.then_inc(s_pr, 1)

                    @block.scalar
                    def _(act):
                        with act.Fori(0, B) as b:
                            act.wait_ge(s_xT, b + 1)
                            act.activation(xT[:, :], PS[:, 0, :], ACT.Copy).then_inc(s_xTr, 1)
                            if first:
                                act.wait_ge(s_qkv, b + 1)
                                act.activation(sq[:, :, :], PS[:, 0:NT, 0:2 * D], ACT.Square).then_inc(s_sq, 1)
                            act.wait_ge(s_spl, b + 1)
                            act.activation(PK[:, 0].rearrange("p n (r k) -> p n r k", r=3),
                                           SP[:, 0].rearrange("p t h c e -> p (t h) (c e)").unsqueeze(2).to_broadcast([P, NT * H, 3, 3 * HD]),
                                           ACT.Copy).then_inc(s_qp, 1)
                            for i in range(H // 2):
                                act.wait_ge(s_qt, b * H + 2 * i + 1)
                                b0 = 4 * (i % 2)
                                act.activation(QT[0:KS, 2 * i:2 * i + 2, :], PS[0:KS, b0:b0 + 2, :], ACT.Copy).then_inc(s_qe, 1)

                            def sums_out(g):
                                act.wait_ge(s_pv, b * NG + g + 1)
                                if g:
                                    act.wait_ge(s_yg, b * NG + g)
                                act.activation(OT[:, :], PS[:, 6, :], ACT.Copy).then_inc(s_pve, 1)

                            for st in range(STEPS):
                                gm, ge = st - 1, st - LAG
                                if LAG and 0 <= gm < NG:
                                    act.wait_ge(s_mt, b * NG + gm + 1)
                                    if gm:
                                        act.wait_ge(s_mc, b * H + GH * gm)
                                    act.activation(MXT[:, :], PS[:, 7, :], ACT.Copy).then_inc(s_me, 1)
                                if 0 <= ge < NG:
                                    for k in range(GH):
                                        h = GH * ge + k
                                        if ge >= 2 and k == 0:
                                            act.wait_ge(s_pv, b * NG + ge - 1)
                                        if first:
                                            act.wait_ge(s_sc, b * H + h + 1)
                                            n = 10 * P
                                            act.activation(PT[:, h % PTN, 0:n],
                                                           PS[:, 3 * (h % 2):3 * (h % 2) + 3, :].rearrange("p k n -> p (k n)")[:, 0:n],
                                                           ACT.Exp, scale=scale).then_inc(s_ex, 1)
                                        else:
                                            for a in range(2):
                                                m = 2 * h + a
                                                act.wait_ge(s_sc, b * 2 * H + m + 1)
                                                act.activation(PT[:, h % PTN, a * 2 * T:(a + 1) * 2 * T],
                                                               PS[:, 2 + 2 * (m % 2):4 + 2 * (m % 2), :].rearrange("p k n -> p (k n)"),
                                                               ACT.Exp, scale=scale).then_inc(s_ex, 1)
                                if 0 <= ge - 1 < NG:
                                    sums_out(ge - 1)
                            if first:
                                act.wait_ge(s_xt, b + 1)
                                act.activation(xdT[:, :], PS[:, 1, :], ACT.Copy).then_inc(s_xe, 1)
                            act.wait_ge(s_yt, b + 1)
                            act.activation(YT[:, :], PS[:, 0, :], ACT.Copy).then_inc(s_ye, 1)

                    @block.vector
                    def _(dve):
                        with dve.Fori(0, B) as b:
                            n = [0]

                            def link(ins):
                                n[0] += 1
                                ins.then_inc(s_ch, 1)
                                dve.wait_ge(s_ch, b * NC + n[0])

                            def parts(src, rest, to):
                                for i in range(3):
                                    for k, r in enumerate(rest):
                                        ins = nc.vector.tensor_copy(to(i, k), r if i else src[k])
                                    if i < 2:
                                        link(ins)
                                        for k, r in enumerate(rest):
                                            ins = nc.vector.tensor_tensor(r, r if i else src[k], to(i, k), ALU.subtract)
                                        link(ins)
                                return ins

                            dve.wait_ge(s_qkv, b + 1)
                            qk = PS[:, 0:NT, 0:2 * D].rearrange("p t (h e) -> p t h e", e=HD)
                            v = PS[:, 0:NT, 2 * D:3 * D].rearrange("p t (h e) -> p t h e", e=hv)
                            split = lambda i, a: SP[:, a, :, :, i, :]
                            if first:
                                dve.wait_ge(s_sq, b + 1)
                            for t in range(NT):
                                nc.vector.tensor_copy(V[:, t, :, 0:hv], v[:, t])
                            q4 = qn[:, :, :].rearrange("p t (h e) -> p t h e", e=HD)
                            if first:
                                link(nc.vector.tensor_reduce(rms[:, 0, :, :], sq[:, :, :].rearrange("p t (h e) -> p t h e", e=HD), AX.X, ALU.add))
                                link(nc.vector.tensor_scalar(rms[:, 0, :, :], rms[:, 0, :, :], 1.0 / HD, float(np.finfo(np.float32).eps),
                                                             ALU.mult, ALU.add))
                                rsqrt(link, rms[:, 1, :, :], rms[:, 0, :, :], rms[:, 2, :, :])
                                link(nc.vector.tensor_tensor(q4, qk, rms[:, 1, :, :].unsqueeze(3).to_broadcast([P, NT, 2 * H, HD]), ALU.mult))
                                rot = CT[:, C_ROT:C_XP].rearrange("p (a t e) -> p a t e", a=2, t=NT)
                                a4 = ra[:, :, :].rearrange("p t (h e) -> p t h e", e=HD)
                                half = HD // 2
                                wide = lambda z, e: z.unsqueeze(2).to_broadcast([P, NT, 2 * H, e])
                                nc.vector.tensor_tensor(a4[:, :, :, 0:half], q4[:, :, :, half:HD], wide(rot[:, 1, :, 0:half], half), ALU.mult)
                                link(nc.vector.tensor_tensor(a4[:, :, :, half:HD], q4[:, :, :, 0:half], wide(rot[:, 1, :, half:HD], half), ALU.mult))
                                link(nc.vector.tensor_tensor(q4, q4, wide(rot[:, 0, :, :], HD), ALU.mult))
                                link(nc.vector.tensor_tensor(q4, q4, a4, ALU.add))
                            both = lambda z: [z[:, :, a * H:(a + 1) * H, :] for a in range(2)]
                            parts(both(q4 if first else qk), both(q4), split).then_inc(s_spl, 1)
                            dve.wait_ge(s_spl, b + 1)
                            for c in range(3):
                                ins = nc.vector.tensor_copy(PK[:, 1, :, 3 * HD * c:3 * HD * (c + 1)].rearrange("p n (r e) -> p n r e", r=3),
                                                            SP[:, 1, :, :, c, :].rearrange("p t h e -> p (t h) e").unsqueeze(2)
                                                            .to_broadcast([P, NT * H, 3, HD]))
                            ins.then_inc(s_kp, 1)
                            for i in range(H // 2):
                                dve.wait_ge(s_qt, b * H + 2 * i + 2)
                                b0 = 4 * (i % 2) + 2
                                nc.vector.tensor_copy(KT[0:KS, 2 * i:2 * i + 2, :], PS[0:KS, b0:b0 + 2, :]).then_inc(s_ke, 1)
                            if first:
                                fake_quant(link, xs[:, :, :].rearrange("p t d -> p (t d)"),
                                           xd[:, :, :].rearrange("p t d -> p (t d)"), 16).then_inc(s_xd, 1)

                            def outputs(g):
                                dve.wait_ge(s_yg, b * NG + g + 1)
                                o = PS[:, 7, :].rearrange("p (t h e) -> p t h e", t=NT, h=GH)
                                den, rc = o[:, :, :, hv], rec[:, g % 2, :, :]
                                if not first:
                                    link(nc.vector.tensor_scalar(rc, den, 1e-8, None, ALU.add))
                                    den = rc
                                link(nc.vector.reciprocal(rc, den))
                                h0 = GH * g if not first else GH * (g % 2)
                                yo = Y[:, :, h0 * hv:(h0 + GH) * hv].rearrange("p t (h e) -> p t h e", e=hv)
                                rw = rc.unsqueeze(3).to_broadcast([P, NT, GH, hv])
                                if first and g >= 2:
                                    link(nc.vector.tensor_tensor(yt[:, :, :, :], o[:, :, :, 0:hv], rw, ALU.mult))
                                    ins = nc.vector.scalar_tensor_tensor(out=yo, in0=yt[:, :, :, :], scalar=nlam, in1=yo,
                                                                         op0=ALU.mult, op1=ALU.add)
                                else:
                                    ins = nc.vector.tensor_tensor(yo, o[:, :, :, 0:hv], rw, ALU.mult)
                                ins.then_inc(s_yn, 1)

                            for st in range(STEPS):
                                gm, gy = st, st - LAG - 2
                                for k in range(GH):
                                    if LAG and gm < NG:
                                        h = GH * gm + k
                                        for it in range(NT):
                                            m = NT * h + it
                                            dve.wait_ge(s_mp, b * H * NT + m + 1)
                                            nc.vector.tensor_reduce(mxs[:, it, k:k + 1], PS[:, m % 2, :], AX.X, ALU.max, negate=True).then_inc(s_mx, 1)
                                    if k == 1 and 0 <= gy < NG:
                                        outputs(gy)
                                if LAG and gm < NG:
                                    dve.wait_ge(s_mx, (b * H + GH * (gm + 1)) * NT)
                                    if gm:
                                        dve.wait_ge(s_mt, b * NG + gm)
                                    parts([mxs[:, :, :]], [mxs[:, :, :]], lambda i, k: MXS[:, :, :, i]).then_inc(s_ms, 1)
                                    dve.wait_ge(s_ms, b * NG + gm + 1)
                            src = X0 if first else X1
                            dve.wait_ge(s_pr, b + 1)
                            pr = qn[:, 0:2, :].rearrange("p a (t d) -> p (a t) d", d=D)
                            link(nc.vector.tensor_tensor(pr, PS[:, 2, :].rearrange("p (t d) -> p t d", d=D),
                                                         bias_.unsqueeze(1).to_broadcast([P, NT, D]), ALU.add))
                            tiles = lambda z: z[:, :, :].rearrange("p (b t) d -> p b t d", b=B)[:, b]
                            nc.vector.tensor_tensor(tiles(X1), tiles(src), pr, ALU.add).then_inc(s_bt, 1)
                            assert n[0] == NC, n[0]

            attention(True)

            with ExitStack() as c2:
                def sem(name):
                    return scoped(c2, name)

                names = [sem(n) for n in ("ln1_sum", "ln1_centred", "ln1_sq", "ln1_chain")]
                block = phase(c2)
                normalise_rows(block, X1, names, sums, sqs)

            attention(False)

        with ExitStack() as ctx:
            WQ = sb("WQ", [P, 3 * INNER], F32, ctx)
            WO = sb("WO", [P, INNER // P, D], F32, ctx)
            QK = sb("QK", [P, 2, DH], F32, ctx)
            WA = sb("WA", [P, 2 * DI], F32, ctx)
            WB = sb("WB", [P, DCH, D], F32, ctx)
            COL = sb("COL", [P, 2 + 2 * DCH], F32, ctx)
            B2 = sb("B2", [P, D], F32, ctx)
            TC = sb("TC", [P, NT, 2, DH], F32, ctx)
            TS = sb("TS", [P, NT, 2, DH], F32, ctx)

            def two(name, shape):
                return [sb(f"{name}{s}", shape, F32, ctx) for s in range(2)]

            xs = two("ls_xs", [P, NT, D])
            xsT = two("ls_xsT", [P, WIN + T])
            Q = two("ls_q", [P, 2 * INNER])
            A = two("ls_a", [P, 2 * INNER])
            R = two("ls_r", [P, 2 * INNER])
            qT = two("ls_qT", [P, H, P])
            kT = two("ls_kT", [P, 2, H // 2, WIN + P])
            VB = two("ls_vb", [P, NW, H // 2, 2 * (DH + 1)])
            Y = [a[:, 0:INNER] for a in A]
            YT = [a[:, INNER:].rearrange("p (i n) -> p i n", n=P) for a in A]
            ss = two("ls_ss", [P, 2 * H])
            rn = two("ls_rn", [P, 2, 2 * H])
            mx = two("ls_mx", [P, H])
            rc = two("ls_rc", [P, H])
            st = two("ls_st", [P, NT])

            def sem(name):
                return scoped(ctx, name)

            def sems(name):
                return [scoped(ctx, f"{name}{s}") for s in range(2)]

            w_attn, w_ffn = sem("attn_weights"), sem("ffn_weights")
            free_attn, free_ffn = sem("attn_weights_free"), sem("ffn_weights_free")
            s_tab, s_zero = sem("tables"), sem("zeros")
            s_xl, s_xm = sems("stream_new"), sems("stream_mid")
            s_sh, s_xu, s_xlo, s_xt, s_xe = sems("shifted"), sems("xs_upper"), sems("xs_lower"), sems("xs_transposed"), sems("xsT_sbuf")
            s_qk, s_sq, s_qn = sems("qk"), sems("squares_qk"), sems("qk_normal")
            s_v, s_ve, s_a, s_rot = sems("v"), sems("v_sbuf"), sems("cos_term"), sems("rotated")
            s_kt, s_ke, s_qt, s_qe = sems("lk_transposed"), sems("lkT_sbuf"), sems("lq_transposed"), sems("lqT_sbuf")
            s_so, s_sub, s_p, s_pt, s_pte = sems("local_scores"), sems("less_max"), sems("local_exp"), sems("expT"), sems("expT_sbuf")
            s_o, s_yn, s_yt, s_ye, s_w = sems("weighted"), sems("out_normal"), sems("out_T"), sems("outT_sbuf"), sems("attn_out")
            f_sh, f_xu, f_xlo, f_c, f_sq, f_xn = (sems("f_" + n) for n in (
                "shifted", "xs_upper", "xs_lower", "centred", "squares", "normal"))
            f_xt, f_xe, f_g, f_ge, f_a, f_u, f_w, f_rb = (sems("f_" + n) for n in (
                "transposed", "xnT_sbuf", "gate", "gelu", "linear", "product", "out", "residual"))
            ch = sems("vector_chain")
            NA, NF = NT * (3 + NRS + 4 + 1), 4 + NRS
            NB = PAIRS * (NA + NF)
            block = phase(ctx)

            def slots():
                for u in range(2 * NT + 1):
                    front = (u % 2, u // 2) if u < 2 * NT else None
                    back = ((u - 1) % 2, (u - 1) // 2) if u else None
                    yield front, back

            def bank(s, i, n=1):
                v = PS[:, 4 * s + i:4 * s + i + n, :]
                return v.rearrange("p b n -> p (b n)")

            @block.sync
            def _(sp):
                with sp.Fori(0, DEPTH) as l:
                    sp.wait_ge(free_attn, l + 1)
                    sp.dma_start(WQ[:, :], wqkv[l]).then_inc(w_attn, 16)
                    sp.dma_start(WO[:, :, :], wo[l]).then_inc(w_attn, 16)
                    sp.dma_start(QK[:, :, :], qkscale[l].rearrange("p (a e) -> p a e", a=2)).then_inc(w_attn, 16)
                    sp.wait_ge(free_ffn, l + 1)
                    sp.dma_start(WA[:, :], w1[l]).then_inc(w_ffn, 16)
                    sp.dma_start(WB[:, :, :], w2[l]).then_inc(w_ffn, 16)
                    sp.dma_start(COL[:, :], cols[l]).then_inc(w_ffn, 16)
                    sp.dma_start(B2[:, :], b2[l]).then_inc(w_ffn, 16)
                sp.wait_ge(w_ffn, DEPTH * 64)

            @block.gpsimd
            def _(pool):
                pool.memset(nhalf[:, 0:1], -0.5).then_inc(free_attn, 1)
                pool.memset(nhalf[:, 1:2], -0.5).then_inc(free_ffn, 1)
                for s in range(2):
                    for i in range(PAIRS):
                        pool.memset(ss[s][:, i:i + 1], 0.0).then_inc(s_xl[s], 1)
                    pool.memset(qT[s][:, :, :], 0.0)
                    pool.memset(xsT[s][:, 0:WIN], 0.0)
                    pool.memset(kT[s][:, 0, :, 0:WIN], 0.0)
                    pool.memset(VB[s][:, :, :, :], 0.0).then_inc(s_zero, 1)
                pool.wait_ge(s_zero, 2)
                for s in range(2):
                    for a in range(2):
                        pool.memset(VB[s][a * DH:a * DH + DH, :, :, a * (DH + 1) + DH:a * (DH + 1) + DH + 1], 1.0).then_inc(s_zero, 1)
                        pool.wait_ge(s_zero, 3 + 2 * s + a)
                    pool.memset(ss[s][:, 0:1], 0.0).then_inc(s_xm[s], 1)
                with pool.Fori(0, DEPTH) as l:
                    pool.wait_ge(w_attn, l * 48 + 48)
                    base = CT[:, C_XP:C_ALL].rearrange("p (k t e) -> p k t e", k=4, t=NT)
                    h2 = DH // 2
                    for a in range(2):
                        wide = lambda z, e: z.unsqueeze(1).to_broadcast([P, NT, e])
                        pool.tensor_tensor(TC[:, :, a, :], base[:, 2 * a], wide(QK[:, a, :], DH), ALU.mult)
                        pool.tensor_tensor(TS[:, :, a, 0:h2], base[:, 2 * a + 1, :, 0:h2], wide(QK[:, a, h2:DH], h2), ALU.mult)
                        ins = pool.tensor_tensor(TS[:, :, a, h2:DH], base[:, 2 * a + 1, :, h2:DH], wide(QK[:, a, 0:h2], h2), ALU.mult)
                    ins.then_inc(s_tab, 1)
                    with pool.Fori(0, PAIRS) as p:
                        m = l * PAIRS + p + 1
                        for s in range(2):
                            pool.wait_ge(s_xl[s], (l + 1) * PAIRS)
                            pool.wait_ge(s_xm[s], m * NT - NT + 1)
                            pool.tensor_copy(xs[s][:, :, 0:D // 2], XL[:, p + s * PAIRS, 1:SLOTS, 0:D // 2]).then_inc(s_xlo[s], 1)
                        v4 = lambda z: z[:, :].rearrange("p (a h e) -> p a h e", a=2, h=H)
                        for front, back in slots():
                            if front:
                                s, t = front
                                n = (m - 1) * NT + t + 1
                                if t == 0 and s == 0:
                                    pool.wait_ge(s_tab, l + 1)
                                for i, a in enumerate((1, 0)):
                                    tab = TC[:, t, a, :].unsqueeze(1).to_broadcast([P, H, DH])
                                    pool.wait_ge(s_qn[s], 2 * n - 1 + i)
                                    pool.tensor_tensor(v4(A[s])[:, a], v4(Q[s])[:, a], tab, ALU.mult).then_inc(s_a[s], 1)
                    with pool.Fori(0, PAIRS) as p:
                        m = l * PAIRS + p + 1
                        pool.wait_ge(w_ffn, l * 64 + 64)
                        for s in range(2):
                            pool.wait_ge(s_xm[s], (l + 1) * PAIRS * NT + 1)
                            pool.wait_ge(s_xl[s], m + PAIRS - 1)
                            pool.tensor_copy(xs[s][:, :, 0:D // 2], XL[:, p + s * PAIRS, 1:SLOTS, 0:D // 2]).then_inc(f_xlo[s], 1)
                        for s in range(2):
                            pool.tensor_tensor(R[s][:, T:2 * T].rearrange("p (t d) -> p t d", t=NT), XL[:, p + s * PAIRS, 1:SLOTS, :],
                                               B2[:, :].unsqueeze(1).to_broadcast([P, NT, D]), ALU.add).then_inc(f_rb[s], 1)

            @block.tensor
            def _(pe):
                def shift(s, src, b, done):
                    o = bank(s, 0)[:, 0:NT * D // 2]
                    pe.matmul(o, CT[:, C_SH:C_SH + P], src[:, b, 1:SLOTS, D // 2:D], start=True, stop=False)
                    pe.matmul(o, CT[:, C_ED:C_ED + P], src[:, b, 0:NT, D // 2:D], start=False, stop=True).then_inc(done, 1)

                with pe.Fori(0, DEPTH) as l:
                    with pe.Fori(0, PAIRS) as p:
                        m = l * PAIRS + p + 1
                        for s in range(2):
                            pe.wait_ge(s_xl[s], (l + 1) * PAIRS)
                            pe.wait_ge(s_xm[s], m * NT - NT + 1)
                            shift(s, XL, p + s * PAIRS, s_sh[s])
                        for s in range(2):
                            pe.wait_ge(s_xu[s], m)
                            pe.wait_ge(s_xlo[s], m)
                            for t in range(NT):
                                ins = pe.transpose(bank(s, 1)[:, t * P:t * P + P], xs[s][:, t, :], ident)
                            ins.then_inc(s_xt[s], 1)
                        for front, back in slots():
                            if front:
                                s, t = front
                                n = (m - 1) * NT + t + 1
                                if t == 0:
                                    pe.wait_ge(s_xe[s], m)
                                    pe.wait_ge(w_attn, l * 48 + 48)
                                else:
                                    pe.wait_ge(s_xm[s], n)
                                rows = xsT[s][:, WIN + t * P:WIN + t * P + P]
                                for c in range(4):
                                    ins = pe.matmul(bank(s, c), rows, WQ[:, c * 512:c * 512 + 512], start=True, stop=True)
                                    if c % 2:
                                        ins.then_inc(s_qk[s], 1)
                            if back:
                                s, t = back
                                n = (m - 1) * NT + t + 1
                                pe.wait_ge(s_ke[s], n)
                                pe.wait_ge(s_qe[s], n)
                                for c in range(2):
                                    pe.matmul(bank(s, c), identb[:, :], winb[:, 0 if t else 1, :].unsqueeze(1).to_broadcast([P, H // 2, 2 * WIN]),
                                              start=True, stop=False)
                                    for h in range(c * H // 2, (c + 1) * H // 2):
                                        for w in range(NW):
                                            at = (h % (H // 2)) * 2 * WIN
                                            ins = pe.matmul(bank(s, c)[WIN * w:WIN * w + WIN, at:at + 2 * WIN], qT[s][:, h, WIN * w:WIN * w + WIN],
                                                            kT[s][:, t % 2, h // 2, WIN * w:WIN * w + 2 * WIN],
                                                            start=False, stop=(h % (H // 2) == H // 2 - 1))
                                    ins.then_inc(s_so[s], 1)
                                for c in range(2):
                                    pe.wait_ge(s_p[s], 2 * n - 1 + c)
                                    for i in range(4):
                                        at = c * 4 * P + i * P
                                        ins = pe.transpose(bank(s, 2 + c)[:, i * P:i * P + P], Q[s][:, at:at + P], ident)
                                    ins.then_inc(s_pt[s], 1)
                                for i in range(H // 2):
                                    if i in (0, 4):
                                        pe.wait_ge(s_pte[s], 2 * n - 1 + i // 4)
                                    for w in range(NW):
                                        at = (i % 3) * 2 * (DH + 1)
                                        ins = pe.matmul(bank(s, i // 3)[WIN * w:WIN * w + WIN, at:at + 2 * (DH + 1)],
                                                        R[s][:, i * P + WIN * w:i * P + WIN * w + WIN], VB[s][:, w, i, :], start=True, stop=True)
                                ins.then_inc(s_o[s], 1)
                            def values(c):
                                s, t = front
                                n = (m - 1) * NT + t + 1
                                pe.wait_ge(s_qn[s], 2 * n - 1 + c)
                                for w in (2 * c, 2 * c + 1):
                                    rows = xsT[s][:, t * P + WIN * w:t * P + WIN * w + 2 * WIN]
                                    for a in range(2):
                                        wv = WQ[:, 2 * INNER:].rearrange("p (i a e) -> p a i e", a=2, e=DH)[:, a]
                                        ins = pe.matmul(bank(s, 2 - 2 * c + w % 2)[a * DH:a * DH + DH, :], rows, wv, start=True, stop=True)
                                ins.then_inc(s_v[s], 1)

                            if front:
                                values(0)
                            if back:
                                s, t = back
                                n = (m - 1) * NT + t + 1
                                pe.wait_ge(s_yn[s], n)
                                for i in range(INNER // P):
                                    ins = pe.transpose(bank(s, 0, 2)[:, i * P:i * P + P], Y[s][:, i * P:i * P + P], ident)
                                ins.then_inc(s_yt[s], 1)
                            if front:
                                values(1)
                            if back:
                                s, t = back
                                n = (m - 1) * NT + t + 1
                                pe.wait_ge(s_ye[s], n)
                                for i in range(INNER // P):
                                    ins = pe.matmul(bank(s, 2)[:, 0:D], YT[s][:, i, :], WO[:, i, :], start=(i == 0), stop=(i == INNER // P - 1))
                                ins.then_inc(s_w[s], 1)
                            if front:
                                s, t = front
                                n = (m - 1) * NT + t + 1
                                for a, done in ((1, s_kt), (0, s_qt)):
                                    pe.wait_ge(s_rot[s], 2 * n - a)
                                    pe.wait_ge(s_ve[s], 2 * n - a)
                                    for i in range(H // 2):
                                        at = a * INNER + i * P
                                        ins = pe.transpose(bank(s, 2 * a, 2)[:, i * P:i * P + P], A[s][:, at:at + P], ident)
                                    ins.then_inc(done[s], 1)
                    with pe.Fori(0, PAIRS) as p:
                        m = l * PAIRS + p + 1
                        for s in range(2):
                            pe.wait_ge(s_xm[s], m * NT + 1)
                            pe.wait_ge(s_xl[s], m + PAIRS - 1)
                            shift(s, XL, p + s * PAIRS, f_sh[s])
                        for s in range(2):
                            pe.wait_ge(f_xn[s], m)
                            for t in range(NT):
                                ins = pe.transpose(bank(s, 1)[:, t * P:t * P + P], xs[s][:, t, :], ident)
                            ins.then_inc(f_xt[s], 1)
                        for part, done, after in ((1, f_g, f_xe), (0, f_a, f_ge)):
                            for s in range(2):
                                if part and s == 0:
                                    pe.wait_ge(w_ffn, l * 64 + 64)
                                pe.wait_ge(after[s], m)
                                for c in range(DCH):
                                    k = P if c < DCH - 1 else DLAST
                                    at = part * DI + c * P
                                    ins = pe.matmul(bank(s, 1 + c)[0:k], WA[:, at:at + k], xsT[s][:, WIN:], start=True, stop=True)
                                ins.then_inc(done[s], 1)
                        for s in range(2):
                            pe.wait_ge(f_u[s], m)
                            for t in range(NT):
                                for c in range(DCH):
                                    k = P if c < DCH - 1 else DLAST
                                    ins = pe.matmul(bank(s, 0)[:, t * P:t * P + P], A[s][0:k, c * T + t * P:c * T + t * P + P], WB[0:k, c, :],
                                                    start=(c == 0), stop=(c == DCH - 1))
                            ins.then_inc(f_w[s], 1)

            @block.scalar
            def _(act):
                with act.Fori(0, DEPTH) as l:
                    with act.Fori(0, PAIRS) as p:
                        m = l * PAIRS + p + 1
                        for s in range(2):
                            act.wait_ge(s_sh[s], m)
                            act.activation(xs[s][:, :, D // 2:D], bank(s, 0)[:, 0:NT * D // 2].rearrange("p (t d) -> p t d", t=NT), ACT.Copy).then_inc(s_xu[s], 1)
                        for s in range(2):
                            act.wait_ge(s_xt[s], m)
                            act.activation(xsT[s][:, WIN:], bank(s, 1), ACT.Copy).then_inc(s_xe[s], 1)
                        for front, back in slots():
                            if front:
                                s, t = front
                                n = (m - 1) * NT + t + 1
                                for c in range(2):
                                    act.wait_ge(s_qk[s], 2 * n - 1 + c)
                                    act.activation(R[s][:, c * INNER:(c + 1) * INNER], bank(s, 2 * c, 2), ACT.Square).then_inc(s_sq[s], 1)
                            if back:
                                s, t = back
                                n = (m - 1) * NT + t + 1
                                for c in range(2):
                                    half = Q[s][:, c * T:c * T + T]
                                    act.wait_ge(s_sub[s], 2 * n - 1 + c)
                                    act.activation(half, half, ACT.Exp).then_inc(s_p[s], 1)
                                for c in range(2):
                                    act.wait_ge(s_pt[s], 2 * n - 1 + c)
                                    act.activation(R[s][:, c * T:c * T + T], bank(s, 2 + c), ACT.Copy).then_inc(s_pte[s], 1)
                            if front:
                                s, t = front
                                n = (m - 1) * NT + t + 1
                                for c in range(2):
                                    act.wait_ge(s_v[s], 2 * n - 1 + c)
                                    for a in range(2):
                                        ins = act.activation(VB[s][a * DH:a * DH + DH, 2 * c:2 * c + 2, :, a * (DH + 1):a * (DH + 1) + DH],
                                                             bank(s, 2 - 2 * c, 2)[a * DH:a * DH + DH].rearrange("p (w i e) -> p w i e", w=2, e=DH), ACT.Copy)
                                    ins.then_inc(s_ve[s], 1)
                            if front:
                                s, t = front
                                n = (m - 1) * NT + t + 1
                                act.wait_ge(s_kt[s], n)
                                k_ = bank(s, 2, 2).rearrange("p (i n) -> p i n", n=P)
                                ins = act.activation(kT[s][:, t % 2, :, WIN:], k_, ACT.Copy)
                                if t < NT - 1:
                                    ins = act.activation(kT[s][:, 1 - t % 2, :, 0:WIN], k_[:, :, P - WIN:P], ACT.Copy)
                                ins.then_inc(s_ke[s], 1)
                                act.wait_ge(s_qt[s], n)
                                for a in range(2):
                                    ins = act.activation(qT[s][a * DH:a * DH + DH, a:H:2, :],
                                                         bank(s, 0, 2)[a * DH:a * DH + DH].rearrange("p (i n) -> p i n", n=P), ACT.Copy)
                                ins.then_inc(s_qe[s], 1)
                    with act.Fori(0, PAIRS) as p:
                        m = l * PAIRS + p + 1
                        for s in range(2):
                            act.wait_ge(f_sh[s], m)
                            act.activation(xs[s][:, :, D // 2:D], bank(s, 0)[:, 0:NT * D // 2].rearrange("p (t d) -> p t d", t=NT), ACT.Copy).then_inc(f_xu[s], 1)
                        for s in range(2):
                            act.wait_ge(f_c[s], m)
                            act.activation(R[s][:, 0:T].rearrange("p (t d) -> p t d", t=NT), xs[s][:, :, :], ACT.Square).then_inc(f_sq[s], 1)
                        for s in range(2):
                            if s == 0:
                                act.wait_ge(w_ffn, l * 64 + 64)
                            act.wait_ge(f_xt[s], m)
                            act.activation(xsT[s][:, WIN:], bank(s, 1), ACT.Identity, scale=COL[:, 0:1], bias=COL[:, 1:2]).then_inc(f_xe[s], 1)
                        for s in range(2):
                            act.wait_ge(f_g[s], m)
                            for c in range(DCH):
                                k = P if c < DCH - 1 else DLAST
                                at = 2 + DCH + c
                                ins = act.activation(Q[s][0:k, c * T:c * T + T], bank(s, 1 + c)[0:k], ACT.Gelu, bias=COL[0:k, at:at + 1])
                            ins.then_inc(f_ge[s], 1)

            @block.vector
            def _(dve):
                with dve.Fori(0, DEPTH) as l:
                    with dve.Fori(0, PAIRS) as p:
                        m = l * PAIRS + p + 1
                        k = [0, 0]

                        def link(s, ins):
                            k[s] += 1
                            ins.then_inc(ch[s], 1)
                            dve.wait_ge(ch[s], l * NB + p * NA + k[s])

                        v4 = lambda z: z[:, :].rearrange("p (a h e) -> p a h e", a=2, h=H)
                        h2 = DH // 2
                        for front, back in slots():
                            if front:
                                s, t = front
                                n = (m - 1) * NT + t + 1
                                for c in range(2):
                                    dve.wait_ge(s_sq[s], 2 * n - 1 + c)
                                    link(s, nc.vector.tensor_reduce(ss[s][:, c * H:c * H + H], v4(R[s])[:, c], AX.X, ALU.add))
                            if back:
                                s, t = back
                                n = (m - 1) * NT + t + 1
                                for c in range(2):
                                    so = bank(s, c).rearrange("p (h n) -> p h n", n=2 * WIN)
                                    hs = slice(c * H // 2, (c + 1) * H // 2)
                                    dve.wait_ge(s_so[s], 2 * n - 1 + c)
                                    link(s, nc.vector.tensor_reduce(mx[s][:, hs], so, AX.X, ALU.max))
                                    nc.vector.tensor_tensor(Q[s][:, c * T:c * T + T].rearrange("p (h n) -> p h n", n=2 * WIN), so,
                                                            mx[s][:, hs].unsqueeze(2).to_broadcast([P, H // 2, 2 * WIN]), ALU.subtract).then_inc(s_sub[s], 1)
                            if front:
                                s, t = front
                                n = (m - 1) * NT + t + 1
                                link(s, nc.vector.tensor_scalar(ss[s][:, :], ss[s][:, :], 1e-24, None, ALU.max))
                                rsqrt(lambda ins: link(s, ins), rn[s][:, 0, :], ss[s][:, :], rn[s][:, 1, :])
                                for a in (1, 0):
                                    nc.vector.tensor_tensor(v4(Q[s])[:, a], bank(s, 2 * a, 2).rearrange("p (h e) -> p h e", e=DH),
                                                            rn[s][:, 0, a * H:a * H + H].unsqueeze(2).to_broadcast([P, H, DH]),
                                                            ALU.mult).then_inc(s_qn[s], 1)
                                if t == 0 and s == 0:
                                    dve.wait_ge(s_tab, l + 1)
                                for i, a in enumerate((1, 0)):
                                    dve.wait_ge(s_qn[s], 2 * n - 1 + i)
                                    for lo, hi in ((0, h2), (h2, 0)):
                                        ins = nc.vector.tensor_tensor(v4(R[s])[:, a, :, lo:lo + h2], v4(Q[s])[:, a, :, hi:hi + h2],
                                                                      TS[:, t, a, lo:lo + h2].unsqueeze(1).to_broadcast([P, H, h2]), ALU.mult)
                                    link(s, ins)
                            if back:
                                s, t = back
                                n = (m - 1) * NT + t + 1
                                dve.wait_ge(s_o[s], n)
                                full = PS[:, 4 * s:4 * s + 2, 0:6 * (DH + 1)].rearrange("p b (h e) -> p b h e", h=6)
                                rest = bank(s, 2)[:, 0:4 * (DH + 1)].rearrange("p (h e) -> p h e", h=4)
                                r6 = rc[s][:, 0:12].rearrange("p (b h) -> p b h", b=2)
                                y6 = Y[s][:, 0:12 * DH].rearrange("p (b h e) -> p b h e", b=2, e=DH)
                                nc.vector.reciprocal(r6, full[:, :, :, DH])
                                link(s, nc.vector.reciprocal(rc[s][:, 12:H], rest[:, :, DH]))
                                nc.vector.tensor_tensor(y6, full[:, :, :, 0:DH], r6.unsqueeze(3).to_broadcast([P, 2, 6, DH]), ALU.mult)
                                nc.vector.tensor_tensor(Y[s][:, 12 * DH:].rearrange("p (h e) -> p h e", e=DH), rest[:, :, 0:DH],
                                                        rc[s][:, 12:H].unsqueeze(2).to_broadcast([P, 4, DH]), ALU.mult).then_inc(s_yn[s], 1)
                            def rotated(i, a):
                                s, t = front
                                n = (m - 1) * NT + t + 1
                                dve.wait_ge(s_a[s], 2 * n - 1 + i)
                                nc.vector.tensor_tensor(v4(A[s])[:, a], v4(A[s])[:, a], v4(R[s])[:, a], ALU.add).then_inc(s_rot[s], 1)

                            if front:
                                rotated(0, 1)
                            if back:
                                s, t = back
                                n = (m - 1) * NT + t + 1
                                dve.wait_ge(s_yt[s], n)
                                nc.vector.tensor_copy(YT[s][:, :, :].rearrange("p i n -> p (i n)"), bank(s, 0, 2)).then_inc(s_ye[s], 1)
                            if front:
                                rotated(1, 0)
                            if back:
                                s, t = back
                                n = (m - 1) * NT + t + 1
                                dve.wait_ge(s_w[s], n)
                                tile = XL[:, p + s * PAIRS, t + 1, :]
                                nc.vector.tensor_tensor(tile, bank(s, 2)[:, 0:D], tile, ALU.add).then_inc(s_xm[s], 1)
                        assert k == [NA, NA], k
                    nc.vector.memset(mx[0][:, 0:1], 0.0).then_inc(free_attn, 1)
                    with dve.Fori(0, PAIRS) as p:
                        m = l * PAIRS + p + 1
                        k = [0, 0]

                        def link(s, ins):
                            k[s] += 1
                            ins.then_inc(ch[s], 1)
                            dve.wait_ge(ch[s], l * NB + p * NF + PAIRS * NA + k[s])

                        wide = lambda z: z[:, :].unsqueeze(2).to_broadcast([P, NT, D])
                        for s in range(2):
                            dve.wait_ge(f_xu[s], m)
                            dve.wait_ge(f_xlo[s], m)
                            link(s, nc.vector.tensor_reduce(st[s][:, :], xs[s][:, :, :], AX.X, ALU.add))
                            link(s, nc.vector.tensor_scalar(st[s][:, :], st[s][:, :], -1.0 / D, None, ALU.mult))
                            nc.vector.tensor_tensor(xs[s][:, :, :], xs[s][:, :, :], wide(st[s]), ALU.add).then_inc(f_c[s], 1)
                        for s in range(2):
                            dve.wait_ge(f_sq[s], m)
                            link(s, nc.vector.tensor_reduce(st[s][:, :], R[s][:, 0:T].rearrange("p (t d) -> p t d", t=NT), AX.X, ALU.add))
                            link(s, nc.vector.tensor_scalar(st[s][:, :], st[s][:, :], 1.0 / D, 1e-5, ALU.mult, ALU.add))
                            rsqrt(lambda ins: link(s, ins), rn[s][:, 0, 0:NT], st[s][:, :], rn[s][:, 1, 0:NT])
                            nc.vector.tensor_tensor(xs[s][:, :, :], xs[s][:, :, :], rn[s][:, 0, 0:NT].unsqueeze(2).to_broadcast([P, NT, D]), ALU.mult).then_inc(f_xn[s], 1)
                        for s in range(2):
                            dve.wait_ge(f_a[s], m)
                            for c in range(DCH):
                                kk = P if c < DCH - 1 else DLAST
                                ins = nc.vector.scalar_tensor_tensor(out=A[s][0:kk, c * T:c * T + T], in0=bank(s, 1 + c)[0:kk], scalar=COL[0:kk, 2 + c:3 + c],
                                                                     in1=Q[s][0:kk, c * T:c * T + T], op0=ALU.add, op1=ALU.mult)
                            ins.then_inc(f_u[s], 1)
                        for s in range(2):
                            dve.wait_ge(f_rb[s], m)
                            dve.wait_ge(f_w[s], m)
                            nc.vector.tensor_tensor(XL[:, p + s * PAIRS, 1:SLOTS, :], bank(s, 0).rearrange("p (t d) -> p t d", t=NT),
                                                    R[s][:, T:2 * T].rearrange("p (t d) -> p t d", t=NT), ALU.add).then_inc(s_xl[s], 1)
                        assert k == [NF, NF], k
                    nc.vector.memset(mx[0][:, 0:1], 0.0).then_inc(free_ffn, 1)

        with ExitStack() as c2:
            s_o = scoped(c2, "stored")
            s_f = scoped(c2, "summed")
            block = phase(c2)

            @block.vector
            def _(dve):
                for b in range(B):
                    o = X1[:, b * NT:b * NT + NT, :]
                    dve.tensor_tensor(o, o, XL[:, b, 1:SLOTS, :], ALU.add).then_inc(s_f, 1)

            @block.sync
            def _(sp):
                ov = out.rearrange("b (t p) d -> p b t d", p=P)
                for b in range(B):
                    sp.wait_ge(s_f, b + 1)
                    sp.dma_start(ov[:, b], X1[:, b * NT:b * NT + NT, :]).then_inc(s_o, 16)
                sp.wait_ge(s_o, 16 * B)


def kernel(**inputs):
    import concourse.bacc as _bacc
    from concourse.bass_utils import run_bass_kernel_spmd as _run

    a = {k: np.asarray(v) for k, v in inputs.items()}
    rep = lambda v, n=P: np.ascontiguousarray(np.broadcast_to(v, (n,) + v.shape))
    l0, l1, lf = "L0_attn_", "L1_attn_", "L1_ffn_"
    rows0 = np.concatenate([a["L0_ffn_bias"], a[l1 + "bo"], a[l0 + "lambda_q1"], a[l0 + "lambda_q2"],
                            a[l0 + "lambda_k1"], a[l0 + "lambda_k2"]])
    qk = np.concatenate([a[lf + "q_scale"], a[lf + "k_scale"]], 1)
    pad = lambda w, n: np.concatenate([w, np.zeros((DEPTH, n) + w.shape[2:], w.dtype)], 1)
    fill = DCH * P - DI
    b1 = a[lf + "b1"]
    b1c = [pad(b1[:, i * DI:(i + 1) * DI], fill).reshape(DEPTH, DCH, P).transpose(0, 2, 1) for i in range(2)]
    cols = np.concatenate([a[lf + "ln_g"][:, :, None], a[lf + "ln_b"][:, :, None]] + b1c, 2)
    arrays = {
        "x": a[l0 + "x"], "consts": constants(),
        "wqkv0": np.concatenate([a[l0 + n].T for n in ("Wq", "Wk", "Wv")], 1), "wproj0": a[l0 + "Wproj"].T,
        "wff0": a["L0_ffn_weight"], "rows0": rep(rows0),
        "wqkv1": np.concatenate([a[l1 + n].T for n in ("Wq", "Wk", "Wv")], 1), "wo1": a[l1 + "Wo"].T,
        "wqkv": a[lf + "Wqkv"], "wo": a[lf + "Wo"].reshape(DEPTH, INNER // P, P, D).transpose(0, 2, 1, 3),
        "qkscale": rep(qk).transpose(1, 0, 2), "w1": a[lf + "W1"],
        "w2": pad(a[lf + "W2"], fill).reshape(DEPTH, DCH, P, D).transpose(0, 2, 1, 3),
        "cols": cols, "b2": rep(a[lf + "b2"]).transpose(1, 0, 2),
    }
    arrays = {k: np.ascontiguousarray(v) for k, v in arrays.items()}
    nc = _bacc.Bacc("TRN2", target_bir_lowering=False, num_devices=1)
    args = [nc.dram_tensor(k, v.shape, mybir.dt.from_np(v.dtype), kind="ExternalInput").ap() for k, v in arrays.items()]
    out = nc.dram_tensor("out", (B, T, D), F32, kind="ExternalOutput").ap()
    program(nc, *args, out)
    r = _run(nc, [arrays], core_ids=[0])
    return r.results[0]["out"]
```

```python
from contextlib import ExitStack

import numpy as np

import concourse.bass as bass
from concourse import mybir

F32 = mybir.dt.float32
BF16 = mybir.dt.bfloat16
ALU = mybir.AluOpType
ACT = mybir.ActivationFunctionType
AX = mybir.AxisListType

P = 128
D = 128
B = 8
T = 512
NT = T // P
SLOTS = NT + 1
NEG = -1e30
H = 16
HD = D // H
HV0 = 2 * HD
NV0 = H // 2
PAD = 32
GH = P // PAD
NG = H // GH
PTN = 2 * GH
KS = 9 * HD
MROW = 96
DEPTH = 6
DH = 64
INNER = H * DH
WIN = 32
NW = P // WIN
DI = int(D * 4 * 2 / 3)
DCH = 3
DLAST = DI - 2 * P
LAMBDA_INIT = 0.8 - 0.6 * float(np.exp(-0.3 * 1))
MAGIC = 1.5 * 2.0 ** 23
PAIRS = B // 2

C_ID, C_SH, C_ED, C_TRI, C_WIN, C_WIN0 = 0, 128, 256, 384, 512, 576
C_ROT = C_WIN0 + 2 * WIN
C_XP = C_ROT + 2 * NT * HD
C_ALL = C_XP + 4 * NT * DH


def constants():
    c = np.zeros((P, C_ALL), np.float32)
    i = np.arange(P)
    c[:, C_ID:C_ID + P] = np.eye(P)
    c[i[:-1], C_SH + i[1:]] = 1.0
    c[P - 1, C_ED] = 1.0
    q, k = i[:, None], i[None, :]
    w, r = np.arange(P)[:, None] % WIN, np.arange(2 * WIN)[None, :] - WIN
    c[:, C_WIN:C_WIN + 2 * WIN] = np.where((r <= w) & (w - r <= WIN), 0.0, NEG)
    c[:, C_WIN0:C_WIN0 + 2 * WIN] = c[:, C_WIN:C_WIN + 2 * WIN]
    c[:WIN, C_WIN0:C_WIN0 + WIN] = NEG
    c[:, C_TRI:C_TRI + P] = np.where(q <= k, 0.0, NEG)
    pos = np.arange(T, dtype=np.float64).reshape(NT, P).T
    f = 1.0 / 10000.0 ** (np.arange(0, HD, 2) / HD)
    a = pos[:, :, None] * f
    rot = np.stack([np.concatenate([np.cos(a), np.cos(a)], -1),
                    np.concatenate([np.sin(a), -np.sin(a)], -1)], 1)
    c[:, C_ROT:C_XP] = rot.reshape(P, -1)
    half = np.arange(0, DH, 2)
    a = pos[:, :, None] * (1.0 / 10000.0 ** (half / DH))
    s = ((half + 0.4 * DH) / (1.4 * DH)) ** ((pos[:, :, None] - T // 2) / (WIN // 2))
    cos, sin = np.cos(a), np.sin(a)
    xp = [np.concatenate([cos * s, cos * s], -1), np.concatenate([-sin * s, sin * s], -1),
          np.concatenate([cos / s, cos / s], -1) * 8.0, np.concatenate([-sin / s, sin / s], -1) * 8.0]
    c[:, C_XP:] = np.stack(xp, 1).reshape(P, -1)
    return c


def program(nc, x, consts, wqkv0, wproj0, wff0, rows0, wqkv1, wo1, wqkv, wo, qkscale, w1, w2, cols, b2, out):
    with ExitStack() as outer:
        def sb(name, shape, dt=F32, ctx=outer):
            return ctx.enter_context(nc.sbuf_tensor(name, shape, dt))

        PS = outer.enter_context(nc.psum_tensor("PS", [P, 8, 512], F32))
        CT = sb("CT", [P, C_ALL])
        ident = CT[:, C_ID:C_ID + P]
        identb = sb("identb", [P, P], BF16)
        winb = sb("winb", [P, 2, 2 * WIN], BF16)
        trib = sb("trib", [P, P], BF16)
        spare = sb("spare", [P, 2])
        X1 = sb("X1", [P, B * NT, D])
        XL = sb("XL", [P, B, SLOTS, D])

        I32 = mybir.dt.int32

        def rsqrt(link, y, v, t):
            link(nc.vector.tensor_scalar(y.bitcast(I32), v.bitcast(I32), -0.5, float(0x5F3759DF), ALU.mult, ALU.add))
            for _ in range(3):
                link(nc.vector.tensor_tensor(t, y, y, ALU.mult))
                link(nc.vector.scalar_tensor_tensor(out=t, in0=t, scalar=-0.5, in1=v, op0=ALU.mult, op1=ALU.mult))
                link(nc.vector.scalar_tensor_tensor(out=y, in0=t, scalar=1.5, in1=y, op0=ALU.add, op1=ALU.mult))

        NRS = 10

        used = []

        def scoped(ctx, name):
            used.append(ctx.enter_context(nc.semaphore(name)))
            return used[-1]

        def phase(ctx):
            mine = used[:]
            used.clear()

            def clear():
                with nc.Block() as block:
                    @block.gpsimd
                    def _(pool):
                        for s in mine:
                            pool.sem_clear(s)

            ctx.callback(clear)
            return ctx.enter_context(nc.Block())

        def normalise_rows(block, src, sem, sums, sqs, loaded=None):
            s_sum, s_cen, s_sq, s_ch = sem
            mean, var, inv, tmp = (sums[:, i] for i in range(4))

            @block.vector
            def _(dve):
                n = [0]

                def link(ins):
                    n[0] += 1
                    ins.then_inc(s_ch, 1)
                    dve.wait_ge(s_ch, n[0])

                wide = lambda z: z.unsqueeze(2).to_broadcast([P, NT, D])
                for b in range(B):
                    s = src[:, b * NT:b * NT + NT, :]
                    if loaded is not None:
                        dve.wait_ge(loaded[b], 16)
                    link(dve.tensor_reduce(mean[:, b, :], s, AX.X, ALU.add))
                    link(dve.tensor_scalar(mean[:, b, :], mean[:, b, :], -1.0 / D, None, ALU.mult))
                    dve.tensor_tensor(XL[:, b, 1:SLOTS, :], s, wide(mean[:, b, :]), ALU.add).then_inc(s_cen, 1)
                    if b:
                        dve.wait_ge(s_sq, b)
                        dve.tensor_reduce(var[:, b - 1, :], sqs[:, (b - 1) % 2, :, :], AX.X, ALU.add).then_inc(s_sum, 1)
                dve.wait_ge(s_sq, B)
                link(dve.tensor_reduce(var[:, B - 1, :], sqs[:, (B - 1) % 2, :, :], AX.X, ALU.add))
                dve.wait_ge(s_sum, B - 1)
                flat = lambda z: z.rearrange("p b t -> p (b t)")
                link(dve.tensor_scalar(flat(var), flat(var), 1.0 / D, 1e-5, ALU.mult, ALU.add))
                rsqrt(link, flat(inv), flat(var), flat(tmp))
                dve.wait_ge(s_cen, B)
                for b in range(B):
                    o = XL[:, b, 1:SLOTS, :]
                    dve.tensor_tensor(o, o, wide(inv[:, b, :]), ALU.mult)

            @block.scalar
            def _(act):
                for b in range(B):
                    act.wait_ge(s_cen, b + 1)
                    if b >= 2:
                        act.wait_ge(s_sum, b - 1)
                    act.activation(sqs[:, b % 2, :, :], XL[:, b, 1:SLOTS, :], ACT.Square).then_inc(s_sq, 1)

        with ExitStack() as ctx:
            X0 = sb("X0", [P, B * NT, D], F32, ctx)
            W0 = sb("W0", [P, 3 * D], F32, ctx)
            WP0 = sb("WP0", [P, D], F32, ctx)
            WF0 = sb("WF0", [P, D], F32, ctx)
            WFT = sb("WFT", [P, D], F32, ctx)
            W1q = sb("W1q", [P, 3 * D], F32, ctx)
            WO1 = sb("WO1", [P, D], F32, ctx)
            ROWS = sb("ROWS", [P, 2 * D + 16], F32, ctx)
            bias0, bias1, lamv = ROWS[:, 0:D], ROWS[:, D:2 * D], ROWS[:, 2 * D:]
            lam = sb("lam", [P, 8], F32, ctx)
            sums = sb("sums", [P, 4, B, NT], F32, ctx)
            xs = sb("xs", [P, NT, D], F32, ctx)
            xT = sb("xT", [P, T], F32, ctx)
            rms = sb("rms", [P, 3, NT, 2 * H], F32, ctx)
            SP = sb("SP", [P, 2, NT, H, 3, HD], BF16, ctx)
            QT = sb("QT", [P, H, T], BF16, ctx)
            KT = sb("KT", [P, H, T], BF16, ctx)
            mxs = sb("mxs", [P, NT, GH], F32, ctx)
            MXS = sb("MXS", [P, NT, GH, PAD], BF16, ctx)
            MXT = sb("MXT", [P, T], BF16, ctx)
            ONE = sb("ONE", [P, T], BF16, ctx)
            V1 = sb("V1", [P, NT, NV0, PAD], F32, ctx)
            V2 = sb("V2", [P, NT, H, PAD], F32, ctx)
            PT = sb("PT", [P, PTN, NT * T], F32, ctx)
            half = NT * T // 2
            sq, ra = (PT[:, 0, i * half:(i + 1) * half].rearrange("p (t c) -> p t c", t=NT) for i in range(2))
            qn = PT[:, 1, 0:half].rearrange("p (t c) -> p t c", t=NT)
            PK = PT[:, 2:5, :].rearrange("p a n -> p (a n)")[:, 0:NT * H * KS].bitcast(BF16)
            PK = PK.rearrange("p (a n k) -> p a n k", a=2, k=KS)
            sqs = PT[:, 1, half:].rearrange("p (a t d) -> p a t d", a=2, t=NT)
            OT = sb("OT", [P, T], F32, ctx)
            Y = sb("Y", [P, NT, D], F32, ctx)
            yt = sb("yt", [P, NT, GH, HV0], F32, ctx)
            rec = sb("rec", [P, 2, NT, GH], F32, ctx)
            YT = sb("YT", [P, T], F32, ctx)
            xd = sb("xd", [P, NT, D], F32, ctx)
            xdT = sb("xdT", [P, T], F32, ctx)
            qa = sb("qa", [P, NT * D], F32, ctx)
            qb = sb("qb", [P, NT * D], F32, ctx)
            qc = sb("qc", [P, NT * D], F32, ctx)
            qs = sb("qs", [P, 2, 16], F32, ctx)

            with ExitStack() as c2:
                def sem(name):
                    return scoped(c2, name)

                s_ld = [sem(f"x_loaded{b}") for b in range(B)]
                s_cst = sem("constants_loaded")
                s_mem = sem("memsets_done")
                names = [sem(n) for n in ("ln0_sum", "ln0_centred", "ln0_sq", "ln0_chain")]
                block = phase(c2)

                @block.sync
                def _(sp):
                    xv = x.rearrange("b (t p) d -> p b t d", p=P)
                    for b in range(B):
                        sp.dma_start(X0[:, b * NT:b * NT + NT, :], xv[:, b]).then_inc(s_ld[b], 16)
                    for dst, src in ((CT, consts), (W0, wqkv0), (WP0, wproj0), (WF0, wff0), (ROWS, rows0), (W1q, wqkv1), (WO1, wo1)):
                        sp.dma_start(dst[:, :], src).then_inc(s_cst, 16)
                    sp.wait_ge(s_cst, 7 * 16)

                @block.gpsimd
                def _(pool):
                    pool.memset(QT[:, :, :], 0.0).then_inc(s_mem, 1)
                    pool.memset(KT[:, :, :], 0.0).then_inc(s_mem, 1)
                    pool.memset(MXS[:, :, :, :], 0.0).then_inc(s_mem, 1)
                    pool.memset(ONE[:, :], 1.0).then_inc(s_mem, 1)
                    pool.memset(V1[:, :, :, :], 0.0).then_inc(s_mem, 1)
                    pool.memset(V2[:, :, :, :], 0.0).then_inc(s_mem, 1)
                    for b in range(B):
                        pool.memset(XL[:, b, 0, :], 0.0).then_inc(s_mem, 1)
                    pool.wait_ge(s_mem, 6 + B)
                    pool.memset(KT[MROW:MROW + 3, :, :], 1.0).then_inc(s_mem, 1)
                    pool.wait_ge(s_mem, 7 + B)
                    pool.memset(V1[:, :, :, HV0:HV0 + 1], 1.0)
                    pool.memset(V2[:, :, :, HD:HD + 1], 1.0)

                normalise_rows(block, X0, names, sums, sqs, s_ld)

            with ExitStack() as c2:
                def sem(name):
                    return scoped(c2, name)

                s_lam = sem("lambda_chain")
                s_exp = sem("lambda_exp")
                block = phase(c2)

                @block.vector
                def _(dve):
                    dve.tensor_copy(identb[:, :], ident)
                    dve.tensor_copy(winb[:, :, :].rearrange("p a r -> p (a r)"), CT[:, C_WIN:C_ROT])
                    dve.tensor_copy(trib[:, :], CT[:, C_TRI:C_TRI + P])
                    dve.tensor_tensor(qa[:, 0:8], lamv[:, 0:8], lamv[:, 8:16], ALU.mult).then_inc(s_lam, 1)
                    dve.wait_ge(s_lam, 1)
                    dve.tensor_reduce(lam[:, 0:2], qa[:, 0:8].rearrange("p (a c) -> p a c", a=2), AX.X, ALU.add).then_inc(s_lam, 1)
                    dve.wait_ge(s_exp, 1)
                    dve.tensor_tensor(lam[:, 4:5], lam[:, 3:4], lam[:, 2:3], ALU.subtract).then_inc(s_lam, 1)
                    dve.wait_ge(s_lam, 3)
                    dve.tensor_scalar(lam[:, 5:6], lam[:, 4:5], -LAMBDA_INIT, None, ALU.add).then_inc(s_lam, 1)

                @block.scalar
                def _(act):
                    act.wait_ge(s_lam, 2)
                    act.activation(lam[:, 2:4], lam[:, 0:2], ACT.Exp).then_inc(s_exp, 1)

            nlam = lam[:, 5:6]

            def fake_quant(link, src, dst, nblk):
                n = nblk * 32
                v, a, bb = qa[:, 0:n], qb[:, 0:n], qc[:, 0:n]
                blk = lambda t: t.rearrange("p (n k) -> p n k", k=32)
                sc, rs = qs[:, 0, 0:nblk], qs[:, 1, 0:nblk]
                wide = lambda t: t.unsqueeze(2).to_broadcast([P, nblk, 32])
                e = nc.vector
                link(e.tensor_reduce(sc, blk(src), AX.X, ALU.max, apply_absolute_value=True))
                link(e.tensor_scalar(sc, sc, 1.0 / 7.5, 1e-30, ALU.mult, ALU.max))
                link(e.reciprocal(rs, sc))
                link(e.tensor_tensor(blk(v), blk(src), wide(rs), ALU.mult))
                link(e.tensor_tensor(a, v, v, ALU.mult))
                link(e.tensor_scalar(bb, a, 16.0, 0.25, ALU.is_ge, ALU.mult))
                link(e.tensor_scalar(a, a, 4.0, 0.125, ALU.is_ge, ALU.mult))
                link(e.scalar_tensor_tensor(out=a, in0=a, scalar=0.125, in1=bb, op0=ALU.add, op1=ALU.add))
                link(e.reciprocal(bb, a))
                link(e.tensor_tensor(v, v, bb, ALU.mult))
                link(e.tensor_scalar(v, v, -0.5, None, ALU.add))
                link(e.tensor_scalar(bb, v, MAGIC, None, ALU.add))
                link(e.tensor_scalar(bb, bb, -MAGIC, None, ALU.add))
                link(e.tensor_tensor(v, bb, v, ALU.is_lt))
                link(e.tensor_tensor(v, v, bb, ALU.add))
                link(e.tensor_tensor(v, v, a, ALU.mult))
                return e.tensor_tensor(blk(dst), blk(v), wide(sc), ALU.mult)
            NQ = 17

            with ExitStack() as c2:
                def sem(name):
                    return scoped(c2, name)

                s_ch, s_wt = sem("wquant_chain"), sem("wquant_transposed")
                block = phase(c2)

                @block.vector
                def _(dve):
                    n = [0]

                    def link(ins):
                        n[0] += 1
                        ins.then_inc(s_ch, 1)
                        dve.wait_ge(s_ch, n[0])

                    link(fake_quant(link, WF0[:, :], WF0[:, :], 4))
                    dve.wait_ge(s_wt, 1)
                    dve.tensor_copy(WFT[:, :], PS[:, 0, 0:P])

                @block.tensor
                def _(pe):
                    pe.wait_ge(s_ch, NQ)
                    pe.transpose(PS[:, 0, 0:P], WF0[:, :], ident).then_inc(s_wt, 1)

            def attention(first):
                with ExitStack() as c2:
                    def sem(name):
                        return scoped(c2, f"a{0 if first else 1}_{name}")

                    s_xs, s_xT, s_xTr, s_qkv = sem("xs"), sem("xT"), sem("xT_sbuf"), sem("qkv")
                    s_sq, s_spl, s_ch = sem("squares"), sem("parts"), sem("dve_chain")
                    s_qkp = sem("qk_repeated")
                    s_qt, s_qe, s_ke = sem("qk_transposed"), sem("qT_sbuf"), sem("kT_sbuf")
                    s_mp, s_mx, s_ms = sem("max_scores"), sem("max_taken"), sem("max_parts")
                    s_mt, s_me, s_mc = sem("max_transposed"), sem("max_sbuf"), sem("max_rows")
                    s_sc, s_ex, s_pv, s_pve = sem("scores"), sem("exps"), sem("values_summed"), sem("sums_sbuf")
                    s_yg, s_yn = sem("group_transposed"), sem("group_normal")
                    s_yt, s_ye, s_xd, s_xt, s_xe = sem("y_transposed"), sem("yT_sbuf"), sem("xd"), sem("xd_transposed"), sem("xdT_sbuf")
                    s_pr, s_bt = sem("projected"), sem("batch_done")
                    block = phase(c2)
                    wqkv_, wo_, bias_ = (W0, WP0, bias0) if first else (W1q, WO1, bias1)
                    hv = HV0 if first else HD
                    V = V1 if first else V2
                    scale = float(HD) ** -0.5
                    LAG = 0 if first else 1
                    STEPS = NG + LAG + 2
                    NC = 43 if first else 29

                    def keys(jt):
                        if not first:
                            return jt * T, 0
                        return (0, T, 2 * T, T + 3 * P)[jt], jt * P

                    @block.gpsimd
                    def _(pool):
                        pool.memset(spare[:, 0:1], 0.0).then_inc(s_xT, 1)
                        pool.memset(spare[:, 1:2], 0.0).then_inc(s_bt, 1)
                        with pool.Fori(0, B) as b:
                            pool.wait_ge(s_xT, b + 1)
                            pool.tensor_copy(xs[:, :, :], XL[:, b, 1:SLOTS, :]).then_inc(s_xs, 1)
                            if not first:
                                for g in range(NG):
                                    pool.wait_ge(s_me, b * NG + g + 1)
                                    for i in range(GH):
                                        pool.tensor_tensor(QT[MROW:MROW + 3, GH * g + i, :], MXT[PAD * i:PAD * i + 3, :],
                                                           ONE[PAD * i:PAD * i + 3, :], ALU.mult).then_inc(s_mc, 1)
                                pool.wait_ge(s_mc, (b + 1) * H)

                    @block.tensor
                    def _(pe):
                        with pe.Fori(0, B) as b:
                            pe.wait_ge(s_xs, b + 1)
                            pe.wait_ge(s_bt, b + 1)
                            for t in range(NT):
                                ins = pe.transpose(PS[:, 0, t * P:t * P + P], xs[:, t, :], ident)
                            ins.then_inc(s_xT, 1)
                            pe.wait_ge(s_xTr, b + 1)
                            for t in range(NT):
                                ins = pe.matmul(PS[:, t, 0:3 * D], xT[:, t * P:t * P + P], wqkv_[:, :], start=True, stop=True)
                            ins.then_inc(s_qkv, 1)
                            pe.wait_ge(s_qkp, b + 1)
                            for i in range(H // 2):
                                if i >= 2:
                                    pe.wait_ge(s_qe, b * (H // 2) + i - 1)
                                    pe.wait_ge(s_ke, b * (H // 2) + i - 1)
                                for a in range(2):
                                    for j in range(2):
                                        h = 2 * i + j
                                        for t in range(NT):
                                            ins = pe.matmul(PS[0:KS, 4 * (i % 2) + 2 * a + j, t * P:t * P + P],
                                                            PK[:, a, t * H + h, :], identb[:, :], start=True, stop=True)
                                    ins.then_inc(s_qt, 1)
                            pe.wait_ge(s_qe, (b + 1) * (H // 2))
                            pe.wait_ge(s_ke, (b + 1) * (H // 2))

                            def maxima(h, it):
                                m = NT * h + it
                                if m >= 2:
                                    pe.wait_ge(s_mx, b * H * NT + m - 1)
                                pe.matmul(PS[:, m % 2, :], QT[0:KS, h, it * P:it * P + P], KT[0:KS, h, :],
                                          start=True, stop=True).then_inc(s_mp, 1)

                            def scores(h, part):
                                if first:
                                    if h >= 2:
                                        pe.wait_ge(s_ex, b * H + h - 1)
                                    base = 3 * (h % 2)
                                    for jt in range(NT):
                                        n = T - jt * P
                                        o = PS[:, base + (0, 1, 2, 1)[jt], (0, 0, 0, 3 * P)[jt]:]
                                        pe.matmul(o[:, 0:n], KT[0:KS, h, jt * P:jt * P + P], QT[0:KS, h, jt * P:T], start=True, stop=False)
                                        ins = pe.matmul(o[:, 0:P], identb[:, :], trib[:, :], start=False, stop=True)
                                    ins.then_inc(s_sc, 1)
                                else:
                                    if part == 0:
                                        pe.wait_ge(s_mc, b * H + h + 1)
                                    m = 2 * h + part
                                    if m >= 2:
                                        pe.wait_ge(s_ex, b * 2 * H + m - 1)
                                    for i in range(2):
                                        jt = 2 * part + i
                                        ins = pe.matmul(PS[:, 2 + 2 * (m % 2) + i, :], KT[:, h, jt * P:jt * P + P], QT[:, h, :],
                                                        start=True, stop=True)
                                    ins.then_inc(s_sc, 1)

                            def values(g, jt):
                                if jt == 0:
                                    pe.wait_ge(s_ex, (b * H + GH * (g + 1)) * (1 if first else 2))
                                    if g:
                                        pe.wait_ge(s_pve, b * NG + g)
                                for i in range(GH):
                                    h = GH * g + i
                                    at, q0 = keys(jt)
                                    ins = pe.matmul(PS[PAD * i:PAD * i + PAD, 6, q0:T], V[:, jt, h % NV0 if first else h, :],
                                                    PT[:, h % PTN, at:at + T - q0], start=(jt == 0), stop=(jt == NT - 1),
                                                    skip_group_check=True)
                                if jt == NT - 1:
                                    ins.then_inc(s_pv, 1)

                            for st in range(STEPS):
                                gm, ge, gv, gy = st, st - LAG, st - LAG - 1, st - LAG - 2
                                if LAG and 0 <= gm - 1 < NG:
                                    pe.wait_ge(s_ms, b * NG + gm)
                                    if gy - 1 >= 0:
                                        pe.wait_ge(s_yn, b * NG + gy)
                                    for t in range(NT):
                                        ins = pe.matmul(PS[:, 7, t * P:t * P + P], MXS[:, t, :, :].rearrange("p h k -> p (h k)"), identb[:, :],
                                                        start=True, stop=True)
                                    ins.then_inc(s_mt, 1)
                                for k in range(GH):
                                    if LAG and gm < NG:
                                        maxima(GH * gm + k, 0)
                                        maxima(GH * gm + k, 1)
                                    if k == 0 and 0 <= gy < NG:
                                        pe.wait_ge(s_pve, b * NG + gy + 1)
                                        if LAG and gm - 1 < NG:
                                            pe.wait_ge(s_me, b * NG + gm)
                                        elif gy:
                                            pe.wait_ge(s_yn, b * NG + gy)
                                        for t in range(NT):
                                            ins = pe.transpose(PS[:, 7, t * P:t * P + P], OT[:, t * P:t * P + P], ident)
                                        ins.then_inc(s_yg, 1)
                                    if 0 <= ge < NG:
                                        scores(GH * ge + k, 0)
                                    if LAG and gm < NG:
                                        maxima(GH * gm + k, 2)
                                    if LAG and 0 <= ge < NG:
                                        scores(GH * ge + k, 1)
                                    if LAG and gm < NG:
                                        maxima(GH * gm + k, 3)
                                    if 0 <= gv < NG:
                                        values(gv, k)
                            if first:
                                pe.wait_ge(s_xd, b + 1)
                                for t in range(NT):
                                    ins = pe.transpose(PS[:, 1, t * P:t * P + P], xd[:, t, :], ident)
                                ins.then_inc(s_xt, 1)
                            pe.wait_ge(s_yn, (b + 1) * NG)
                            for t in range(NT):
                                ins = pe.transpose(PS[:, 0, t * P:t * P + P], Y[:, t, :], ident)
                            ins.then_inc(s_yt, 1)
                            pe.wait_ge(s_ye, b + 1)
                            if first:
                                pe.wait_ge(s_xe, b + 1)
                            for t in range(NT):
                                o = PS[:, 2, t * P:t * P + P]
                                if first:
                                    pe.matmul(o, xdT[:, t * P:t * P + P], WFT[:, :], start=True, stop=False)
                                ins = pe.matmul(o, YT[:, t * P:t * P + P], wo_[:, :], start=not first, stop=True)
                            ins.then_inc(s_pr, 1)

                    @block.scalar
                    def _(act):
                        with act.Fori(0, B) as b:
                            act.wait_ge(s_xT, b + 2)
                            act.activation(xT[:, :], PS[:, 0, :], ACT.Copy).then_inc(s_xTr, 1)
                            if first:
                                act.wait_ge(s_qkv, b + 1)
                                act.activation(sq[:, :, :], PS[:, 0:NT, 0:2 * D], ACT.Square).then_inc(s_sq, 1)
                            for i in range(H // 2):
                                act.wait_ge(s_qt, b * H + 2 * i + 1)
                                b0 = 4 * (i % 2)
                                act.activation(QT[0:KS, 2 * i:2 * i + 2, :], PS[0:KS, b0:b0 + 2, :], ACT.Copy).then_inc(s_qe, 1)

                            def sums_out(g):
                                act.wait_ge(s_pv, b * NG + g + 1)
                                if g:
                                    act.wait_ge(s_yg, b * NG + g)
                                act.activation(OT[:, :], PS[:, 6, :], ACT.Copy).then_inc(s_pve, 1)

                            for st in range(STEPS):
                                gm, ge = st - 1, st - LAG
                                if LAG and 0 <= gm < NG:
                                    act.wait_ge(s_mt, b * NG + gm + 1)
                                    if gm:
                                        act.wait_ge(s_mc, b * H + GH * gm)
                                    act.activation(MXT[:, :], PS[:, 7, :], ACT.Copy).then_inc(s_me, 1)
                                if 0 <= ge < NG:
                                    for k in range(GH):
                                        h = GH * ge + k
                                        if ge >= 2 and k == 0:
                                            act.wait_ge(s_pv, b * NG + ge - 1)
                                        if first:
                                            act.wait_ge(s_sc, b * H + h + 1)
                                            n = 10 * P
                                            act.activation(PT[:, h % PTN, 0:n],
                                                           PS[:, 3 * (h % 2):3 * (h % 2) + 3, :].rearrange("p k n -> p (k n)")[:, 0:n],
                                                           ACT.Exp, scale=scale).then_inc(s_ex, 1)
                                        else:
                                            for a in range(2):
                                                m = 2 * h + a
                                                act.wait_ge(s_sc, b * 2 * H + m + 1)
                                                act.activation(PT[:, h % PTN, a * 2 * T:(a + 1) * 2 * T],
                                                               PS[:, 2 + 2 * (m % 2):4 + 2 * (m % 2), :].rearrange("p k n -> p (k n)"),
                                                               ACT.Exp, scale=scale).then_inc(s_ex, 1)
                                if 0 <= ge - 1 < NG:
                                    sums_out(ge - 1)
                            if first:
                                act.wait_ge(s_xt, b + 1)
                                act.activation(xdT[:, :], PS[:, 1, :], ACT.Copy).then_inc(s_xe, 1)
                            act.wait_ge(s_yt, b + 1)
                            act.activation(YT[:, :], PS[:, 0, :], ACT.Copy).then_inc(s_ye, 1)

                    @block.vector
                    def _(dve):
                        with dve.Fori(0, B) as b:
                            n = [0]

                            def link(ins):
                                n[0] += 1
                                ins.then_inc(s_ch, 1)
                                dve.wait_ge(s_ch, b * NC + n[0])

                            def parts(src, rest, to):
                                for i in range(3):
                                    for k, r in enumerate(rest):
                                        ins = nc.vector.tensor_copy(to(i, k), r if i else src[k])
                                    if i < 2:
                                        link(ins)
                                        for k, r in enumerate(rest):
                                            ins = nc.vector.tensor_tensor(r, r if i else src[k], to(i, k), ALU.subtract)
                                        link(ins)
                                return ins

                            dve.wait_ge(s_qkv, b + 1)
                            qk = PS[:, 0:NT, 0:2 * D].rearrange("p t (h e) -> p t h e", e=HD)
                            v = PS[:, 0:NT, 2 * D:3 * D].rearrange("p t (h e) -> p t h e", e=hv)
                            split = lambda i, a: SP[:, a, :, :, i, :]
                            if first:
                                dve.wait_ge(s_sq, b + 1)
                            for t in range(NT):
                                nc.vector.tensor_copy(V[:, t, :, 0:hv], v[:, t])
                            q4 = qn[:, :, :].rearrange("p t (h e) -> p t h e", e=HD)
                            if first:
                                link(nc.vector.tensor_reduce(rms[:, 0, :, :], sq[:, :, :].rearrange("p t (h e) -> p t h e", e=HD), AX.X, ALU.add))
                                link(nc.vector.tensor_scalar(rms[:, 0, :, :], rms[:, 0, :, :], 1.0 / HD, float(np.finfo(np.float32).eps),
                                                             ALU.mult, ALU.add))
                                rsqrt(link, rms[:, 1, :, :], rms[:, 0, :, :], rms[:, 2, :, :])
                                link(nc.vector.tensor_tensor(q4, qk, rms[:, 1, :, :].unsqueeze(3).to_broadcast([P, NT, 2 * H, HD]), ALU.mult))
                                rot = CT[:, C_ROT:C_XP].rearrange("p (a t e) -> p a t e", a=2, t=NT)
                                a4 = ra[:, :, :].rearrange("p t (h e) -> p t h e", e=HD)
                                half = HD // 2
                                wide = lambda z, e: z.unsqueeze(2).to_broadcast([P, NT, 2 * H, e])
                                nc.vector.tensor_tensor(a4[:, :, :, 0:half], q4[:, :, :, half:HD], wide(rot[:, 1, :, 0:half], half), ALU.mult)
                                link(nc.vector.tensor_tensor(a4[:, :, :, half:HD], q4[:, :, :, 0:half], wide(rot[:, 1, :, half:HD], half), ALU.mult))
                                link(nc.vector.tensor_tensor(q4, q4, wide(rot[:, 0, :, :], HD), ALU.mult))
                                link(nc.vector.tensor_tensor(q4, q4, a4, ALU.add))
                            both = lambda z: [z[:, :, a * H:(a + 1) * H, :] for a in range(2)]
                            parts(both(q4 if first else qk), both(q4), split).then_inc(s_spl, 1)
                            dve.wait_ge(s_spl, b + 1)
                            nc.vector.tensor_copy(PK[:, 0].rearrange("p n (r k) -> p n r k", r=3),
                                                  SP[:, 0].rearrange("p t h c e -> p (t h) (c e)").unsqueeze(2).to_broadcast([P, NT * H, 3, 3 * HD]))
                            for c in range(3):
                                ins = nc.vector.tensor_copy(PK[:, 1, :, 3 * HD * c:3 * HD * (c + 1)].rearrange("p n (r e) -> p n r e", r=3),
                                                            SP[:, 1, :, :, c, :].rearrange("p t h e -> p (t h) e").unsqueeze(2)
                                                            .to_broadcast([P, NT * H, 3, HD]))
                            ins.then_inc(s_qkp, 1)
                            for i in range(H // 2):
                                dve.wait_ge(s_qt, b * H + 2 * i + 2)
                                b0 = 4 * (i % 2) + 2
                                nc.vector.tensor_copy(KT[0:KS, 2 * i:2 * i + 2, :], PS[0:KS, b0:b0 + 2, :]).then_inc(s_ke, 1)
                            if first:
                                fake_quant(link, XL[:, b, 1:SLOTS, :].rearrange("p t d -> p (t d)"),
                                           xd[:, :, :].rearrange("p t d -> p (t d)"), 16).then_inc(s_xd, 1)

                            def outputs(g):
                                dve.wait_ge(s_yg, b * NG + g + 1)
                                o = PS[:, 7, :].rearrange("p (t h e) -> p t h e", t=NT, h=GH)
                                den, rc = o[:, :, :, hv], rec[:, g % 2, :, :]
                                if not first:
                                    link(nc.vector.tensor_scalar(rc, den, 1e-8, None, ALU.add))
                                    den = rc
                                link(nc.vector.reciprocal(rc, den))
                                h0 = GH * g if not first else GH * (g % 2)
                                yo = Y[:, :, h0 * hv:(h0 + GH) * hv].rearrange("p t (h e) -> p t h e", e=hv)
                                rw = rc.unsqueeze(3).to_broadcast([P, NT, GH, hv])
                                if first and g >= 2:
                                    link(nc.vector.tensor_tensor(yt[:, :, :, :], o[:, :, :, 0:hv], rw, ALU.mult))
                                    ins = nc.vector.scalar_tensor_tensor(out=yo, in0=yt[:, :, :, :], scalar=nlam, in1=yo,
                                                                         op0=ALU.mult, op1=ALU.add)
                                else:
                                    ins = nc.vector.tensor_tensor(yo, o[:, :, :, 0:hv], rw, ALU.mult)
                                ins.then_inc(s_yn, 1)

                            for st in range(STEPS):
                                gm, gy = st, st - LAG - 2
                                for k in range(GH):
                                    if LAG and gm < NG:
                                        h = GH * gm + k
                                        for it in range(NT):
                                            m = NT * h + it
                                            dve.wait_ge(s_mp, b * H * NT + m + 1)
                                            nc.vector.tensor_reduce(mxs[:, it, k:k + 1], PS[:, m % 2, :], AX.X, ALU.max, negate=True).then_inc(s_mx, 1)
                                    if k == 1 and 0 <= gy < NG:
                                        outputs(gy)
                                if LAG and gm < NG:
                                    dve.wait_ge(s_mx, (b * H + GH * (gm + 1)) * NT)
                                    if gm:
                                        dve.wait_ge(s_mt, b * NG + gm)
                                    parts([mxs[:, :, :]], [mxs[:, :, :]], lambda i, k: MXS[:, :, :, i]).then_inc(s_ms, 1)
                                    dve.wait_ge(s_ms, b * NG + gm + 1)
                            src = X0 if first else X1
                            dve.wait_ge(s_pr, b + 1)
                            pr = qn[:, 0:2, :].rearrange("p a (t d) -> p (a t) d", d=D)
                            link(nc.vector.tensor_tensor(pr, PS[:, 2, :].rearrange("p (t d) -> p t d", d=D),
                                                         bias_.unsqueeze(1).to_broadcast([P, NT, D]), ALU.add))
                            tiles = lambda z: z[:, :, :].rearrange("p (b t) d -> p b t d", b=B)[:, b]
                            nc.vector.tensor_tensor(tiles(X1), tiles(src), pr, ALU.add).then_inc(s_bt, 1)
                            assert n[0] == NC, n[0]

            attention(True)

            with ExitStack() as c2:
                def sem(name):
                    return scoped(c2, name)

                names = [sem(n) for n in ("ln1_sum", "ln1_centred", "ln1_sq", "ln1_chain")]
                block = phase(c2)
                normalise_rows(block, X1, names, sums, sqs)

            attention(False)

        with ExitStack() as ctx:
            WQ = sb("WQ", [P, 3 * INNER], F32, ctx)
            WO = sb("WO", [P, INNER // P, D], F32, ctx)
            QK = sb("QK", [P, 2, DH], F32, ctx)
            WA = sb("WA", [P, 2 * DI], F32, ctx)
            WB = sb("WB", [P, DCH, D], F32, ctx)
            COL = sb("COL", [P, 2 + 2 * DCH], F32, ctx)
            B2 = sb("B2", [P, D], F32, ctx)
            TC = sb("TC", [P, NT, 2, DH], F32, ctx)
            TS = sb("TS", [P, NT, 2, DH], F32, ctx)

            def two(name, shape):
                return [sb(f"{name}{s}", shape, F32, ctx) for s in range(2)]

            xs = two("ls_xs", [P, NT, D])
            xsT = two("ls_xsT", [P, WIN + T])
            Q = two("ls_q", [P, 2 * INNER])
            A = two("ls_a", [P, 2 * INNER])
            R = two("ls_r", [P, 2 * INNER])
            qT = two("ls_qT", [P, H, P])
            kT = two("ls_kT", [P, 2, H // 2, WIN + P])
            VB = two("ls_vb", [P, NW, H // 2, 2 * (DH + 1)])
            Y = [a[:, 0:INNER] for a in A]
            YT = [a[:, INNER:].rearrange("p (i n) -> p i n", n=P) for a in A]
            ss = two("ls_ss", [P, 2 * H])
            rn = two("ls_rn", [P, 2, 2 * H])
            mx = two("ls_mx", [P, H])
            rc = two("ls_rc", [P, H])
            fs = sb("ls_fs", [P, 4, 2, NT], F32, ctx)

            def sem(name):
                return scoped(ctx, name)

            def sems(name):
                return [scoped(ctx, f"{name}{s}") for s in range(2)]

            w_attn, w_ffn = sem("attn_weights"), sem("ffn_weights")
            free_attn, free_ffn = sem("attn_weights_free"), sem("ffn_weights_free")
            s_tab, s_zero = sem("tables"), sem("zeros")
            s_xl, s_xm = sems("stream_new"), sems("stream_mid")
            s_sh, s_xu, s_xlo, s_xt, s_xe = sems("shifted"), sems("xs_upper"), sems("xs_lower"), sems("xs_transposed"), sems("xsT_sbuf")
            s_qk, s_sq, s_qn = sems("qk"), sems("squares_qk"), sems("qk_normal")
            s_v, s_ve, s_a, s_rot = sems("v"), sems("v_sbuf"), sems("cos_term"), sems("rotated")
            s_kt, s_ke, s_qt, s_qe = sems("lk_transposed"), sems("lkT_sbuf"), sems("lq_transposed"), sems("lqT_sbuf")
            s_so, s_sub, s_p, s_pt, s_pte = sems("local_scores"), sems("less_max"), sems("local_exp"), sems("expT"), sems("expT_sbuf")
            s_o, s_yn, s_yt, s_ye, s_w = sems("weighted"), sems("out_normal"), sems("out_T"), sems("outT_sbuf"), sems("attn_out")
            f_sh, f_xu, f_c, f_sq, f_xn = (sems("f_" + n) for n in ("shifted", "xs_upper", "centred", "squares", "normal"))
            f_xt, f_xe, f_g, f_ge, f_a, f_u, f_w, f_rb = (sems("f_" + n) for n in (
                "transposed", "xnT_sbuf", "gate", "gelu", "linear", "product", "out", "residual"))
            ch = sems("vector_chain")
            FRONT, BACK = 5 + NRS, 3
            NA, NF = NT * (FRONT + BACK), 8 + NRS
            NB = [PAIRS * (NA + NF), PAIRS * NA]
            block = phase(ctx)

            def half_steps(eng, begin, slot):
                begin((0, 0))
                slot((0, 0, 0), None, (1, 0))
                with eng.Fori(0, PAIRS - 1) as p:
                    for u in range(1, 2 * NT + 1):
                        slot((u % 2, u // 2, p) if u < 2 * NT else (0, 0, p + 1), ((u - 1) % 2, (u - 1) // 2, p),
                             {2 * NT - 1: (0, p + 1), 2 * NT: (1, p + 1)}.get(u))
                for u in range(1, 2 * NT + 1):
                    slot((u % 2, u // 2, PAIRS - 1) if u < 2 * NT else None, ((u - 1) % 2, (u - 1) // 2, PAIRS - 1), None)

            def ahead(eng, ready, layer):
                ready(0)
                with eng.Fori(0, PAIRS - 1) as p:
                    layer(p, True)
                layer(PAIRS - 1, False)

            def bank(s, i, n=1):
                v = PS[:, 4 * s + i:4 * s + i + n, :]
                return v.rearrange("p b n -> p (b n)")

            @block.sync
            def _(sp):
                with sp.Fori(0, DEPTH) as l:
                    sp.wait_ge(free_attn, l + 1)
                    sp.dma_start(WQ[:, :], wqkv[l]).then_inc(w_attn, 16)
                    sp.dma_start(WO[:, :, :], wo[l]).then_inc(w_attn, 16)
                    sp.dma_start(QK[:, :, :], qkscale[l].rearrange("p (a e) -> p a e", a=2)).then_inc(w_attn, 16)
                    sp.wait_ge(free_ffn, l + 1)
                    sp.dma_start(WA[:, :], w1[l]).then_inc(w_ffn, 16)
                    sp.dma_start(WB[:, :, :], w2[l]).then_inc(w_ffn, 16)
                    sp.dma_start(COL[:, :], cols[l]).then_inc(w_ffn, 16)
                    sp.dma_start(B2[:, :], b2[l]).then_inc(w_ffn, 16)
                sp.wait_ge(w_ffn, DEPTH * 64)

            @block.gpsimd
            def _(pool):
                pool.memset(spare[:, 0:1], 0.0).then_inc(free_attn, 1)
                pool.memset(spare[:, 1:2], 0.0).then_inc(free_ffn, 1)
                for s in range(2):
                    for i in range(PAIRS):
                        pool.memset(ss[s][:, i:i + 1], 0.0).then_inc(s_xl[s], 1)
                    pool.memset(qT[s][:, :, :], 0.0)
                    pool.memset(xsT[s][:, 0:WIN], 0.0)
                    pool.memset(kT[s][:, 0, :, 0:WIN], 0.0)
                    pool.memset(VB[s][:, :, :, :], 0.0).then_inc(s_zero, 1)
                pool.wait_ge(s_zero, 2)
                for s in range(2):
                    for a in range(2):
                        pool.memset(VB[s][a * DH:a * DH + DH, :, :, a * (DH + 1) + DH:a * (DH + 1) + DH + 1], 1.0).then_inc(s_zero, 1)
                        pool.wait_ge(s_zero, 3 + 2 * s + a)
                    pool.memset(ss[s][:, 0:1], 0.0).then_inc(s_xm[s], 1)
                    pool.memset(ss[s][:, 1:2], 0.0).then_inc(f_xt[s], 1)
                with pool.Fori(0, DEPTH) as l:
                    pool.wait_ge(s_xl[0], (l + 1) * PAIRS)
                    pool.wait_ge(s_xl[1], (l + 1) * PAIRS)
                    pool.wait_ge(w_attn, l * 48 + 48)
                    base = CT[:, C_XP:C_ALL].rearrange("p (k t e) -> p k t e", k=4, t=NT)
                    h2 = DH // 2
                    for a in range(2):
                        wide = lambda z, e: z.unsqueeze(1).to_broadcast([P, NT, e])
                        pool.tensor_tensor(TC[:, :, a, :], base[:, 2 * a], wide(QK[:, a, :], DH), ALU.mult)
                        pool.tensor_tensor(TS[:, :, a, 0:h2], base[:, 2 * a + 1, :, 0:h2], wide(QK[:, a, h2:DH], h2), ALU.mult)
                        ins = pool.tensor_tensor(TS[:, :, a, h2:DH], base[:, 2 * a + 1, :, h2:DH], wide(QK[:, a, 0:h2], h2), ALU.mult)
                    ins.then_inc(s_tab, 1)
                    def lower(prep):
                        s, p = prep
                        pool.tensor_copy(xs[s][:, :, 0:D // 2], XL[:, p + s * PAIRS, 1:SLOTS, 0:D // 2]).then_inc(s_xlo[s], 1)

                    v4 = lambda z: z[:, :].rearrange("p (a h e) -> p a h e", a=2, h=H)

                    def slot(front, back, prep):
                        if prep:
                            lower(prep)
                        if front:
                            s, t, p = front
                            n = (l * PAIRS + p) * NT + t + 1
                            if t == 0 and s == 0:
                                pool.wait_ge(s_tab, l + 1)
                            for i, a in enumerate((1, 0)):
                                tab = TC[:, t, a, :].unsqueeze(1).to_broadcast([P, H, DH])
                                pool.wait_ge(s_qn[s], 2 * n - 1 + i)
                                pool.tensor_tensor(v4(A[s])[:, a], v4(Q[s])[:, a], tab, ALU.mult).then_inc(s_a[s], 1)

                    half_steps(pool, lower, slot)
                    with pool.Fori(0, PAIRS) as p:
                        m = l * PAIRS + p + 1
                        pool.wait_ge(w_ffn, l * 64 + 64)
                        for s in range(2):
                            pool.wait_ge(s_xm[s], (l + 1) * PAIRS * NT + 1)
                            pool.wait_ge(s_xl[s], m + PAIRS - 1)
                            pool.tensor_tensor(R[s][:, T:2 * T].rearrange("p (t d) -> p t d", t=NT), XL[:, p + s * PAIRS, 1:SLOTS, :],
                                               B2[:, :].unsqueeze(1).to_broadcast([P, NT, D]), ALU.add).then_inc(f_rb[s], 1)

            @block.tensor
            def _(pe):
                def shift(s, at, b, done):
                    src = XL
                    o = bank(s, at)[:, 0:NT * D // 2]
                    pe.matmul(o, CT[:, C_SH:C_SH + P], src[:, b, 1:SLOTS, D // 2:D], start=True, stop=False)
                    pe.matmul(o, CT[:, C_ED:C_ED + P], src[:, b, 0:NT, D // 2:D], start=False, stop=True).then_inc(done, 1)

                with pe.Fori(0, DEPTH) as l:
                    def rows_up(prep):
                        s, p = prep
                        pe.wait_ge(s_xu[s], l * PAIRS + p + 1)
                        pe.wait_ge(s_xlo[s], l * PAIRS + p + 1)
                        for t in range(NT):
                            ins = pe.transpose(bank(s, 3)[:, t * P:t * P + P], xs[s][:, t, :], ident)
                        ins.then_inc(s_xt[s], 1)

                    def begin(prep):
                        pe.wait_ge(s_xl[0], (l + 1) * PAIRS)
                        pe.wait_ge(s_xl[1], (l + 1) * PAIRS)
                        shift(prep[0], 3, prep[1] + prep[0] * PAIRS, s_sh[prep[0]])
                        rows_up(prep)

                    def slot(front, back, prep):
                        if front:
                            s, t, p = front
                            n = (l * PAIRS + p) * NT + t + 1
                            if t == 0:
                                pe.wait_ge(s_xe[s], l * PAIRS + p + 1)
                                pe.wait_ge(w_attn, l * 48 + 48)
                            pe.wait_ge(s_xm[s], n)
                            rows = xsT[s][:, WIN + t * P:WIN + t * P + P]
                            for c in range(4):
                                ins = pe.matmul(bank(s, c), rows, WQ[:, c * 512:c * 512 + 512], start=True, stop=True)
                                if c % 2:
                                    ins.then_inc(s_qk[s], 1)
                        if back:
                            s, t, p = back
                            n = (l * PAIRS + p) * NT + t + 1
                            pe.wait_ge(s_ke[s], n)
                            pe.wait_ge(s_qe[s], 2 * n)
                            for c in range(2):
                                pe.matmul(bank(s, c), identb[:, :], winb[:, 0 if t else 1, :].unsqueeze(1).to_broadcast([P, H // 2, 2 * WIN]),
                                          start=True, stop=False)
                                for h in range(c * H // 2, (c + 1) * H // 2):
                                    for w in range(NW):
                                        at = (h % (H // 2)) * 2 * WIN
                                        ins = pe.matmul(bank(s, c)[WIN * w:WIN * w + WIN, at:at + 2 * WIN], qT[s][:, h, WIN * w:WIN * w + WIN],
                                                        kT[s][:, t % 2, h // 2, WIN * w:WIN * w + 2 * WIN],
                                                        start=False, stop=(h % (H // 2) == H // 2 - 1))
                                ins.then_inc(s_so[s], 1)
                            for c in range(2):
                                pe.wait_ge(s_p[s], 2 * n - 1 + c)
                                for i in range(4):
                                    at = c * 4 * P + i * P
                                    ins = pe.transpose(bank(s, 2 + c)[:, i * P:i * P + P], Q[s][:, at:at + P], ident)
                                ins.then_inc(s_pt[s], 1)
                            for i in range(H // 2):
                                if i in (0, 4):
                                    pe.wait_ge(s_pte[s], 2 * n - 1 + i // 4)
                                for w in range(NW):
                                    at = (i % 3) * 2 * (DH + 1)
                                    ins = pe.matmul(bank(s, i // 3)[WIN * w:WIN * w + WIN, at:at + 2 * (DH + 1)],
                                                    R[s][:, i * P + WIN * w:i * P + WIN * w + WIN], VB[s][:, w, i, :], start=True, stop=True)
                            ins.then_inc(s_o[s], 1)
                        def values(c):
                            s, t, p = front
                            n = (l * PAIRS + p) * NT + t + 1
                            pe.wait_ge(s_qn[s], 2 * n - 1 + c)
                            for w in (2 * c, 2 * c + 1):
                                rows = xsT[s][:, t * P + WIN * w:t * P + WIN * w + 2 * WIN]
                                for a in range(2):
                                    wv = WQ[:, 2 * INNER:].rearrange("p (i a e) -> p a i e", a=2, e=DH)[:, a]
                                    ins = pe.matmul(bank(s, 2 - 2 * c + w % 2)[a * DH:a * DH + DH, :], rows, wv, start=True, stop=True)
                            ins.then_inc(s_v[s], 1)

                        if prep:
                            shift(prep[0], 3, prep[1] + prep[0] * PAIRS, s_sh[prep[0]])
                        if front:
                            values(0)
                        if back:
                            s, t, p = back
                            n = (l * PAIRS + p) * NT + t + 1
                            pe.wait_ge(s_yn[s], n)
                            for i in range(INNER // P):
                                ins = pe.transpose(bank(s, 0, 2)[:, i * P:i * P + P], Y[s][:, i * P:i * P + P], ident)
                            ins.then_inc(s_yt[s], 1)
                        if front:
                            values(1)
                        if prep:
                            rows_up(prep)
                        if back:
                            s, t, p = back
                            n = (l * PAIRS + p) * NT + t + 1
                            pe.wait_ge(s_ye[s], n)
                            for i in range(INNER // P):
                                ins = pe.matmul(bank(s, 2)[:, 0:D], YT[s][:, i, :], WO[:, i, :], start=(i == 0), stop=(i == INNER // P - 1))
                            ins.then_inc(s_w[s], 1)
                        if front:
                            s, t, p = front
                            n = (l * PAIRS + p) * NT + t + 1
                            for a, done in ((1, s_kt), (0, s_qt)):
                                pe.wait_ge(s_rot[s], 2 * n - a)
                                pe.wait_ge(s_ve[s], 2 * n - a)
                                for i in range(H // 2):
                                    at = a * INNER + i * P
                                    ins = pe.transpose(bank(s, 2 * a, 2)[:, i * P:i * P + P], A[s][:, at:at + P], ident)
                                ins.then_inc(done[s], 1)

                    half_steps(pe, begin, slot)

                    def ready(p):
                        for s in range(2):
                            pe.wait_ge(s_xm[s], (l + 1) * PAIRS * NT + 1)
                            pe.wait_ge(s_xl[s], l * PAIRS + p + PAIRS - 1)
                            shift(s, 0, p + s * PAIRS, f_sh[s])

                    def layer(p, more):
                        m = l * PAIRS + p + 1
                        for s in range(2):
                            pe.wait_ge(f_xn[s], m)
                            for t in range(NT):
                                ins = pe.transpose(bank(s, 1)[:, t * P:t * P + P], xs[s][:, t, :], ident)
                            ins.then_inc(f_xt[s], 1)
                        for part, done, after in ((1, f_g, f_xe), (0, f_a, f_ge)):
                            for s in range(2):
                                if part and s == 0:
                                    pe.wait_ge(w_ffn, l * 64 + 64)
                                pe.wait_ge(after[s], m)
                                for c in range(DCH):
                                    k = P if c < DCH - 1 else DLAST
                                    at = part * DI + c * P
                                    ins = pe.matmul(bank(s, 1 + c)[0:k], WA[:, at:at + k], xsT[s][:, WIN:], start=True, stop=True)
                                ins.then_inc(done[s], 1)
                            if part and more:
                                ready(p + 1)
                        for s in range(2):
                            pe.wait_ge(f_u[s], m)
                            if more:
                                pe.wait_ge(f_xu[s], m + 1)
                            for t in range(NT):
                                for c in range(DCH):
                                    k = P if c < DCH - 1 else DLAST
                                    ins = pe.matmul(bank(s, 0)[:, t * P:t * P + P], A[s][0:k, c * T + t * P:c * T + t * P + P], WB[0:k, c, :],
                                                    start=(c == 0), stop=(c == DCH - 1))
                            ins.then_inc(f_w[s], 1)

                    ahead(pe, ready, layer)

            @block.scalar
            def _(act):
                with act.Fori(0, DEPTH) as l:
                    def upper(prep):
                        s, p = prep
                        act.wait_ge(s_sh[s], l * PAIRS + p + 1)
                        act.activation(xs[s][:, :, D // 2:D], bank(s, 3)[:, 0:NT * D // 2].rearrange("p (t d) -> p t d", t=NT), ACT.Copy).then_inc(s_xu[s], 1)

                    def rows_sbuf(prep):
                        s, p = prep
                        act.wait_ge(s_xt[s], l * PAIRS + p + 1)
                        act.activation(xsT[s][:, WIN:], bank(s, 3), ACT.Copy).then_inc(s_xe[s], 1)

                    def begin(prep):
                        upper(prep)
                        rows_sbuf(prep)

                    def slot(front, back, prep):
                        if front:
                            s, t, p = front
                            n = (l * PAIRS + p) * NT + t + 1
                            for c in range(2):
                                act.wait_ge(s_qk[s], 2 * n - 1 + c)
                                act.activation(R[s][:, c * INNER:(c + 1) * INNER], bank(s, 2 * c, 2), ACT.Square).then_inc(s_sq[s], 1)
                        if back:
                            s, t, p = back
                            n = (l * PAIRS + p) * NT + t + 1
                            for c in range(2):
                                half = Q[s][:, c * T:c * T + T]
                                act.wait_ge(s_sub[s], 2 * n - 1 + c)
                                act.activation(half, half, ACT.Exp).then_inc(s_p[s], 1)
                            for c in range(2):
                                act.wait_ge(s_pt[s], 2 * n - 1 + c)
                                act.activation(R[s][:, c * T:c * T + T], bank(s, 2 + c), ACT.Copy).then_inc(s_pte[s], 1)
                        if prep:
                            upper(prep)
                        if front:
                            s, t, p = front
                            n = (l * PAIRS + p) * NT + t + 1
                            for c in range(2):
                                act.wait_ge(s_v[s], 2 * n - 1 + c)
                                for a in range(2):
                                    ins = act.activation(VB[s][a * DH:a * DH + DH, 2 * c:2 * c + 2, :, a * (DH + 1):a * (DH + 1) + DH],
                                                         bank(s, 2 - 2 * c, 2)[a * DH:a * DH + DH].rearrange("p (w i e) -> p w i e", w=2, e=DH), ACT.Copy)
                                ins.then_inc(s_ve[s], 1)
                        if prep:
                            rows_sbuf(prep)
                        if front:
                            s, t, p = front
                            n = (l * PAIRS + p) * NT + t + 1
                            act.wait_ge(s_kt[s], n)
                            k_ = bank(s, 2, 2).rearrange("p (i n) -> p i n", n=P)
                            ins = act.activation(kT[s][:, t % 2, :, WIN:], k_, ACT.Copy)
                            if t < NT - 1:
                                ins = act.activation(kT[s][:, 1 - t % 2, :, 0:WIN], k_[:, :, P - WIN:P], ACT.Copy)
                            ins.then_inc(s_ke[s], 1)
                            act.wait_ge(s_qt[s], n)
                            act.activation(qT[s][0:DH, 0:H:2, :], bank(s, 0, 2)[0:DH].rearrange("p (i n) -> p i n", n=P),
                                           ACT.Copy).then_inc(s_qe[s], 1)

                    half_steps(act, begin, slot)

                    def ready(p):
                        m = l * PAIRS + p + 1
                        for s in range(2):
                            act.wait_ge(f_sh[s], m)
                            act.activation(xs[s][:, :, D // 2:D], bank(s, 0)[:, 0:NT * D // 2].rearrange("p (t d) -> p t d", t=NT), ACT.Copy).then_inc(f_xu[s], 1)
                        for s in range(2):
                            act.wait_ge(f_c[s], m)
                            act.activation(R[s][:, 0:T].rearrange("p (t d) -> p t d", t=NT), xs[s][:, :, :], ACT.Square).then_inc(f_sq[s], 1)

                    def layer(p, more):
                        m = l * PAIRS + p + 1
                        for s in range(2):
                            if s == 0:
                                act.wait_ge(w_ffn, l * 64 + 64)
                            act.wait_ge(f_xt[s], m + 1)
                            act.activation(xsT[s][:, WIN:], bank(s, 1), ACT.Identity, scale=COL[:, 0:1], bias=COL[:, 1:2]).then_inc(f_xe[s], 1)
                        for s in range(2):
                            act.wait_ge(f_g[s], m)
                            for c in range(DCH):
                                k = P if c < DCH - 1 else DLAST
                                at = 2 + DCH + c
                                ins = act.activation(Q[s][0:k, c * T:c * T + T], bank(s, 1 + c)[0:k], ACT.Gelu, bias=COL[0:k, at:at + 1])
                            ins.then_inc(f_ge[s], 1)
                        if more:
                            ready(p + 1)

                    ahead(act, ready, layer)

            @block.vector
            def _(dve):
                with dve.Fori(0, DEPTH) as l:
                    v4 = lambda z: z[:, :].rearrange("p (a h e) -> p a h e", a=2, h=H)
                    h2 = DH // 2

                    def slot(front, back, prep):
                        if back and back[0:2] == (0, 0):
                            k[:] = [0, 0]
                        done = [FRONT * (1 - i) + NA * back[2] if back else 0 for i in range(2)]

                        def link(s, ins):
                            k[s] += 1
                            ins.then_inc(ch[s], 1)
                            dve.wait_ge(ch[s], l * NB[s] + done[s] + k[s])

                        def sines(i, a):
                            s, t, p = front
                            n = (l * PAIRS + p) * NT + t + 1
                            if t == 0 and s == 0:
                                dve.wait_ge(s_tab, l + 1)
                            dve.wait_ge(s_qn[s], 2 * n - 1 + i)
                            for lo, hi in ((0, h2), (h2, 0)):
                                ins = nc.vector.tensor_tensor(v4(R[s])[:, a, :, lo:lo + h2], v4(Q[s])[:, a, :, hi:hi + h2],
                                                              TS[:, t, a, lo:lo + h2].unsqueeze(1).to_broadcast([P, H, h2]), ALU.mult)
                            link(s, ins)

                        if front:
                            s, t, p = front
                            n = (l * PAIRS + p) * NT + t + 1
                            for c in range(2):
                                dve.wait_ge(s_sq[s], 2 * n - 1 + c)
                                link(s, nc.vector.tensor_reduce(ss[s][:, c * H:c * H + H], v4(R[s])[:, c], AX.X, ALU.add))
                        if back:
                            s, t, p = back
                            n = (l * PAIRS + p) * NT + t + 1
                            for c in range(2):
                                so = bank(s, c).rearrange("p (h n) -> p h n", n=2 * WIN)
                                hs = slice(c * H // 2, (c + 1) * H // 2)
                                dve.wait_ge(s_so[s], 2 * n - 1 + c)
                                link(s, nc.vector.tensor_reduce(mx[s][:, hs], so, AX.X, ALU.max))
                                nc.vector.tensor_tensor(Q[s][:, c * T:c * T + T].rearrange("p (h n) -> p h n", n=2 * WIN), so,
                                                        mx[s][:, hs].unsqueeze(2).to_broadcast([P, H // 2, 2 * WIN]), ALU.subtract).then_inc(s_sub[s], 1)
                        if front:
                            s, t, p = front
                            n = (l * PAIRS + p) * NT + t + 1
                            link(s, nc.vector.tensor_scalar(ss[s][:, :], ss[s][:, :], 1e-24, None, ALU.max))
                            rsqrt(lambda ins: link(s, ins), rn[s][:, 0, :], ss[s][:, :], rn[s][:, 1, :])
                            for a in (1, 0):
                                nc.vector.tensor_tensor(v4(Q[s])[:, a], bank(s, 2 * a, 2).rearrange("p (h e) -> p h e", e=DH),
                                                        rn[s][:, 0, a * H:a * H + H].unsqueeze(2).to_broadcast([P, H, DH]),
                                                        ALU.mult).then_inc(s_qn[s], 1)
                            sines(0, 1)
                        if back:
                            s, t, p = back
                            n = (l * PAIRS + p) * NT + t + 1
                            dve.wait_ge(s_o[s], n)
                            full = PS[:, 4 * s:4 * s + 2, 0:6 * (DH + 1)].rearrange("p b (h e) -> p b h e", h=6)
                            rest = bank(s, 2)[:, 0:4 * (DH + 1)].rearrange("p (h e) -> p h e", h=4)
                            r6 = rc[s][:, 0:12].rearrange("p (b h) -> p b h", b=2)
                            y6 = Y[s][:, 0:12 * DH].rearrange("p (b h e) -> p b h e", b=2, e=DH)
                            nc.vector.reciprocal(r6, full[:, :, :, DH])
                            link(s, nc.vector.reciprocal(rc[s][:, 12:H], rest[:, :, DH]))
                            nc.vector.tensor_tensor(y6, full[:, :, :, 0:DH], r6.unsqueeze(3).to_broadcast([P, 2, 6, DH]), ALU.mult)
                            nc.vector.tensor_tensor(Y[s][:, 12 * DH:].rearrange("p (h e) -> p h e", e=DH), rest[:, :, 0:DH],
                                                    rc[s][:, 12:H].unsqueeze(2).to_broadcast([P, 4, DH]), ALU.mult).then_inc(s_yn[s], 1)
                        if front:
                            sines(1, 0)

                        def rotated(i, a):
                            s, t, p = front
                            n = (l * PAIRS + p) * NT + t + 1
                            dve.wait_ge(s_a[s], 2 * n - 1 + i)
                            nc.vector.tensor_tensor(v4(A[s])[:, a], v4(A[s])[:, a], v4(R[s])[:, a], ALU.add).then_inc(s_rot[s], 1)

                        if back:
                            s, t, p = back
                            n = (l * PAIRS + p) * NT + t + 1
                            dve.wait_ge(s_yt[s], n)
                            nc.vector.tensor_copy(YT[s][:, :, :].rearrange("p i n -> p (i n)"), bank(s, 0, 2)).then_inc(s_ye[s], 1)
                        if front:
                            rotated(0, 1)
                            rotated(1, 0)
                        if back:
                            s, t, p = back
                            n = (l * PAIRS + p) * NT + t + 1
                            dve.wait_ge(s_w[s], n)
                            tile = XL[:, p + s * PAIRS, t + 1, :]
                            nc.vector.tensor_tensor(tile, bank(s, 2)[:, 0:D], tile, ALU.add).then_inc(s_xm[s], 1)
                        if front:
                            s, t, p = front
                            n = (l * PAIRS + p) * NT + t + 1
                            dve.wait_ge(s_qt[s], n)
                            nc.vector.tensor_copy(qT[s][DH:P, 1:H:2, :], bank(s, 0, 2)[DH:P].rearrange("p (i n) -> p i n", n=P)).then_inc(s_qe[s], 1)

                    k = [0, 0]
                    half_steps(dve, lambda prep: None, slot)
                    assert k == [NA - FRONT, NA], k
                    nc.vector.memset(mx[0][:, 0:1], 0.0).then_inc(free_attn, 1)
                    kf = [0]
                    wide = lambda z: z.unsqueeze(2).to_broadcast([P, NT, D])

                    def flink(p, ins):
                        kf[0] += 1
                        ins.then_inc(ch[0], 1)
                        dve.wait_ge(ch[0], l * NB[0] + p * NF + PAIRS * NA + kf[0])

                    def centred(p):
                        m = l * PAIRS + p + 1
                        kf[0] = 0
                        for s in range(2):
                            dve.wait_ge(f_xt[s], m)
                            flink(p, nc.vector.tensor_copy(xs[s][:, :, 0:D // 2], XL[:, p + s * PAIRS, 1:SLOTS, 0:D // 2]))
                        for s in range(2):
                            dve.wait_ge(f_xu[s], m)
                            flink(p, nc.vector.tensor_reduce(fs[:, 0, s, :], xs[s][:, :, :], AX.X, ALU.add))
                            flink(p, nc.vector.tensor_scalar(fs[:, 0, s, :], fs[:, 0, s, :], -1.0 / D, None, ALU.mult))
                            nc.vector.tensor_tensor(xs[s][:, :, :], xs[s][:, :, :], wide(fs[:, 0, s, :]), ALU.add).then_inc(f_c[s], 1)

                    def scaled(p):
                        m = l * PAIRS + p + 1
                        for s in range(2):
                            dve.wait_ge(f_sq[s], m)
                            ins = nc.vector.tensor_reduce(fs[:, 1, s, :], R[s][:, 0:T].rearrange("p (t d) -> p t d", t=NT), AX.X, ALU.add)
                        flink(p, ins)
                        f = lambda i: fs[:, i].rearrange("p s t -> p (s t)")
                        flink(p, nc.vector.tensor_scalar(f(1), f(1), 1.0 / D, 1e-5, ALU.mult, ALU.add))
                        rsqrt(lambda ins: flink(p, ins), f(2), f(1), f(3))
                        for s in range(2):
                            nc.vector.tensor_tensor(xs[s][:, :, :], xs[s][:, :, :], wide(fs[:, 2, s, :]), ALU.mult).then_inc(f_xn[s], 1)
                        assert kf[0] == NF, kf

                    def ready(p):
                        centred(p)
                        scaled(p)

                    def layer(p, more):
                        m = l * PAIRS + p + 1
                        if more:
                            centred(p + 1)
                        for s in range(2):
                            dve.wait_ge(f_a[s], m)
                            for c in range(DCH):
                                kk = P if c < DCH - 1 else DLAST
                                ins = nc.vector.scalar_tensor_tensor(out=A[s][0:kk, c * T:c * T + T], in0=bank(s, 1 + c)[0:kk], scalar=COL[0:kk, 2 + c:3 + c],
                                                                     in1=Q[s][0:kk, c * T:c * T + T], op0=ALU.add, op1=ALU.mult)
                            ins.then_inc(f_u[s], 1)
                        if more:
                            scaled(p + 1)
                        for s in range(2):
                            dve.wait_ge(f_rb[s], m)
                            dve.wait_ge(f_w[s], m)
                            nc.vector.tensor_tensor(XL[:, p + s * PAIRS, 1:SLOTS, :], bank(s, 0).rearrange("p (t d) -> p t d", t=NT),
                                                    R[s][:, T:2 * T].rearrange("p (t d) -> p t d", t=NT), ALU.add).then_inc(s_xl[s], 1)

                    ahead(dve, ready, layer)
                    nc.vector.memset(mx[0][:, 0:1], 0.0).then_inc(free_ffn, 1)

        with ExitStack() as c2:
            s_o = scoped(c2, "stored")
            s_f = scoped(c2, "summed")
            block = phase(c2)

            @block.vector
            def _(dve):
                for b in range(B):
                    o = X1[:, b * NT:b * NT + NT, :]
                    dve.tensor_tensor(o, o, XL[:, b, 1:SLOTS, :], ALU.add).then_inc(s_f, 1)

            @block.sync
            def _(sp):
                ov = out.rearrange("b (t p) d -> p b t d", p=P)
                for b in range(B):
                    sp.wait_ge(s_f, b + 1)
                    sp.dma_start(ov[:, b], X1[:, b * NT:b * NT + NT, :]).then_inc(s_o, 16)
                sp.wait_ge(s_o, 16 * B)


def kernel(**inputs):
    import concourse.bacc as _bacc
    from concourse.bass_utils import run_bass_kernel_spmd as _run

    a = {k: np.asarray(v) for k, v in inputs.items()}
    rep = lambda v, n=P: np.ascontiguousarray(np.broadcast_to(v, (n,) + v.shape))
    l0, l1, lf = "L0_attn_", "L1_attn_", "L1_ffn_"
    rows0 = np.concatenate([a["L0_ffn_bias"], a[l1 + "bo"], a[l0 + "lambda_q1"], a[l0 + "lambda_q2"],
                            a[l0 + "lambda_k1"], a[l0 + "lambda_k2"]])
    qk = np.concatenate([a[lf + "q_scale"], a[lf + "k_scale"]], 1)
    pad = lambda w, n: np.concatenate([w, np.zeros((DEPTH, n) + w.shape[2:], w.dtype)], 1)
    fill = DCH * P - DI
    b1 = a[lf + "b1"]
    b1c = [pad(b1[:, i * DI:(i + 1) * DI], fill).reshape(DEPTH, DCH, P).transpose(0, 2, 1) for i in range(2)]
    cols = np.concatenate([a[lf + "ln_g"][:, :, None], a[lf + "ln_b"][:, :, None]] + b1c, 2)
    arrays = {
        "x": a[l0 + "x"], "consts": constants(),
        "wqkv0": np.concatenate([a[l0 + n].T for n in ("Wq", "Wk", "Wv")], 1), "wproj0": a[l0 + "Wproj"].T,
        "wff0": a["L0_ffn_weight"], "rows0": rep(rows0),
        "wqkv1": np.concatenate([a[l1 + n].T for n in ("Wq", "Wk", "Wv")], 1), "wo1": a[l1 + "Wo"].T,
        "wqkv": a[lf + "Wqkv"], "wo": a[lf + "Wo"].reshape(DEPTH, INNER // P, P, D).transpose(0, 2, 1, 3),
        "qkscale": rep(qk).transpose(1, 0, 2), "w1": a[lf + "W1"],
        "w2": pad(a[lf + "W2"], fill).reshape(DEPTH, DCH, P, D).transpose(0, 2, 1, 3),
        "cols": cols, "b2": rep(a[lf + "b2"]).transpose(1, 0, 2),
    }
    arrays = {k: np.ascontiguousarray(v) for k, v in arrays.items()}
    nc = _bacc.Bacc("TRN2", target_bir_lowering=False, num_devices=1)
    args = [nc.dram_tensor(k, v.shape, mybir.dt.from_np(v.dtype), kind="ExternalInput").ap() for k, v in arrays.items()]
    out = nc.dram_tensor("out", (B, T, D), F32, kind="ExternalOutput").ap()
    program(nc, *args, out)
    r = _run(nc, [arrays], core_ids=[0])
    return r.results[0]["out"]
```
